# Optimizing a Trainium2 kernel written in Bass

```python
import numpy as np
import jax
import jax.numpy as jnp

def _softmax(x, axis=-1):
    return jax.nn.softmax(x, axis=axis)

def _gelu(x):
    return jax.nn.gelu(x, approximate=True)

def _silu(x):
    return jax.nn.silu(x)

def _sigmoid(x):
    return jax.nn.sigmoid(x)

def _layernorm(x, axis=-1, eps=1e-05):
    m = jnp.mean(x, axis=axis, keepdims=True)
    v = jnp.var(x, axis=axis, keepdims=True)
    return (x - m) / jnp.sqrt(v + eps)

def _scatter_add(tgt, idx, src, axis=0):
    return tgt.at[idx].add(src)

def _segment_sum(src, seg, n):
    return jax.ops.segment_sum(src, seg, n)
kernel_name = 'mk_xattn_ffn_d2_seqx_r8_e75682'

def setup_inputs(seed: int=0):
    np.random.seed(seed)
    _w = jnp.asarray

    def _rec_inputs():
        import jax
        import jax.numpy as jnp
        _rk = jax.random.key(seed)
        x = 0.01048 + 0.1018 * jax.random.normal(jax.random.fold_in(_rk, 1), (4, 256, 256), jnp.float32)
        _lenS = 256 - jax.random.randint(jax.random.fold_in(_rk, 7), (4,), 0, max(1, 256 // 4) + 1, jnp.int32)
        _lenS2 = 256 - jax.random.randint(jax.random.fold_in(_rk, 8), (4,), 0, max(1, 256 // 4) + 1, jnp.int32)
        _ctx_512P = jax.random.normal(jax.random.fold_in(_rk, 11), (4, 16, 64), jnp.float32)
        _ctx_512c = jax.random.dirichlet(jax.random.fold_in(_rk, 511), 0.3 * jnp.ones((16,), jnp.float32), (4, 256))
        _ctx_512t = jnp.einsum('bsk,bkd->bsd', _ctx_512c, _ctx_512P)
        _ctx_512t = _ctx_512t * jax.lax.rsqrt(jnp.mean(jnp.square(_ctx_512t)) + 1e-12) * 0.953939
        ctx_512 = -0.000292821 + 1.00034 * (_ctx_512t + 0.3 * jax.random.normal(jax.random.fold_in(_rk, 611), (4, 256, 64), jnp.float32))
        return (x, ctx_512)
    x, ctx_512 = _rec_inputs()

    def _L0_xattn_setup():
        import jax, jax.numpy as jnp
        import numpy as np
        LRELU_ALPHA = 0.2
        MASK_VAL = -10000000000.0
        B, N, F_IN = (4, 256, 64)
        H, F_OUT = (8, 32)
        F_HID = H * F_OUT

        def gat_layer(x, adj, W, a_self, a_neigh, b):
            feat = jnp.einsum('nf,hfo->hno', x, W)
            attn_self = jnp.einsum('hno,ho->hn', feat, a_self)
            attn_neigh = jnp.einsum('hno,ho->hn', feat, a_neigh)
            e = attn_self[:, :, None] + attn_neigh[:, None, :]
            e = jax.nn.leaky_relu(e, LRELU_ALPHA)
            e = e + MASK_VAL * (1.0 - adj)[None, :, :]
            alpha = jax.nn.softmax(e, axis=-1)
            out = jnp.einsum('hnm,hmo->hno', alpha, feat) + b[:, None, :]
            out = jnp.transpose(out, (1, 0, 2)).reshape(out.shape[1], -1)
            return jax.nn.elu(out)
        key = jax.random.key(seed)
        ks = jax.random.split(key, 10)
        feats = jax.random.normal(ks[0], (B, N, F_IN), dtype=jnp.float32)
        a = (jax.random.uniform(ks[1], (B, N, N)) < 0.01).astype(jnp.float32)
        adj = jnp.maximum(a, jnp.eye(N, dtype=jnp.float32)[None])
        s0 = 1.0 / np.sqrt(F_IN)
        s1 = 1.0 / np.sqrt(F_HID)
        return {'feats': feats, 'adj': adj, 'W0': jax.random.normal(ks[2], (H, F_IN, F_OUT), dtype=jnp.float32) * s0, 'a_self0': jax.random.normal(ks[3], (H, F_OUT), dtype=jnp.float32) * 0.1, 'a_neigh0': jax.random.normal(ks[4], (H, F_OUT), dtype=jnp.float32) * 0.1, 'b0': jnp.zeros((H, F_OUT), dtype=jnp.float32), 'W1': jax.random.normal(ks[5], (H, F_HID, F_OUT), dtype=jnp.float32) * s1, 'a_self1': jax.random.normal(ks[6], (H, F_OUT), dtype=jnp.float32) * 0.1, 'a_neigh1': jax.random.normal(ks[7], (H, F_OUT), dtype=jnp.float32) * 0.1, 'b1': jnp.zeros((H, F_OUT), dtype=jnp.float32)}
    _L0_xattn_all = _L0_xattn_setup()
    _L0_xattn_in = {k: v for k, v in _L0_xattn_all.items() if k in ('W0', 'a_self0', 'a_neigh0', 'b0', 'W1', 'a_self1', 'a_neigh1', 'b1')}
    del _L0_xattn_all

    def _L0_ffn_setup():
        import jax, jax.numpy as jnp
        import numpy as np
        B, S, H = (1, 256, 256)
        E, K, I = (16, 4, 176)
        IS = 352
        CAP = 128
        key = jax.random.key(seed)
        ks = jax.random.split(key, 8)
        sc = 0.02
        return {'hidden_states': jax.random.normal(ks[0], (B, S, H), jnp.float32), 'gate_w': jax.random.normal(ks[1], (E, H), jnp.float32) * sc, 'w_gate': jax.random.normal(ks[2], (E, H, I), jnp.float32) * sc, 'w_up': jax.random.normal(ks[3], (E, H, I), jnp.float32) * sc, 'w_down': jax.random.normal(ks[4], (E, I, H), jnp.float32) * sc, 'sw_gate': jax.random.normal(ks[5], (H, IS), jnp.float32) * sc, 'sw_up': jax.random.normal(ks[6], (H, IS), jnp.float32) * sc, 'sw_down': jax.random.normal(ks[7], (IS, H), jnp.float32) * sc}
    _L0_ffn_all = _L0_ffn_setup()
    _L0_ffn_in = {k: v for k, v in _L0_ffn_all.items() if k in ('gate_w', 'w_gate', 'w_up', 'w_down', 'sw_gate', 'sw_up', 'sw_down')}
    del _L0_ffn_all

    def _L1_xattn_setup():
        import jax, jax.numpy as jnp
        import numpy as np
        B, S, L = (2, 128, 128)
        DIM_Q, H, K, D_C, D_CQ, R = (256, 16, 128, 64, 192, 64)

        def _rope_tables(seq_len, dim, dtype):
            inv_freq = 1.0 / 10000.0 ** (jnp.arange(0, dim, 2, dtype=dtype) / dim)
            t = jnp.arange(seq_len, dtype=dtype)
            freqs = t[:, None] * inv_freq[None, :]
            sin = jnp.repeat(jnp.sin(freqs), 2, axis=-1)
            cos = jnp.repeat(jnp.cos(freqs), 2, axis=-1)
            return (sin, cos)

        def _rotate_half(x):
            h = x.shape[-1] // 2
            return jnp.concatenate([-x[..., h:], x[..., :h]], axis=-1)
        key = jax.random.key(seed)
        ks = jax.random.split(key, 8)
        s_in = 1.0 / np.sqrt(DIM_Q)
        s_k = 1.0 / np.sqrt(K)
        s_cq = 1.0 / np.sqrt(D_CQ)
        s_c = 1.0 / np.sqrt(D_C)
        return {'hidden_q': jax.random.normal(ks[0], (B, S, DIM_Q), jnp.float32), 'kv_c': jax.random.normal(ks[1], (B, L, D_C), jnp.float32), 'Wq': jax.random.normal(ks[2], (H * K, DIM_Q), jnp.float32) * s_in, 'w_kc_q': jax.random.normal(ks[3], (H, K, D_CQ), jnp.float32) * s_k, 'w_kc_kv': jax.random.normal(ks[4], (H, K, D_C), jnp.float32) * s_k, 'W_qr': jax.random.normal(ks[5], (H, D_CQ, R), jnp.float32) * s_cq / np.sqrt(R), 'W_kr': jax.random.normal(ks[6], (H, D_C, R), jnp.float32) * s_c, 'Wo': jax.random.normal(ks[7], (DIM_Q, H * K), jnp.float32) * s_k}
    _L1_xattn_all = _L1_xattn_setup()
    _L1_xattn_in = {k: v for k, v in _L1_xattn_all.items() if k in ('Wq', 'w_kc_q', 'w_kc_kv', 'W_qr', 'W_kr', 'Wo')}
    del _L1_xattn_all

    def _L1_ffn_setup():
        import jax, jax.numpy as jnp
        import numpy as np
        NORM_EPS = 1e-05

        def _quant_input(x):
            s = 127.0 / jnp.clip(jnp.max(jnp.abs(x), axis=-1, keepdims=True), 1e-05, None)
            return jnp.clip(jnp.round(x * s), -128.0, 127.0) / s

        def _rmsnorm(x, w, eps):
            return x * jax.lax.rsqrt(jnp.mean(x * x, axis=-1, keepdims=True) + eps) * w
        key = jax.random.key(seed)
        k0, k1, k2 = jax.random.split(key, 3)
        dim, hidden = (256, 704)
        x = jax.random.normal(k0, (4, 256, dim), dtype=jnp.float32)
        w13 = jax.random.normal(k1, (2 * hidden, dim), dtype=jnp.float32) * 0.02
        w2 = jax.random.normal(k2, (dim, hidden), dtype=jnp.float32) * 0.02
        norm_w = jnp.ones((hidden,), dtype=jnp.float32)
        return {'x': x, 'w13': w13, 'w2': w2, 'norm_w': norm_w}
    _L1_ffn_all = _L1_ffn_setup()
    _L1_ffn_in = {k: v for k, v in _L1_ffn_all.items() if k in ('w13', 'w2', 'norm_w')}
    del _L1_ffn_all
    return {'x': x, 'ctx_512': ctx_512, 'L0_xattn_W0': _L0_xattn_in['W0'], 'L0_xattn_a_self0': _L0_xattn_in['a_self0'], 'L0_xattn_a_neigh0': _L0_xattn_in['a_neigh0'], 'L0_xattn_b0': _L0_xattn_in['b0'], 'L0_xattn_W1': _L0_xattn_in['W1'], 'L0_xattn_a_self1': _L0_xattn_in['a_self1'], 'L0_xattn_a_neigh1': _L0_xattn_in['a_neigh1'], 'L0_xattn_b1': _L0_xattn_in['b1'], 'L0_ffn_gate_w': _L0_ffn_in['gate_w'], 'L0_ffn_w_gate': _L0_ffn_in['w_gate'], 'L0_ffn_w_up': _L0_ffn_in['w_up'], 'L0_ffn_w_down': _L0_ffn_in['w_down'], 'L0_ffn_sw_gate': _L0_ffn_in['sw_gate'], 'L0_ffn_sw_up': _L0_ffn_in['sw_up'], 'L0_ffn_sw_down': _L0_ffn_in['sw_down'], 'L1_xattn_Wq': _L1_xattn_in['Wq'], 'L1_xattn_w_kc_q': _L1_xattn_in['w_kc_q'], 'L1_xattn_w_kc_kv': _L1_xattn_in['w_kc_kv'], 'L1_xattn_W_qr': _L1_xattn_in['W_qr'], 'L1_xattn_W_kr': _L1_xattn_in['W_kr'], 'L1_xattn_Wo': _L1_xattn_in['Wo'], 'L1_ffn_w13': _L1_ffn_in['w13'], 'L1_ffn_w2': _L1_ffn_in['w2'], 'L1_ffn_norm_w': _L1_ffn_in['norm_w']}

def reference(x, ctx_512, L0_xattn_W0, L0_xattn_a_self0, L0_xattn_a_neigh0, L0_xattn_b0, L0_xattn_W1, L0_xattn_a_self1, L0_xattn_a_neigh1, L0_xattn_b1, L0_ffn_gate_w, L0_ffn_w_gate, L0_ffn_w_up, L0_ffn_w_down, L0_ffn_sw_gate, L0_ffn_sw_up, L0_ffn_sw_down, L1_xattn_Wq, L1_xattn_w_kc_q, L1_xattn_w_kc_kv, L1_xattn_W_qr, L1_xattn_W_kr, L1_xattn_Wo, L1_ffn_w13, L1_ffn_w2, L1_ffn_norm_w):
    import jax
    import jax.numpy as jnp

    def _L0_xattn_ref(feats, adj, W0, a_self0, a_neigh0, b0, W1, a_self1, a_neigh1, b1):
        import jax, jax.numpy as jnp
        import numpy as np
        LRELU_ALPHA = 0.2
        MASK_VAL = -10000000000.0
        B, N, F_IN = (4, 256, 64)
        H, F_OUT = (8, 32)
        F_HID = H * F_OUT

        def gat_layer(x, adj, W, a_self, a_neigh, b):
            feat = jnp.einsum('nf,hfo->hno', x, W)
            attn_self = jnp.einsum('hno,ho->hn', feat, a_self)
            attn_neigh = jnp.einsum('hno,ho->hn', feat, a_neigh)
            e = attn_self[:, :, None] + attn_neigh[:, None, :]
            e = jax.nn.leaky_relu(e, LRELU_ALPHA)
            e = e + MASK_VAL * (1.0 - adj)[None, :, :]
            alpha = jax.nn.softmax(e, axis=-1)
            out = jnp.einsum('hnm,hmo->hno', alpha, feat) + b[:, None, :]
            out = jnp.transpose(out, (1, 0, 2)).reshape(out.shape[1], -1)
            return jax.nn.elu(out)

        def per_graph(x, a):
            h = gat_layer(x, a, W0, a_self0, a_neigh0, b0)
            return gat_layer(h, a, W1, a_self1, a_neigh1, b1)
        return jax.vmap(per_graph)(feats, adj)

    def _L0_ffn_ref(hidden_states, gate_w, w_gate, w_up, w_down, sw_gate, sw_up, sw_down):
        import jax, jax.numpy as jnp
        import numpy as np
        B, S, H = (1, 256, 256)
        E, K, I = (16, 4, 176)
        IS = 352
        CAP = 128
        b, s, h = hidden_states.shape
        x = hidden_states.reshape(-1, h)
        T = x.shape[0]
        scores = jax.nn.softmax(x @ gate_w.T, axis=-1)
        topk_w, topk_i = jax.lax.top_k(scores, K)
        topk_w = topk_w / (topk_w.sum(-1, keepdims=True) + 1e-20)
        flat_i = topk_i.reshape(-1)
        flat_w = topk_w.reshape(-1)
        order = jnp.argsort(flat_i)
        se = flat_i[order]
        counts = jax.ops.segment_sum(jnp.ones_like(flat_i), flat_i, num_segments=E)
        starts = jnp.cumsum(counts) - counts
        rank = jnp.arange(T * K) - starts[se]
        tok = order // K
        slot = jnp.where(rank < CAP, rank, CAP)
        buf = jnp.full((E, CAP + 1), T, dtype=jnp.int32).at[se, slot].set(tok)[:, :CAP]
        wbuf = jnp.zeros((E, CAP + 1), x.dtype).at[se, slot].set(flat_w[order])[:, :CAP]
        xpad = jnp.concatenate([x, jnp.zeros((1, h), x.dtype)], axis=0)
        xg = xpad[buf]
        gact = jax.nn.silu(jnp.einsum('ech,ehi->eci', xg, w_gate))
        mid = gact * jnp.einsum('ech,ehi->eci', xg, w_up)
        eout = jnp.einsum('eci,eih->ech', mid, w_down) * wbuf[..., None]
        y = jnp.zeros((T + 1, h), x.dtype).at[buf.reshape(-1)].add(eout.reshape(-1, h))[:T]
        shared = jax.nn.silu(x @ sw_gate) * (x @ sw_up) @ sw_down
        return (y + shared).reshape(b, s, h)

    def _L1_xattn_ref(hidden_q, kv_c, Wq, w_kc_q, w_kc_kv, W_qr, W_kr, Wo):
        import jax, jax.numpy as jnp
        import numpy as np
        B, S, L = (2, 128, 128)
        DIM_Q, H, K, D_C, D_CQ, R = (256, 16, 128, 64, 192, 64)

        def _rope_tables(seq_len, dim, dtype):
            inv_freq = 1.0 / 10000.0 ** (jnp.arange(0, dim, 2, dtype=dtype) / dim)
            t = jnp.arange(seq_len, dtype=dtype)
            freqs = t[:, None] * inv_freq[None, :]
            sin = jnp.repeat(jnp.sin(freqs), 2, axis=-1)
            cos = jnp.repeat(jnp.cos(freqs), 2, axis=-1)
            return (sin, cos)

        def _rotate_half(x):
            h = x.shape[-1] // 2
            return jnp.concatenate([-x[..., h:], x[..., :h]], axis=-1)
        b, s, _ = hidden_q.shape
        l = kv_c.shape[1]
        q_hk = (hidden_q @ Wq.T).reshape(b, s, H, K)
        q_big = jnp.einsum('bshk,hkq->bshq', q_hk, w_kc_q)
        sin, cos = _rope_tables(l, D_C, kv_c.dtype)
        kv_rope = kv_c * cos[None] + _rotate_half(kv_c) * sin[None]
        q_r = jnp.einsum('bshq,hqr->bhsr', q_big, W_qr)
        k_r = jnp.einsum('bld,hdr->bhlr', kv_rope, W_kr)
        scores = jnp.einsum('bhsr,bhlr->bhsl', q_r, k_r)
        attn = jax.nn.softmax(scores, axis=-1)
        ctx_c = jnp.einsum('bhsl,bld->bhsd', attn, kv_rope)
        ctx_lat = jnp.einsum('bhsd,hkd->bshk', ctx_c, w_kc_kv)
        out = ctx_lat.reshape(b, s, H * K) @ Wo.T
        return out

    def _L1_ffn_ref(x, w13, w2, norm_w):
        import jax, jax.numpy as jnp
        import numpy as np
        NORM_EPS = 1e-05

        def _quant_input(x):
            s = 127.0 / jnp.clip(jnp.max(jnp.abs(x), axis=-1, keepdims=True), 1e-05, None)
            return jnp.clip(jnp.round(x * s), -128.0, 127.0) / s

        def _rmsnorm(x, w, eps):
            return x * jax.lax.rsqrt(jnp.mean(x * x, axis=-1, keepdims=True) + eps) * w
        xq = _quant_input(x)
        x13 = jnp.einsum('bsd,fd->bsf', xq, w13)
        x1, x3 = jnp.split(x13, 2, axis=-1)
        gated = jnp.square(jax.nn.relu(x1)) * x3
        inner = _rmsnorm(gated, norm_w, NORM_EPS)
        iq = _quant_input(inner)
        out = jnp.einsum('bsh,dh->bsd', iq, w2)
        return out
    x = x + _L0_xattn_ref(ctx_512, _layernorm(x, axis=-1), L0_xattn_W0, L0_xattn_a_self0, L0_xattn_a_neigh0, L0_xattn_b0, L0_xattn_W1, L0_xattn_a_self1, L0_xattn_a_neigh1, L0_xattn_b1)
    x = x + _L0_ffn_ref(_layernorm(x, axis=-1), L0_ffn_gate_w, L0_ffn_w_gate, L0_ffn_w_up, L0_ffn_w_down, L0_ffn_sw_gate, L0_ffn_sw_up, L0_ffn_sw_down)
    x = x + _L1_xattn_ref(_layernorm(x, axis=-1), ctx_512, L1_xattn_Wq, L1_xattn_w_kc_q, L1_xattn_w_kc_kv, L1_xattn_W_qr, L1_xattn_W_kr, L1_xattn_Wo)
    x = x + _L1_ffn_ref(_layernorm(x, axis=-1), L1_ffn_w13, L1_ffn_w2, L1_ffn_norm_w)
    return x

_drawn_inputs = setup_inputs


def setup_inputs(seed=0):
    import zlib

    import numpy as np

    out = dict(_drawn_inputs(seed))
    spreads = {'L0_xattn_b0': (0.0, 0.1), 'L0_xattn_b1': (0.0, 0.1), 'L1_ffn_norm_w': (1.0, 0.587)}
    factors = {'L0_ffn_gate_w': 7.721,
     'L0_ffn_w_gate': 7.493,
     'L0_ffn_w_up': 7.482,
     'L0_ffn_w_down': 7.431,
     'L0_ffn_sw_gate': 8.0,
     'L0_ffn_sw_up': 8.0,
     'L0_ffn_sw_down': 8.0}
    for name, (base, spread) in spreads.items():
        noise = np.random.default_rng([zlib.crc32(name.encode()), seed]).standard_normal(out[name].shape)
        drawn = base * np.exp(spread * noise) if base else spread * noise
        out[name] = jnp.asarray(drawn.astype(out[name].dtype))
    for name, factor in factors.items():
        out[name] = (out[name] * factor).astype(out[name].dtype)
    return out
```

```python
from contextlib import ExitStack

import numpy as np

import concourse.bass as bass
from concourse import mybir

F32 = mybir.dt.float32
F16 = mybir.dt.float16
BF16 = mybir.dt.bfloat16
U32 = mybir.dt.uint32
ALU = mybir.AluOpType
ACT = mybir.ActivationFunctionType
AX_X = mybir.AxisListType.X

P = 128
B, S, D = 4, 256, 256
T = B * S
NT = T // P
TB = S // P
KT = D // P
CD = 64
GH, GO = 8, 32
E, TOPK, IE, CAP = 16, 4, 176, 128
IS = 352
AH, AK, AQ, AR = 16, 128, 192, 64
HID = 704
LN_EPS, RMS_EPS = 1e-5, 1e-5
MASK = 1e10
BIG = 3.0e38
ROUND = 1.5 * 2.0 ** 23
NO_SLOT = 200.0
ZROW = E * CAP


def build(nc, a, out):
    ctx = ExitStack()
    with ctx:
        def sb(name, shape, dt=F32):
            return ctx.enter_context(nc.sbuf_tensor(name, shape, dt))

        def sem(name):
            return ctx.enter_context(nc.semaphore(name))

        bank = [ctx.enter_context(nc.psum_tensor(f"bank{i}", [P, 512], F32)) for i in range(8)]

        X = sb("X", [P, NT, D])
        ident = sb("ident", [P, P])
        identh = sb("identh", [P, P], BF16)
        half = sb("half", [P, 2])
        xlnT = sb("xlnT", [P, KT, T])
        bnst = sb("bnst", [P, TB, 6])
        mv = sb("mv", [P, TB, 2])
        veps = sb("veps", [P, TB])
        rstd = sb("rstd", [P, TB])
        xln = sb("xln", [P, TB, D])
        work = sb("work", [P, 15232])
        place = [0]

        def at(shape, rows=P, dt=F32):
            n = int(np.prod(shape)) * (1 if dt is F32 else 0.5)
            lo = place[0]
            place[0] += int(n)
            assert place[0] <= 15232, place[0]
            x = work[0:rows, lo:place[0]]
            x = x if dt is F32 else x.bitcast(dt)
            names = "abcd"[:len(shape)]
            return x.rearrange(f"p ({' '.join(names)}) -> p {' '.join(names)}", **dict(zip(names[1:], shape[1:])))

        ctxT = at([T], CD)
        ctxb = sb("ctxb", [CD, S])
        w0 = at([1, D], CD)
        w1 = at([KT, D])
        w0T = at([KT, CD])
        w1T = at([KT, D])
        cols = sb("cols", [P, 2, 3, KT])
        acol = cols[:, :, 0:2, :]
        bcol = cols[:, :, 2, :]
        blockmask = sb("blockmask", [P, KT, GH])
        abd = sb("abd", [P, 2, KT, 2 * GH])
        was = [sb("was0", [CD, 1, GH]), sb("was1", [P, KT, GH])]
        wan = [at([1, GH, P], CD), at([KT, GH, P])]
        maskN = at([TB, S])
        featS = at([TB, D])
        selfS = sb("selfS", [P, TB, GH])
        self02 = sb("self02", [P, TB, GH])
        NB = at([GH, S])
        U = at([2, TB, S])
        L = at([2, TB, S])
        M = sb("M", [P, 2, TB])
        Ex = at([2, TB, S])
        Sm = sb("Sm", [P, 2, TB])
        Ri = sb("Ri", [P, 2, TB])
        ETs = at([2, TB, S])
        m0 = at([KT, S])
        r0 = at([KT, S])
        e0 = at([KT, S])
        hT = [at([KT, S]), at([KT, S])]
        place[0] = 0
        gwT = sb("gwT", [P, KT, E])
        Lp = sb("Lp", [P, NT, E + TOPK])
        top8 = sb("top8", [P, NT, 8])
        rep = sb("rep", [P, NT, E + TOPK])
        sel = sb("sel", [P, NT, E])
        selb = sb("selb", [P, NT, E], BF16)
        prob = sb("prob", [P, NT, E])
        wgt = sb("wgt", [P, NT, E])
        ssum = sb("ssum", [P, NT])
        srec = sb("srec", [P, NT])
        keep = sb("keep", [P, NT, E])
        slotf = sb("slotf", [P, NT, E])
        slotv = sb("slotv", [P, NT, E], F16)
        key = sb("key", [P, NT, E])
        rowof = sb("rowof", [P, E])
        keytop = sb("keytop", [P, NT, 8])
        idx = sb("idx", [P, NT, TOPK], U32)
        eq = sb("eq", [P, NT, TOPK, E])
        wk = sb("wk", [P, NT, TOPK])
        upper = sb("upper", [P, P], BF16)
        upperf = sb("upperf", [P, P])
        onesb = sb("onesb", [P, P], BF16)
        iotaf = sb("iotaf", [P, CAP])
        iotah = sb("iotah", [P, CAP], F16)
        xhi = sb("xhi", [P, NT, D], F16)
        xlo = sb("xlo", [P, NT, D], F16)
        arena = sb("arena", [P, 17408])
        disp = arena[:, 0:8192].bitcast(F16).rearrange("p (t e s) -> p t e s", t=NT, e=E)
        gath = arena[:, 8192:16384].rearrange("p (j d) -> p j d", j=NT * TOPK)
        wq = arena[:, 0:4096].rearrange("p (h d) -> p h d", h=AH)
        wo = arena[:, 4096:8192].rearrange("p (h d) -> p h d", h=AH)
        kcqT = arena[0:96, 8192:12288].rearrange("p (t n) -> p t n", t=2)
        qrT = arena[0:AR, 12288:15360].rearrange("p (h q) -> p h q", h=AH)
        krT = arena[0:AR, 15360:16384].rearrange("p (h c) -> p h c", h=AH)
        kckv = arena[:, 16384:17408].rearrange("p (h c) -> p h c", h=AH)
        xgT = at([KT, E * CAP])
        kblk = xgT[:, 0, :].rearrange("p (b h s) -> p b h s", b=B, h=2)
        zrow = sb("zrow", [1, D])
        swg = sb("swg", [P, KT, IS])
        swu = sb("swu", [P, KT, IS])
        swd = sb("swd", [P, 3, D])
        sgs = at([512])
        smid = at([3, 512])
        wg = at([2, KT, IE])
        wu = at([2, KT, IE])
        IH = IE // 2
        wd = at([2, 2, D], IH)
        esg = sb("esg", [IH, 2, 2 * CAP])
        emid = sb("emid", [IH, 2, 2, CAP])
        eoS = sb("eoS", [P, 2, D])
        chs = xgT[0:96, 0, :]
        dhs = xgT[:, 1, 0:AH * CD]
        Nw = sb("Nw", [P, KT, AH * CD])
        Pw = sb("Pw", [P, AH // 2, D])
        early = Pw[:, :, :].rearrange("p j d -> p (j d)")
        kv = early[:, 0:512].rearrange("p (t c) -> p t c", t=NT)
        kvt = early[:, 512:1024].rearrange("p (t c) -> p t c", t=NT)
        cosd = early[:, 1024:1152].rearrange("p (t c) -> p t c", t=TB)
        sind = early[:, 1152:1280].rearrange("p (t c) -> p t c", t=TB)
        kvr = sb("kvr", [P, NT, 2, CD])
        w13f = arena[:, 0:KT * 2 * HID].rearrange("p (k n) -> p k n", k=KT)
        w2f = arena[:, 2816:2816 + 6 * D].rearrange("p (k n) -> p k n", k=6)
        w13p = at([3, KT, 2 * HID], dt=BF16)
        w2p = at([3, 6, D], dt=BF16)
        nwb = arena[:, 4352:4352 + HID]
        qT = arena[:, 8192:10240].rearrange("p (j s) -> p j s", j=AH // 2)
        E2 = arena[:, 10240:12288].rearrange("p (f t h s) -> p f t h s", f=2, t=TB, h=2)
        ET2 = arena[:, 12288:14336].rearrange("p (f h t s) -> p f h t s", f=2, h=2, t=TB)
        cxT = arena[:, 14336:16384].rearrange("p (j s) -> p j s", j=AH // 2)
        xT3 = arena[:, 16384:16896].rearrange("p (k s) -> p k s", k=KT)
        kvb = sb("kvb", [P, TB, CD])
        nmx = sb("nmx", [P, 2, TB, 2])
        S2 = sb("S2", [P, 2, TB, 2])
        R2 = sb("R2", [P, 2, TB, 2])
        r1 = arena[:, 0:HID].rearrange("p (c n) -> p c n", c=2)
        r2 = arena[:, HID:2 * HID].rearrange("p (c n) -> p c n", c=2)
        gated = arena[:, 2 * HID:3 * HID]
        tmpq = arena[:, 3 * HID:4 * HID]
        q1 = sb("q1", [P, D], BF16)
        q1T = sb("q1T", [P, KT, P], BF16)
        q2 = sb("q2", [P, HID], BF16)
        q2T = sb("q2T", [P, 6, P], BF16)
        yt = arena[:, 5056:5056 + TB * D].rearrange("p (t d) -> p t d", t=TB)
        is1 = sb("is1", [P, 1])
        is2 = sb("is2", [P, 1])
        amax = sb("amax", [P, 1])
        ms = sb("ms", [P, 1])
        msq = sb("msq", [P, 1])
        rms = sb("rms", [P, 1])

        eout = nc.dram_tensor("eout", (ZROW + 1, D), F32, kind="Internal").ap()

        ld_x = sem("ld_x")
        ld_ctxT = sem("ld_ctxT")
        ld_gat = sem("ld_gat")
        ld_const = sem("ld_const")
        ld_attn = sem("ld_attn")
        ld_ffn0 = sem("ld_ffn0")
        ld_w13 = sem("ld_w13")
        ld_kv = sem("ld_kv")
        st_out = sem("st_out")
        st_eout = sem("st_eout")
        st_z = sem("st_z")
        consts_ready = sem("consts_ready")
        abd_ready = sem("abd_ready")
        wa_mm = sem("wa_mm")
        wa_ready = sem("wa_ready")
        ctxb_ready = sem("ctxb_ready")
        veps_ready = sem("veps_ready")
        rstd_ready = sem("rstd_ready")
        self_mm = sem("self_mm")
        feat_mm = sem("feat_mm")
        nb_mm = sem("nb_mm")
        feat_evac = sem("feat_evac")
        self_evac = sem("self_evac")
        nb_evac = sem("nb_evac")
        u_ready = sem("u_ready")
        leak_done = sem("leak_done")
        e_ready = sem("e_ready")
        exp_done = sem("exp_done")
        rinv_ready = sem("rinv_ready")
        en_ready = sem("en_ready")
        et_mm = sem("et_mm")
        et_evac = sem("et_evac")
        agg_mm = sem("agg_mm")
        elu_min = sem("elu_min")
        agg_free = sem("agg_free")
        elu_exp = sem("elu_exp")
        h_ready = sem("h_ready")
        otr_mm = sem("otr_mm")
        x1_ready = sem("x1_ready")
        xln_ready = sem("xln_ready")
        lnT_mm = sem("lnT_mm")
        lnT_evac = sem("lnT_evac")
        split_ready = sem("split_ready")
        c_mm = sem("c_mm")
        c_evac = sem("c_evac")
        d_mm = sem("d_mm")
        d_evac = sem("d_evac")
        n_mm = sem("n_mm")
        n_evac = sem("n_evac")
        p_mm = sem("p_mm")
        p_evac = sem("p_evac")
        logit_mm = sem("logit_mm")
        route_exp_in = sem("route_exp_in")
        route_exp = sem("route_exp")
        sel_ready = sem("sel_ready")
        rank_mm = sem("rank_mm")
        disp_ready = sem("disp_ready")
        disp_mm = sem("disp_mm")
        disp_evac = sem("disp_evac")
        idx_ready = sem("idx_ready")
        shg_mm = sem("shg_mm")
        shs_ready = sem("shs_ready")
        shm_ready = sem("shm_ready")
        shd_mm = sem("shd_mm")
        shd_add = sem("shd_add")
        exg_mm = sem("exg_mm")
        exs_ready = sem("exs_ready")
        exm_ready = sem("exm_ready")
        exd_mm = sem("exd_mm")
        exo_ready = sem("exo_ready")
        kvr_ready = sem("kvr_ready")
        kvT_mm = sem("kvT_mm")
        kvT_ready = sem("kvT_ready")
        kvb_ready = sem("kvb_ready")
        l2_veps = sem("l2_veps")
        l2_rstd = sem("l2_rstd")
        l2_xln = sem("l2_xln")
        l2_T_mm = sem("l2_T_mm")
        l2_T_evac = sem("l2_T_evac")
        q_mm = sem("q_mm")
        q_evac = sem("q_evac")
        sc_mm = sem("sc_mm")
        mx_ready = sem("mx_ready")
        ex2_ready = sem("ex2_ready")
        ri2_ready = sem("ri2_ready")
        en2_ready = sem("en2_ready")
        et2_mm = sem("et2_mm")
        et2_evac = sem("et2_evac")
        cx_mm = sem("cx_mm")
        cx_evac = sem("cx_evac")
        o_mm = sem("o_mm")
        x3_ready = sem("x3_ready")
        wsplit_ready = sem("wsplit_ready")
        f_veps = sem("f_veps")
        f_rstd = sem("f_rstd")
        f_q1 = sem("f_q1")
        f_q1T_mm = sem("f_q1T_mm")
        f_q1T = sem("f_q1T")
        f_a_mm = sem("f_a_mm")
        f_r_ready = sem("f_r_ready")
        f_g_ready = sem("f_g_ready")
        f_sq_ready = sem("f_sq_ready")
        f_ms = sem("f_ms")
        f_rms = sem("f_rms")
        f_q2 = sem("f_q2")
        f_q2T_mm = sem("f_q2T_mm")
        f_q2T = sem("f_q2T")
        f_o_mm = sem("f_o_mm")
        f_out = sem("f_out")
        act_step = sem("act_step")
        elu_max = sem("elu_max")
        f_relu = sem("f_relu")
        dve_step = sem("dve_step")
        pool_step = sem("pool_step")
        zero_ready = sem("zero_ready")
        big_ready = sem("big_ready")
        ld_we = [sem(f"ld_we{i}") for i in range(2)]
        g_ld = [sem(f"g_ld{i}") for i in range(8)]

        block = ctx.enter_context(nc.Block())

        @block.sync
        def _(sp):
            for stores in (st_eout, st_out):
                sp.sem_inc(stores, 16)
            sp.dma_start(X[:, :, :], a["x"].rearrange("(t p) d -> p t d", p=P)).then_inc(ld_x, 16)
            sp.dma_start(ctxT[:, :], a["ctxT"]).then_inc(ld_ctxT, 16)
            sp.dma_start(w0T[:, :, :], a["w0T"].rearrange("(k p) n -> p k n", p=P)).then_inc(ld_gat, 16)
            sp.dma_start(w1T[:, :, :], a["w1T"].rearrange("(k p) n -> p k n", p=P)).then_inc(ld_gat, 16)
            sp.dma_start(cols[:, :, :, :], a["cols"].rearrange("p (l i k) -> p l i k", l=2, i=3)).then_inc(ld_gat, 16)
            sp.dma_start(blockmask[:, :, :], a["block"].rearrange("(k p) h -> p k h", p=P)).then_inc(ld_gat, 16)
            sp.dma_start(w0[:, 0, :], a["w0"]).then_inc(ld_gat, 16)
            sp.dma_start(w1[:, :, :], a["w1"].rearrange("(k p) n -> p k n", p=P)).then_inc(ld_gat, 16)
            sp.dma_start(ident[:, :], a["ident"]).then_inc(ld_const, 16)
            sp.dma_start(upperf[:, :], a["upper"]).then_inc(ld_const, 16)
            sp.dma_start(iotaf[:, :], a["iota"]).then_inc(ld_const, 16)
            sp.dma_start(rowof[:, :], a["rowof"]).then_inc(ld_const, 16)
            sp.dma_start(kv[:, :, :], a["ctx"].rearrange("(t p) c -> p t c", p=P)).then_inc(ld_kv, 16)
            sp.dma_start(cosd[:, :, :], a["cos"].rearrange("(t p) c -> p t c", p=P)).then_inc(ld_kv, 16)
            sp.dma_start(sind[:, :, :], a["sin"].rearrange("(t p) c -> p t c", p=P)).then_inc(ld_kv, 16)
            sp.dma_start(gwT[:, :, :], a["gwT"].rearrange("(k p) e -> p k e", p=P)).then_inc(ld_ffn0, 16)
            sp.dma_start(swg[:, :, :], a["swg"].rearrange("(k p) n -> p k n", p=P)).then_inc(ld_ffn0, 16)
            sp.dma_start(swu[:, :, :], a["swu"].rearrange("(k p) n -> p k n", p=P)).then_inc(ld_ffn0, 16)
            sp.dma_start(swd[:, 0:2, :], a["swd"][0:2 * P, :].rearrange("(k p) n -> p k n", p=P),
                         ).then_inc(ld_ffn0, 16)
            sp.dma_start(swd[0:IS - 2 * P, 2, :], a["swd"][2 * P:IS, :]).then_inc(ld_ffn0, 16)
            sp.dma_start(wq, a["wq"].rearrange("(h k) d -> k h d", k=P)).then_inc(ld_attn, 16)
            sp.dma_start(wo, a["woT"].rearrange("(h k) d -> k h d", k=P)).then_inc(ld_attn, 16)
            sp.dma_start(kcqT, a["kcqT"].rearrange("(t q) n -> q t n", q=96)).then_inc(ld_attn, 16)
            sp.dma_start(qrT, a["qrT"].rearrange("r (h q) -> r h q", h=AH)).then_inc(ld_attn, 16)
            sp.dma_start(krT, a["krT"].rearrange("r (h c) -> r h c", h=AH)).then_inc(ld_attn, 16)
            sp.dma_start(kckv, a["kckv"].rearrange("k (h c) -> k h c", h=AH)).then_inc(ld_attn, 16)

            def load_expert(e, f):
                gw, uw = (a[n][bass.ds(e, 1), :, :].rearrange("o (k p) n -> p (o k) n", p=P) for n in ("wg", "wu"))
                dw = a["wd"][bass.ds(e, 1), :, :].rearrange("o (j p) n -> p (o j) n", p=IH)
                sp.dma_start(wg[:, f, :, :], gw).then_inc(ld_we[f], 16)
                sp.dma_start(wu[:, f, :, :], uw).then_inc(ld_we[f], 16)
                sp.dma_start(wd[:, f, :, :], dw).then_inc(ld_we[f], 16)

            sp.wait_ge(otr_mm, B)
            sp.wait_ge(h_ready, 4 * B + 1)
            for f in range(2):
                load_expert(f, f)
            sp.wait_ge(zero_ready, 1)
            sp.dma_start(eout[ZROW:ZROW + 1, :], zrow[:, :]).then_inc(st_z, 16)

            sp.wait_ge(disp_mm, 8)
            sp.dma_start(nwb[:, :], a["nw"].partition_broadcast(P)).then_inc(ld_w13, 16)
            sp.dma_start(w13f, a["w13T"].rearrange("(k p) n -> p k n", p=P)).then_inc(ld_w13, 16)
            sp.dma_start(w2f[:, 0:5, :], a["w2T"][0:5 * P, :].rearrange("(k p) n -> p k n", p=P),
                         ).then_inc(ld_w13, 16)
            sp.dma_start(w2f[0:HID - 5 * P, 5, :], a["w2T"][5 * P:HID, :]).then_inc(ld_w13, 16)

            with sp.Fori(0, E // 2 - 1) as i:
                for f in range(2):
                    sp.wait_ge(exd_mm, i * 2 + (f + 1) + 1)
                    load_expert(i * 2 + (2 + f), f)
                for f in range(2):
                    sp.wait_ge(exo_ready, i * 2 + (f + 1) + 1)
                    sp.dma_start(eout[bass.ds(i * (2 * CAP) + f * CAP, CAP), :], eoS[:, f, :],
                                 ).then_inc(st_eout, 16)
            for f in range(2):
                sp.wait_ge(exo_ready, E - 1 + f + 1)
                sp.dma_start(eout[(E - 2 + f) * CAP:(E - 1 + f) * CAP, :], eoS[:, f, :]).then_inc(st_eout, 16)
            with sp.Fori(0, B) as b:
                for t in range(TB):
                    sp.wait_ge(f_out, b * TB + (t + 1) + 1)
                    sp.dma_start(out[bass.ds(b * S + t * P, P), :], yt[:, t, :]).then_inc(st_out, 16)
            sp.wait_ge(st_out, 16 * NT + 16)
            sp.wait_ge(st_eout, 16 * E + 16)
            sp.wait_ge(st_z, 16)

        @block.tensor
        def _(pe):
            pe.sem_inc(nb_mm, 1)
            pe.sem_inc(agg_mm, 1)
            pe.sem_inc(et_mm, 1)
            pe.sem_inc(q_mm, 1)
            pe.sem_inc(et2_mm, 1)
            pe.sem_inc(cx_mm, 1)
            pe.sem_inc(exd_mm, 1)
            pe.sem_inc(o_mm, 1)
            pe.sem_inc(f_q1T_mm, 1)
            pe.sem_inc(f_a_mm, 1)
            pe.sem_inc(f_q2T_mm, 1)
            pe.sem_inc(f_o_mm, 1)
            pe.wait_ge(ld_gat, 16 * 6)
            pe.wait_ge(abd_ready, 4)
            for k in range(KT):
                mm = pe.matmul(bank[0][0:CD, 0:16], w0T[:, k, :], abd[:, 0, k, :], start=k == 0, stop=k == 1)
            mm.then_inc(wa_mm, 1)
            for f in range(KT):
                for k in range(KT):
                    mm = pe.matmul(bank[1 + f][:, 0:16], w1T[:, k, f * P:(f + 1) * P], abd[:, 1, k, :],
                                   start=k == 0, stop=k == 1)
            mm.then_inc(wa_mm, 1)
            pe.wait_ge(wa_ready, 6)
            pe.wait_ge(ld_const, 16 * 4)
            with pe.Fori(0, B) as b:
                for l in range(2):
                    r = b * 2 + l
                    nk = 1 if l == 0 else 2
                    ft = [ctxb[:, :]] if l == 0 else [hT[0][:, 0, :], hT[0][:, 1, :]]
                    if l == 0:
                        pe.wait_ge(ctxb_ready, b + 1)
                    else:
                        pe.wait_ge(h_ready, b * 4 + 2 + 1)
                    pe.wait_ge(agg_free, r + 1)
                    for t in range(TB):
                        for k in range(nk):
                            mm = pe.matmul(bank[6][:, t * GH:(t + 1) * GH], ft[k][:, t * P:(t + 1) * P],
                                           was[l][:, k, :], start=k == 0, stop=k == nk - 1)
                    mm.then_inc(self_mm, 1)
                    wl = w0 if l == 0 else w1
                    for t in range(TB):
                        for k in range(nk):
                            mm = pe.matmul(bank[7][:, t * D:(t + 1) * D], ft[k][:, t * P:(t + 1) * P],
                                           wl[:, k, :], start=k == 0, stop=k == nk - 1)
                    mm.then_inc(feat_mm, 1)
                    for q in range(4):
                        for h in (2 * q, 2 * q + 1):
                            for k in range(nk):
                                mm = pe.matmul(bank[q][:, (h % 2) * S:(h % 2 + 1) * S], wan[l][:, k, h, :],
                                               ft[k], start=k == 0, stop=k == nk - 1)
                        mm.then_inc(nb_mm, 1)
                    for h in range(GH + 1):
                        if h < GH:
                            pe.wait_ge(en_ready, r * 16 + (2 * h + 2) + 1)
                            pe.wait_ge(et_evac, r * 8 + max(h - 1, 0) + 1)
                            if l == 0 and h == 0:
                                pe.wait_ge(x1_ready, b + 1)
                            if l == 0 and h == 1:
                                pe.wait_ge(lnT_evac, b + 1)
                            for t in range(TB):
                                for m in range(TB):
                                    c = m * S + t * P
                                    mm = pe.transpose(bank[4 + h % 2][:, c:c + P],
                                                      Ex[:, h % 2, t, m * P:(m + 1) * P], ident[:, :])
                            mm.then_inc(et_mm, 1)
                        if h >= 1:
                            g = h - 1
                            if g == 0:
                                pe.wait_ge(self_evac, r * 2 + 2)
                                pe.wait_ge(feat_evac, r + 1)
                            pe.wait_ge(et_evac, r * 8 + (g + 1) + 1)
                            j = g % 4
                            for m in range(TB):
                                mm = pe.matmul(bank[6][32 * j:32 * j + 32, (g // 4) * S:(g // 4 + 1) * S],
                                               featS[:, m, g * GO:(g + 1) * GO], ETs[:, g % 2, m, :],
                                               start=m == 0, stop=m == 1, tile_position=(0, 32 * j))
                            mm.then_inc(agg_mm, 1)
                pe.wait_ge(h_ready, b * 4 + 4 + 1)
                pe.wait_ge(et_evac, b * 16 + 16 + 1)
                for t in range(TB):
                    for g in range(KT):
                        c = t * D + g * P
                        mm = pe.transpose(bank[4][:, c:c + P], hT[1][:, g, t * P:(t + 1) * P], ident[:, :])
                mm.then_inc(otr_mm, 1)
                pe.wait_ge(xln_ready, b + 1)
                for k in range(KT):
                    for t in range(TB):
                        c = k * S + t * P
                        mm = pe.transpose(bank[5][:, c:c + P], xln[:, t, k * P:(k + 1) * P], ident[:, :])
                mm.then_inc(lnT_mm, 1)

            pe.wait_ge(lnT_evac, B + 1)
            pe.wait_ge(ld_ffn0, 16 * 5)
            for t in range(NT):
                for k in range(KT):
                    mm = pe.matmul(bank[7][:, t * E:(t + 1) * E], xlnT[:, k, t * P:(t + 1) * P], gwT[:, k, :],
                                   start=k == 0, stop=k == 1)
            mm.then_inc(logit_mm, 1)

            pe.wait_ge(ld_attn, 16 * 6)
            for q in range(4):
                for h in range(4 * q, 4 * q + 4):
                    for t in range(2):
                        c = (h % 4 * 2 + t) * CD
                        mm = pe.matmul(bank[q][0:96, c:c + CD], qrT[:, h, t * 96:(t + 1) * 96], krT[:, h, :],
                                       start=True, stop=True)
                mm.then_inc(c_mm, 1)
            for q in range(2):
                pe.wait_ge(c_evac, 2 * q + 2)
                for h in range(8 * q, 8 * q + 8):
                    for t in range(2):
                        mm = pe.matmul(bank[4 + q][:, h % 8 * CD:(h % 8 + 1) * CD], kcqT[:, t, h * AK:(h + 1) * AK],
                                       chs[:, (h * 2 + t) * CD:(h * 2 + t + 1) * CD], start=t == 0, stop=t == 1)
                mm.then_inc(d_mm, 1)
            for q in range(4):
                pe.wait_ge(d_evac, q // 2 + 1)
                for h in range(4 * q, 4 * q + 4):
                    for t in range(2):
                        c = (h % 4 * 2 + t) * CD
                        mm = pe.matmul(bank[q][:, c:c + CD], wq[:, h, t * P:(t + 1) * P],
                                       dhs[:, h * CD:(h + 1) * CD], start=True, stop=True)
                mm.then_inc(n_mm, 1)
            for q in range(4):
                pe.wait_ge(d_evac, 2)
                pe.wait_ge(p_evac, max(q - 1, 0))
                for h in range(4 * q, 4 * q + 4):
                    mm = pe.matmul(bank[4 + q % 2][h % 2 * CD:(h % 2 + 1) * CD, h % 4 // 2 * D:(h % 4 // 2 + 1) * D],
                                   kckv[:, h, :], wo[:, h, :], start=True, stop=True,
                                   tile_position=(0, h % 2 * CD))
                mm.then_inc(p_mm, 1)
            n = 0
            for c in range(2):
                for i in range(3):
                    m = min(P, IS - i * P)
                    pe.wait_ge(shm_ready, max(n - 1, 0))
                    if n == 0:
                        pe.wait_ge(n_evac, 4)
                        pe.wait_ge(p_evac, 4)
                    for wt, bk in ((swg, 0), (swu, 2)):
                        for k in range(KT):
                            mm = pe.matmul(bank[bk + n % 2][0:m, :], wt[:, k, i * P:i * P + m],
                                           xlnT[:, k, c * 512:(c + 1) * 512], start=k == 0, stop=k == 1)
                    mm.then_inc(shg_mm, 1)
                    n += 1
                pe.wait_ge(shm_ready, n)
                for t in range(4):
                    pe.wait_ge(shd_add, max(c * 4 + t - 1, 0))
                    for i in range(3):
                        m = min(P, IS - i * P)
                        mm = pe.matmul(bank[4 + t % 2][:, 0:D], smid[0:m, i, t * P:(t + 1) * P], swd[0:m, i, :],
                                       start=i == 0, stop=i == 2)
                    mm.then_inc(shd_mm, 1)

            pe.wait_ge(sel_ready, 1)
            mm = pe.matmul(bank[6][:, 0:P], upper[:, :], selb[:, :, :].rearrange("p t e -> p (t e)"),
                           start=True, stop=True)
            for k in range(1, NT):
                mm = pe.matmul(bank[6][:, k * E:P], onesb[:, :], selb[:, 0:NT - k, :].rearrange("p t e -> p (t e)"),
                               start=False, stop=True, skip_group_check=True)
            mm.then_inc(rank_mm, 1)

            pe.wait_ge(disp_ready, NT)
            n = 0
            for g in range(4):
                for k in range(KT):
                    pe.wait_ge(disp_evac, max(n - 1, 0))
                    for t in range(NT):
                        for i, part in enumerate((xhi, xlo)):
                            mm = pe.matmul(bank[n % 2][:, :], part[:, t, k * P:(k + 1) * P],
                                           disp[:, t, 4 * g:4 * g + 4, :].rearrange("p e s -> p (e s)"),
                                           start=t == 0 and i == 0, stop=t == NT - 1 and i == 1)
                    mm.then_inc(disp_mm, 1)
                    n += 1
            pe.wait_ge(disp_evac, 8)

            with pe.Fori(0, E // 2) as i:
                for f in range(2):
                    e = i * 2 + f
                    pe.wait_ge(ld_we[f], i * 48 + 48)
                    pe.wait_ge(exm_ready, i * 2 + 1)
                    for wt, bk in ((wg, 0), (wu, 2)):
                        for j in range(2):
                            for k in range(KT):
                                mm = pe.matmul(bank[bk + f][0:IH, j * CAP:(j + 1) * CAP],
                                               wt[:, f, k, j * IH:(j + 1) * IH], xgT[:, k, bass.ds(e * CAP, CAP)],
                                               start=k == 0, stop=k == 1)
                    mm.then_inc(exg_mm, 1)
                for f in range(2):
                    pe.wait_ge(exm_ready, i * 2 + (f + 1) + 1)
                    pe.wait_ge(exo_ready, i * 2 + 1)
                    for j in range(2):
                        mm = pe.matmul(bank[4 + f][:, 0:D], emid[:, f, j, :], wd[:, f, j, :],
                                       start=j == 0, stop=j == 1)
                    mm.then_inc(exd_mm, 1)

            pe.wait_ge(exo_ready, E + 1)
            pe.wait_ge(shd_add, NT)
            pe.wait_ge(kvr_ready, 1)
            for b in range(B):
                pe.wait_ge(kvT_ready, 2 * b)
                for t in range(TB):
                    mm = pe.transpose(bank[6][:, t * P:(t + 1) * P],
                                      kvr[:, b * TB + t, :, :].rearrange("p a c -> p (a c)"), ident[:, :])
                mm.then_inc(kvT_mm, 1)
            pe.wait_ge(kvT_ready, 2 * B)
            with pe.Fori(0, B) as b:
                pe.wait_ge(l2_xln, b + 1)
                for k in range(KT):
                    for t in range(TB):
                        c = k * S + t * P
                        mm = pe.transpose(bank[6][:, c:c + P], xln[:, t, k * P:(k + 1) * P], ident[:, :])
                mm.then_inc(l2_T_mm, 1)
                pe.wait_ge(l2_T_evac, b + 1)
                for j in range(AH // 2):
                    pe.wait_ge(q_evac, b * 8 + max(j - 1, 0) + 1)
                    for k in range(KT):
                        mm = pe.matmul(bank[6 + j % 2][:, 0:S], Nw[:, k, j * P:(j + 1) * P], xT3[:, k, :],
                                       start=k == 0, stop=k == 1)
                    mm.then_inc(q_mm, 1)
                for j in range(AH // 2 + 1):
                    if j < AH // 2:
                        if j == 0:
                            pe.wait_ge(q_evac, b * 8 + 8 + 1)
                        for t in range(TB):
                            pe.wait_ge(ex2_ready, (b * 32 + max(4 * j - 4 + 2 * t + 2, 0) if j else b * 32) + 1)
                            mm = pe.matmul(bank[t][:, :], qT[:, j, t * P:(t + 1) * P],
                                           kblk[:, bass.ds(b, 1), :, :].rearrange("p b h s -> p (b h s)"),
                                           start=True, stop=True)
                            mm.then_inc(sc_mm, 1)
                    if j >= 1:
                        i = j - 1
                        pe.wait_ge(en2_ready, b * 32 + 4 * (i + 1) + 1)
                        for h in range(2):
                            pe.wait_ge(et2_evac, b * 16 + max(2 * i + h - 1, 0) + 1)
                            for t in range(TB):
                                for m in range(TB):
                                    c = m * S + t * P
                                    mm = pe.transpose(bank[2 + h][:, c:c + P], E2[:, i % 2, t, h, m * P:(m + 1) * P],
                                                      ident[:, :])
                            mm.then_inc(et2_mm, 1)
                        pe.wait_ge(cx_evac, b * 8 + max(i - 1, 0) + 1)
                        pe.wait_ge(kvb_ready, b + 1)
                        for h in range(2):
                            pe.wait_ge(et2_evac, b * 16 + (2 * i + h + 1) + 1)
                            for m in range(TB):
                                mm = pe.matmul(bank[4 + i % 2][h * CD:(h + 1) * CD, 0:S], kvb[:, m, :],
                                               ET2[:, i % 2, h, m, :], start=m == 0, stop=m == 1,
                                               tile_position=(0, h * CD))
                        mm.then_inc(cx_mm, 1)
                pe.wait_ge(cx_evac, b * 8 + 8 + 1)
                for t in range(TB):
                    for j in range(AH // 2):
                        mm = pe.matmul(bank[7][:, t * D:(t + 1) * D], cxT[:, j, t * P:(t + 1) * P], Pw[:, j, :],
                                       start=j == 0, stop=j == AH // 2 - 1)
                mm.then_inc(o_mm, 1)
                pe.wait_ge(x3_ready, b + 1)

            pe.wait_ge(wsplit_ready, 1)
            with pe.Fori(0, B) as b:
                for t in range(TB):
                    n = b * TB + t
                    pe.wait_ge(f_q1, n + 1)
                    pe.wait_ge(f_q1T, n + 1)
                    tr = bank[6][:, :].bitcast(BF16)
                    for k in range(KT):
                        mm = pe.transpose(tr[:, k * P:(k + 1) * P], q1[:, k * P:(k + 1) * P], identh[:, :])
                    mm.then_inc(f_q1T_mm, 1)
                    pe.wait_ge(f_q1T, n + 1 + 1)
                    pe.wait_ge(f_g_ready, n + 1)
                    for c in range(2):
                        for u in range(2):
                            lo = u * HID + c * (HID // 2)
                            i = 0
                            for part in range(3):
                                for k in range(KT):
                                    mm = pe.matmul(bank[2 * u + c][:, 0:HID // 2], q1T[:, k, :],
                                                   w13p[:, part, k, lo:lo + HID // 2], start=i == 0, stop=i == 5)
                                    i += 1
                    mm.then_inc(f_a_mm, 1)
                    pe.wait_ge(f_q2, n + 1 + 1)
                    tr = bank[7][:, :].bitcast(BF16)
                    for k in range(6):
                        m = min(P, HID - k * P)
                        mm = pe.transpose(tr[0:m, k * P:(k + 1) * P], q2[:, k * P:k * P + m], identh[:, :])
                    mm.then_inc(f_q2T_mm, 1)
                    pe.wait_ge(f_q2T, n + 1)
                    pe.wait_ge(f_out, n + 1)
                    for k in range(6):
                        m = min(P, HID - k * P)
                        for part in range(3):
                            mm = pe.matmul(bank[5][:, 0:D], q2T[0:m, k, :], w2p[0:m, part, k, :],
                                           start=k == 0 and part == 0, stop=k == 5 and part == 2)
                    mm.then_inc(f_o_mm, 1)

        @block.scalar
        def _(act):
            act.sem_inc(et_evac, 1)
            act.sem_inc(lnT_evac, 1)
            act.sem_inc(exo_ready, 1)
            act.sem_inc(q_evac, 1)
            act.sem_inc(ex2_ready, 1)
            act.sem_inc(et2_evac, 1)
            act.sem_inc(exp_done, 1)
            act.sem_inc(elu_exp, 1)
            act.sem_inc(f_sq_ready, 1)
            with act.Fori(0, B) as b:
                act.wait_ge(ld_ctxT, 16)
                act.wait_ge(nb_mm, b * 8 + 1)
                act.activation(ctxb[:, :], ctxT[:, bass.ds(b * S, S)], ACT.Copy).then_inc(ctxb_ready, 1)
                for l in range(2):
                    r = b * 2 + l
                    act.wait_ge(feat_mm, r + 1)
                    act.wait_ge(agg_mm, r * 8 + 1)
                    act.activation(featS[:, :, :].rearrange("p t d -> p (t d)"), bank[7][:, :],
                                   ACT.Copy).then_inc(feat_evac, 1)
                    act.wait_ge(leak_done, r * 16 + 1)
                    act.wait_ge(u_ready, r * 16 + 1)
                    for q in range(2):
                        act.wait_ge(nb_mm, r * 4 + (q + 1) + 1)
                        act.activation(NB[:, 2 * q:2 * q + 2, :].rearrange("p h s -> p (h s)"), bank[q][:, :],
                                       ACT.Copy).then_inc(nb_evac, 1)
                    for h in range(GH + 1):
                        if h < GH:
                            act.wait_ge(et_mm, r * 8 + max(h - 1, 0) + 1)
                            act.wait_ge(rinv_ready, r * 8 + max(h - 1, 0) + 1)
                            for t in range(TB):
                                act.wait_ge(e_ready, r * 16 + (2 * h + t + 1))
                                act.activation(Ex[:, h % 2, t, :], L[:, h % 2, t, :], ACT.Exp,
                                               bias=M[:, h % 2, t:t + 1], scale=-1.0,
                                               accum_out=Sm[:, h % 2, t:t + 1]).then_inc(exp_done, 1)
                        if h >= 1:
                            g = h - 1
                            act.wait_ge(et_mm, r * 8 + (g + 1) + 1)
                            act.wait_ge(agg_mm, r * 8 + max(g - 1, 0) + 1)
                            act.activation(ETs[:, g % 2, :, :].rearrange("p t s -> p (t s)"), bank[4 + g % 2][:, :],
                                           ACT.Copy).then_inc(et_evac, 1)
                    act.wait_ge(h_ready, r * 2 + 1)
                    for g in range(KT):
                        act.wait_ge(elu_min, r * 2 + (g + 1))
                        act.activation(e0[:, g, :], m0[:, g, :], ACT.Exp).then_inc(elu_exp, 1)
                act.wait_ge(lnT_mm, b + 1)
                act.activation(xlnT[:, :, bass.ds(b * S, S)], bank[5][:, :].rearrange("p (k s) -> p k s", k=KT),
                               ACT.Copy).then_inc(lnT_evac, 1)

            act.wait_ge(route_exp_in, 1)
            act.activation(prob[:, :, :], prob[:, :, :], ACT.Exp).then_inc(route_exp, 1)

            for q in range(4):
                act.wait_ge(c_mm, q + 1)
                act.activation(chs[:, q * 512:(q + 1) * 512], bank[q][0:96, :], ACT.Copy).then_inc(c_evac, 1)
            for q in range(2):
                act.wait_ge(d_mm, q + 1)
                act.activation(dhs[:, q * 512:(q + 1) * 512], bank[4 + q][:, :], ACT.Copy).then_inc(d_evac, 1)
            for q in range(4):
                act.wait_ge(n_mm, q + 1)
                src = bank[q][:, :].rearrange("p (h t c) -> p h t c", h=4, t=2)
                dst = Nw[:, :, q * 4 * CD:(q + 1) * 4 * CD].rearrange("p t (h c) -> p t h c", h=4)
                for t in range(2):
                    ins = act.activation(dst[:, t, :, :], src[:, :, t, :], ACT.Copy)
                    if t == 0:
                        ins.then_inc(act_step, 1)
                ins.then_inc(n_evac, 1)
            for q in range(4):
                act.wait_ge(p_mm, q + 1)
                act.activation(Pw[:, 2 * q:2 * q + 2, :].rearrange("p j d -> p (j d)"), bank[4 + q % 2][:, :],
                               ACT.Copy).then_inc(p_evac, 1)
            n = 0
            for c in range(2):
                for i in range(3):
                    m = min(P, IS - i * P)
                    act.wait_ge(shg_mm, n + 1)
                    act.wait_ge(shm_ready, n)
                    act.activation(sgs[0:m, :], bank[n % 2][0:m, :], ACT.Silu).then_inc(shs_ready, 1)
                    n += 1

            for n in range(0, 8, 2):
                act.wait_ge(disp_mm, n + 1)
                act.activation(xgT[:, 0, n // 2 * 512:(n // 2 + 1) * 512], bank[n % 2][:, :],
                               ACT.Copy).then_inc(disp_evac, 1)
                act.wait_ge(disp_mm, n + 2)
                act.activation(xgT[:, 1, n // 2 * 512:(n // 2 + 1) * 512], bank[1][:, :],
                               ACT.Copy).then_inc(disp_evac, 1)
            with act.Fori(0, E // 2) as i:
                for f in range(2):
                    act.wait_ge(exg_mm, i * 2 + (f + 1))
                    act.wait_ge(exm_ready, i * 2 + f + 1)
                    act.activation(esg[:, f, :], bank[f][0:IH, 0:2 * CAP], ACT.Silu).then_inc(exs_ready, 1)
                act.wait_ge(st_eout, i * 32 + 16)
                for f in range(2):
                    act.wait_ge(exd_mm, i * 2 + (f + 1) + 1)
                    act.activation(eoS[:, f, :], bank[4 + f][:, 0:D], ACT.Copy).then_inc(exo_ready, 1)

            act.wait_ge(zero_ready, 2)
            for b in range(B):
                act.wait_ge(kvT_mm, b + 1)
                for h in range(2):
                    act.activation(kblk[h * CD:(h + 1) * CD, b, h, :], bank[6][h * CD:(h + 1) * CD, 0:S],
                                   ACT.Copy).then_inc(kvT_ready, 1)

            with act.Fori(0, B) as b:
                act.wait_ge(l2_T_mm, b + 1)
                act.wait_ge(q_mm, b * 8 + 1)
                act.activation(xT3[:, :, :].rearrange("p k s -> p (k s)"), bank[6][:, :],
                               ACT.Copy).then_inc(l2_T_evac, 1)
                for j in range(AH // 2):
                    act.wait_ge(q_mm, b * 8 + (j + 1) + 1)
                    act.activation(qT[:, j, :], bank[6 + j % 2][:, 0:S], ACT.Copy).then_inc(q_evac, 1)
                for j in range(AH // 2 + 1):
                    if j < AH // 2:
                        act.wait_ge(et2_mm, b * 16 + max(2 * j - 2, 0) + 1)
                        act.wait_ge(ri2_ready, b * 8 + max(j - 1, 0) + 1)
                        for t in range(TB):
                            act.wait_ge(mx_ready, b * 16 + (2 * j + t + 1))
                            for h in range(2):
                                act.activation(E2[:, j % 2, t, h, :], bank[t][:, h * S:(h + 1) * S], ACT.Exp,
                                               bias=nmx[:, j % 2, t, h:h + 1],
                                               accum_out=S2[:, j % 2, t, h:h + 1]).then_inc(ex2_ready, 1)
                    if j >= 1:
                        i = j - 1
                        act.wait_ge(et2_mm, b * 16 + (2 * i + 1) + 1)
                        act.wait_ge(cx_mm, b * 8 + max(i - 1, 0) + 1)
                        act.activation(ET2[:, i % 2, 0, :, :].rearrange("p t s -> p (t s)"), bank[2][:, :],
                                       ACT.Copy).then_inc(et2_evac, 1)

            with act.Fori(0, B) as b:
                for t in range(TB):
                    n = b * TB + t
                    act.wait_ge(f_g_ready, n + 1)
                    for c in range(2):
                        act.wait_ge(f_a_mm, n + 1 + 1)
                        act.activation(r1[:, c, :], bank[c][:, 0:HID // 2], ACT.Relu,
                                       scale=is1[:, :]).then_inc(f_relu, 1)
                    act.wait_ge(f_relu, n * 2 + 2)
                    act.activation(r2[:, :, :], r1[:, :, :], ACT.Square).then_inc(f_r_ready, 1)
                    act.wait_ge(f_g_ready, n + 1 + 1)
                    act.wait_ge(f_q2, n + 1)
                    act.activation(r1[:, :, :].rearrange("p c n -> p (c n)"), gated[:, :], ACT.Square,
                                   accum_out=ms[:, :]).then_inc(f_sq_ready, 1)

        @block.vector
        def _(dve):
            dve.sem_inc(agg_free, 1)
            dve.sem_inc(x1_ready, 1)
            dve.sem_inc(exm_ready, 1)
            dve.sem_inc(cx_evac, 1)
            dve.sem_inc(f_q1T, 1)
            dve.sem_inc(f_g_ready, 1)
            dve.sem_inc(f_out, 1)
            dve.sem_inc(leak_done, 1)
            dve.sem_inc(rinv_ready, 1)
            dve.sem_inc(h_ready, 1)
            dve.sem_inc(ri2_ready, 1)
            dve.sem_inc(f_q2, 1)
            steps = [0]

            def link(ins, base=0, alone=False):
                steps[0] += 1
                ins.then_inc(dve_step, 1)
                count = base + steps[0]
                if alone:
                    count = dve.to_reg(count)
                    dve.wait_ge(consts_ready, 1)
                dve.wait_ge(dve_step, count)

            def layernorm(b, base, veps_sem, rstd_sem, count, dst):
                for t in range(TB):
                    x = X[:, bass.ds(b * TB + t, 1), :].rearrange("p o d -> p (o d)")
                    link(dve.bn_stats(bnst[:, t, :], x), base, True)
                link(dve.bn_aggr(mv[:, 0, :], bnst[:, 0, :]), base, True)
                link(dve.bn_aggr(mv[:, 1, :], bnst[:, 1, :]), base)
                dve.tensor_scalar(veps[:, :], mv[:, :, 1], LN_EPS, None, ALU.add).then_inc(veps_sem, 1)
                dve.wait_ge(rstd_sem, count)
                for t in range(TB):
                    link(dve.tensor_scalar(dst[:, t, :], X[:, bass.ds(b * TB + t, 1), :].rearrange("p o d -> p (o d)"),
                                           mv[:, t, 0:1], rstd[:, t:t + 1], ALU.subtract, ALU.mult), base)

            dve.memset(half[:, :], -0.5).then_inc(consts_ready, 1)
            dve.memset(zrow[:, :], 0.0).then_inc(zero_ready, 1)
            dve.memset(onesb[:, :], 1.0).then_inc(big_ready, 1)
            dve.memset(Lp[:, :, E:E + TOPK], BIG).then_inc(big_ready, 1)
            dve.wait_ge(ld_gat, 16 * 6)
            for l in range(2):
                for i in range(2):
                    dve.tensor_tensor(abd[:, l, :, i * GH:(i + 1) * GH], blockmask[:, :, :],
                                      acol[:, l, i, :].unsqueeze(2).to_broadcast([P, KT, GH]),
                                      ALU.mult).then_inc(abd_ready, 1)
            dve.wait_ge(ld_const, 16 * 4)
            dve.tensor_copy(identh[:, :], ident[:, :]).then_inc(big_ready, 1)
            dve.tensor_copy(upper[:, :], upperf[:, :]).then_inc(big_ready, 1)
            dve.tensor_copy(iotah[:, :], iotaf[:, :]).then_inc(big_ready, 1)
            dve.wait_ge(wa_mm, 1)
            dve.tensor_copy(was[0][:, 0, :], bank[0][0:CD, 0:GH]).then_inc(wa_ready, 1)
            dve.tensor_copy(wan[0][:, 0, :, :], bank[0][0:CD, GH:2 * GH].unsqueeze(2).to_broadcast([CD, GH, P]),
                            ).then_inc(wa_ready, 1)
            dve.wait_ge(wa_mm, 2)
            for f in range(KT):
                dve.tensor_copy(was[1][:, f, :], bank[1 + f][:, 0:GH]).then_inc(wa_ready, 1)
                dve.tensor_copy(wan[1][:, f, :, :], bank[1 + f][:, GH:2 * GH].unsqueeze(2).to_broadcast([P, GH, P]),
                                ).then_inc(wa_ready, 1)

            dve.wait_ge(ld_x, 16)
            GAT_STEPS = 16
            with dve.Fori(0, B) as b:
                base = b * GAT_STEPS
                steps[0] = 0
                layernorm(b, base, veps_ready, rstd_ready, b * 2 + 1, maskN)
                link(dve.tensor_scalar(maskN[:, :, :], maskN[:, :, :], 1.0, -MASK, ALU.subtract, ALU.mult), base)
                for l in range(2):
                    r = b * 2 + l
                    dve.wait_ge(self_mm, r + 1)
                    dve.wait_ge(u_ready, r * 16 + 1)
                    selfp = bank[6][:, 0:TB * GH].rearrange("p (t h) -> p t h", t=TB)
                    dve.tensor_copy(selfS[:, :, :], selfp).then_inc(self_evac, 1)
                    dve.tensor_scalar(self02[:, :, :], selfp, 0.2, None, ALU.mult).then_inc(self_evac, 1)
                    dve.wait_ge(self_evac, r * 2 + 2)
                    for q in range(2, 4):
                        dve.wait_ge(nb_mm, r * 4 + (q + 1) + 1)
                        dve.tensor_copy(NB[:, 2 * q:2 * q + 2, :].rearrange("p h s -> p (h s)"),
                                        bank[q][:, :]).then_inc(nb_evac, 1)
                    dve.wait_ge(nb_evac, r * 4 + 4)
                    for h in range(GH + 1):
                        if h < GH:
                            dve.wait_ge(u_ready, r * 16 + (2 * h + 2) + 1)
                            dve.wait_ge(exp_done, r * 16 + 2 * max(h - 1, 0) + 1)
                            for t in range(TB):
                                dve.scalar_tensor_tensor(L[:, h % 2, t, :], NB[:, h, :], selfS[:, t, h:h + 1],
                                                         U[:, h % 2, t, :], ALU.add, ALU.min,
                                                         ).then_inc(leak_done, 1)
                            for t in range(TB):
                                held = dve.to_reg(r * 16 + (2 * h + t + 1) + 1)
                                dve.wait_ge(consts_ready, 1)
                                dve.wait_ge(leak_done, held)
                                dve.tensor_tensor_reduce(L[:, h % 2, t, :], L[:, h % 2, t, :], maskN[:, t, :],
                                                         1.0, 3.4e38, ALU.add, ALU.min, M[:, h % 2, t:t + 1],
                                                         ).then_inc(e_ready, 1)
                        if h >= 1:
                            g = h - 1
                            dve.wait_ge(exp_done, r * 16 + (2 * g + 2) + 1)
                            dve.wait_ge(en_ready, r * 16 + 2 * max(g - 1, 0) + 1)
                            dve.reciprocal(Ri[:, g % 2, :], Sm[:, g % 2, :]).then_inc(rinv_ready, 1)
                    dve.wait_ge(agg_mm, r * 8 + 8 + 1)
                    dve.wait_ge(elu_exp, r * 2 + 1)
                    for g in range(KT):
                        dve.tensor_scalar(m0[:, g, :], bank[6][:, g * S:(g + 1) * S], bcol[:, l, g:g + 1], 0.0,
                                          ALU.add, ALU.min).then_inc(elu_min, 1)
                    for g in range(KT):
                        ins = dve.tensor_scalar(r0[:, g, :], bank[6][:, g * S:(g + 1) * S], bcol[:, l, g:g + 1],
                                                0.0, ALU.add, ALU.max)
                        if g == 0:
                            ins.then_inc(elu_max, 1)
                    ins.then_inc(agg_free, 1)
                    dve.wait_ge(agg_free, r + 1 + 1)
                    for g in range(KT):
                        dve.wait_ge(elu_exp, r * 2 + (g + 1) + 1)
                        dve.scalar_tensor_tensor(hT[l][:, g, :], e0[:, g, :], -1.0, r0[:, g, :], ALU.add,
                                                 ALU.add).then_inc(h_ready, 1)
                dve.wait_ge(otr_mm, b + 1)
                xb = X[:, bass.ds(b * TB, TB), :].rearrange("p t d -> p (t d)")
                dve.tensor_tensor(xb, xb, bank[4][:, :], ALU.add).then_inc(x1_ready, 1)
                held = dve.to_reg(b + 1 + 1)
                dve.wait_ge(consts_ready, 1)
                dve.wait_ge(x1_ready, held)
                layernorm(b, base, veps_ready, rstd_ready, b * 2 + 2, xln)
                xh = xhi[:, bass.ds(b * TB, TB), :]
                dve.tensor_copy(xh, xln[:, :, :]).then_inc(xln_ready, 1)
                dve.wait_ge(xln_ready, b + 1)
                link(dve.tensor_tensor(xlo[:, bass.ds(b * TB, TB), :], xln[:, :, :], xh, ALU.subtract), base, True)
                held = dve.to_reg(b + 1)
                dve.wait_ge(consts_ready, 1)
                dve.wait_ge(lnT_mm, held)
                assert steps[0] <= GAT_STEPS, steps[0]
                while steps[0] < GAT_STEPS:
                    steps[0] += 1
                    dve.engine_nop().then_inc(dve_step, 1)
            base = B * GAT_STEPS
            steps[0] = 0

            dve.wait_ge(big_ready, 5)
            dve.wait_ge(logit_mm, 1)
            link(dve.tensor_copy(Lp[:, :, 0:E], bank[7][:, 0:NT * E].rearrange("p (t e) -> p t e", t=NT)), base)
            for t in range(NT):
                link(dve.max(top8[:, t, :], Lp[:, t, :]), base)
            dve.tensor_tensor(prob[:, :, :], Lp[:, :, 0:E], top8[:, :, 4:5].to_broadcast([P, NT, E]),
                              ALU.subtract).then_inc(route_exp_in, 1)
            for t in range(NT):
                link(dve.match_replace(rep[:, t, :], top8[:, t, :], Lp[:, t, :], -BIG), base)
            link(dve.tensor_scalar(sel[:, :, :], rep[:, :, 0:E], -BIG, None, ALU.is_equal), base)
            dve.tensor_copy(selb[:, :, :], sel[:, :, :]).then_inc(sel_ready, 1)
            dve.wait_ge(route_exp, 1)
            link(dve.tensor_reduce(ssum[:, :], prob[:, :, :], AX_X, ALU.add), base)
            link(dve.reciprocal(srec[:, :], ssum[:, :]), base)
            link(dve.tensor_tensor(prob[:, :, :], prob[:, :, :], srec[:, :].unsqueeze(2).to_broadcast([P, NT, E]),
                                   ALU.mult), base)
            link(dve.tensor_tensor(wgt[:, :, :], prob[:, :, :], sel[:, :, :], ALU.mult), base)
            link(dve.tensor_reduce(ssum[:, :], wgt[:, :, :], AX_X, ALU.add), base)
            link(dve.tensor_scalar(ssum[:, :], ssum[:, :], 1e-20, None, ALU.add), base)
            link(dve.reciprocal(srec[:, :], ssum[:, :]), base)
            link(dve.tensor_tensor(wgt[:, :, :], wgt[:, :, :], srec[:, :].unsqueeze(2).to_broadcast([P, NT, E]),
                                   ALU.mult), base)

            n = 0
            m = 0
            for c in range(2):
                for i in range(3):
                    rows = min(P, IS - i * P)
                    dve.wait_ge(shs_ready, n + 1)
                    dve.wait_ge(shd_mm, c * 4)
                    dve.tensor_tensor(smid[0:rows, i, :], sgs[0:rows, :], bank[2 + n % 2][0:rows, :],
                                      ALU.mult).then_inc(shm_ready, 1)
                    n += 1
                for t in range(4):
                    dve.wait_ge(shd_mm, c * 4 + t + 1)
                    dve.tensor_tensor(X[:, c * 4 + t, :], X[:, c * 4 + t, :], bank[4 + t % 2][:, 0:D],
                                      ALU.add).then_inc(shd_add, 1)

            dve.wait_ge(rank_mm, 1)
            rank = bank[6][:, 0:NT * E].rearrange("p (t e) -> p t e", t=NT)
            link(dve.scalar_tensor_tensor(keep[:, :, :], rank, float(CAP), sel[:, :, :], ALU.is_lt, ALU.mult), base)
            link(dve.scalar_tensor_tensor(slotf[:, :, :], rank, NO_SLOT, keep[:, :, :], ALU.subtract, ALU.mult), base)
            link(dve.tensor_scalar(slotv[:, :, :], slotf[:, :, :], NO_SLOT, None, ALU.add), base)
            dve.wait_ge(n_evac, 4)
            dve.wait_ge(p_evac, 4)
            for t in range(NT):
                dve.tensor_tensor(disp[:, t, :, :], iotah[:, :].unsqueeze(1).to_broadcast([P, E, CAP]),
                                  slotv[:, t, :].unsqueeze(2).to_broadcast([P, E, CAP]),
                                  ALU.is_equal).then_inc(disp_ready, 1)
            link(dve.tensor_tensor(key[:, :, :], rowof[:, :].unsqueeze(1).to_broadcast([P, NT, E]), rank,
                                   ALU.subtract), base)
            link(dve.tensor_tensor(key[:, :, :], key[:, :, :], keep[:, :, :], ALU.mult), base)
            for t in range(NT):
                link(dve.max(keytop[:, t, :], key[:, t, :]), base)
            dve.tensor_scalar(idx[:, :, :], keytop[:, :, 0:TOPK], -1.0, float(ZROW), ALU.mult,
                              ALU.add).then_inc(idx_ready, 1)
            link(dve.tensor_tensor(eq[:, :, :, :], key[:, :, :].unsqueeze(2).to_broadcast([P, NT, TOPK, E]),
                                   keytop[:, :, 0:TOPK].unsqueeze(3).to_broadcast([P, NT, TOPK, E]),
                                   ALU.is_equal), base)
            link(dve.tensor_tensor(eq[:, :, :, :], eq[:, :, :, :],
                                   wgt[:, :, :].unsqueeze(2).to_broadcast([P, NT, TOPK, E]), ALU.mult), base)
            link(dve.tensor_reduce(wk[:, :, :], eq[:, :, :, :], AX_X, ALU.add), base)

            with dve.Fori(0, E // 2) as i:
                for f in range(2):
                    dve.wait_ge(exs_ready, i * 2 + (f + 1))
                    dve.wait_ge(exd_mm, i * 2 + 1)
                    dve.tensor_tensor(emid[:, f, :, :].rearrange("p j c -> p (j c)"), esg[:, f, :],
                                      bank[2 + f][0:IH, 0:2 * CAP], ALU.mult).then_inc(exm_ready, 1)

            dve.wait_ge(exg_mm, E)
            dve.memset(kblk[:, :, :, :], 0.0).then_inc(zero_ready, 1)

            dve.wait_ge(ld_w13, 16 * 4)
            for src, dst, sl in ((w13f, w13p, (slice(0, P), slice(0, KT))), (w2f, w2p, (slice(0, P), slice(0, 5))),
                                 (w2f, w2p, (slice(0, HID - 5 * P), slice(5, 6)))):
                x = src[sl[0], sl[1], :]
                for part in range(3):
                    y = dst[sl[0], part, sl[1], :]
                    ins = dve.tensor_copy(y, x)
                    if part < 2:
                        link(ins, base)
                        link(dve.tensor_tensor(x, x, y, ALU.subtract), base)
                    else:
                        link(ins, base)
            dve.engine_nop().then_inc(wsplit_ready, 1)

            for t in range(NT):
                dve.wait_ge(g_ld[t], 16 * TOPK)
                for k in range(TOPK):
                    link(dve.scalar_tensor_tensor(X[:, t, :], gath[:, t * TOPK + k, :], wk[:, t, k:k + 1],
                                                  X[:, t, :], ALU.mult, ALU.add), base)
            base += steps[0]

            ATT_STEPS = 8
            with dve.Fori(0, B) as b:
                base2 = b * ATT_STEPS + base
                steps[0] = 0
                layernorm(b, base2, l2_veps, l2_rstd, b + 1, xln)
                dve.wait_ge(cx_mm, b * 8 + 1)
                dve.tensor_copy(kvb[:, :, :], kvr[:, bass.ds(b * TB, TB), 0, :]).then_inc(kvb_ready, 1)
                held = dve.to_reg(b + 1)
                dve.wait_ge(consts_ready, 1)
                dve.wait_ge(kvb_ready, held)
                dve.engine_nop().then_inc(l2_xln, 1)
                for j in range(AH // 2 + 1):
                    if j < AH // 2:
                        dve.wait_ge(ex2_ready, b * 32 + 4 * max(j - 1, 0) + 1)
                        for t in range(TB):
                            dve.wait_ge(sc_mm, b * 16 + (2 * j + t + 1))
                            dve.tensor_reduce(nmx[:, j % 2, t, :], bank[t][:, :].rearrange("p (h s) -> p h s", h=2),
                                              AX_X, ALU.max, negate=True).then_inc(mx_ready, 1)
                    if j >= 1:
                        i = j - 1
                        dve.wait_ge(ex2_ready, b * 32 + 4 * (i + 1) + 1)
                        dve.wait_ge(en2_ready, b * 32 + 4 * max(i - 1, 0) + 1)
                        dve.reciprocal(R2[:, i % 2, :, :], S2[:, i % 2, :, :]).then_inc(ri2_ready, 1)
                        dve.wait_ge(et2_mm, b * 16 + (2 * i + 2) + 1)
                        dve.wait_ge(cx_mm, b * 8 + max(i - 1, 0) + 1)
                        dve.wait_ge(et2_evac, b * 16 + (2 * i + 1) + 1)
                        dve.tensor_copy(ET2[:, i % 2, 1, :, :].rearrange("p t s -> p (t s)"),
                                        bank[3][:, :]).then_inc(et2_evac, 1)
                        dve.wait_ge(cx_mm, b * 8 + (i + 1) + 1)
                        dve.wait_ge(o_mm, b + 1)
                        dve.tensor_copy(cxT[:, i, :], bank[4 + i % 2][:, 0:S]).then_inc(cx_evac, 1)
                dve.wait_ge(o_mm, b + 1 + 1)
                xb = X[:, bass.ds(b * TB, TB), :].rearrange("p t d -> p (t d)")
                dve.tensor_tensor(xb, xb, bank[7][:, :], ALU.add).then_inc(x3_ready, 1)
                assert steps[0] <= ATT_STEPS, steps[0]
                while steps[0] < ATT_STEPS:
                    steps[0] += 1
                    dve.engine_nop().then_inc(dve_step, 1)
            base += B * ATT_STEPS
            dve.wait_ge(x3_ready, B)

            FF_STEPS = 40
            with dve.Fori(0, B) as b:
                base3 = b * FF_STEPS + base
                steps[0] = 0
                layernorm(b, base3, f_veps, f_rstd, b + 1, xln)
                for t in range(TB):
                    n = b * TB + t

                    def quantise(dst, x, tmp, inv):
                        link(dve.tensor_reduce(amax[:, :], x, AX_X, ALU.max, apply_absolute_value=True), base3)
                        link(dve.tensor_scalar(amax[:, :], amax[:, :], 1e-5, None, ALU.max), base3)
                        link(dve.tensor_scalar(inv, amax[:, :], 1.0 / 127.0, None, ALU.mult), base3)
                        link(dve.reciprocal(amax[:, :], amax[:, :]), base3)
                        link(dve.tensor_scalar(amax[:, :], amax[:, :], 127.0, None, ALU.mult), base3)
                        link(dve.tensor_scalar(tmp, x, amax[:, 0:1], ROUND, ALU.mult, ALU.add), base3)
                        link(dve.tensor_scalar(tmp, tmp, ROUND, 127.0, ALU.subtract, ALU.min), base3)
                        return dve.tensor_scalar(dst, tmp, -128.0, None, ALU.max)

                    dve.wait_ge(f_q1T_mm, n + 1)
                    dve.wait_ge(f_sq_ready, n + 1)
                    quantise(q1[:, :], xln[:, t, :], tmpq[:, 0:D], is1[:, :]).then_inc(f_q1, 1)
                    dve.wait_ge(f_q1T_mm, n + 1 + 1)
                    dve.wait_ge(f_a_mm, n + 1)
                    dve.tensor_copy(q1T[:, :, :].rearrange("p k s -> p (k s)"),
                                    bank[6][:, :].bitcast(BF16)[:, 0:KT * P]).then_inc(f_q1T, 1)
                    dve.wait_ge(f_r_ready, n + 1)
                    for c in range(2):
                        ins = dve.scalar_tensor_tensor(gated[:, c * 352:(c + 1) * 352], bank[2 + c][:, 0:HID // 2],
                                                       is1[:, 0:1], r2[:, c, :], ALU.mult, ALU.mult)
                        if c == 0:
                            link(ins, base3)
                    ins.then_inc(f_g_ready, 1)
                    dve.wait_ge(f_sq_ready, n + 1 + 1)
                    dve.tensor_scalar(msq[:, :], ms[:, :], 1.0 / HID, RMS_EPS, ALU.mult, ALU.add,
                                      ).then_inc(f_ms, 1)
                    dve.wait_ge(f_rms, n + 1)
                    link(dve.scalar_tensor_tensor(gated[:, :], gated[:, :], rms[:, 0:1], nwb[:, :], ALU.mult,
                                                  ALU.mult), base3)
                    dve.wait_ge(f_q2T_mm, n + 1)
                    quantise(q2[:, :], gated[:, :], tmpq[:, :], is2[:, :]).then_inc(f_q2, 1)
                    dve.wait_ge(f_q2T_mm, n + 1 + 1)
                    dve.wait_ge(f_o_mm, n + 1)
                    tr = bank[7][:, :].bitcast(BF16)
                    link(dve.tensor_copy(q2T[:, 0:5, :].rearrange("p k s -> p (k s)"), tr[:, 0:5 * P]), base3)
                    dve.tensor_copy(q2T[0:HID - 5 * P, 5, :], tr[0:HID - 5 * P, 5 * P:6 * P]).then_inc(f_q2T, 1)
                    dve.wait_ge(f_o_mm, n + 1 + 1)
                    dve.wait_ge(st_out, b * 32 + 16)
                    dve.scalar_tensor_tensor(yt[:, t, :], bank[5][:, 0:D], is2[:, 0:1],
                                             X[:, bass.ds(b * TB + t, 1), :].rearrange("p o d -> p (o d)"),
                                             ALU.mult, ALU.add).then_inc(f_out, 1)
                assert steps[0] == FF_STEPS, steps[0]
                while steps[0] < FF_STEPS:
                    steps[0] += 1
                    dve.engine_nop().then_inc(dve_step, 1)

        @block.gpsimd
        def _(pool):
            pool.sem_inc(u_ready, 1)
            pool.sem_inc(en_ready, 1)
            pool.sem_inc(en2_ready, 1)
            pool.wait_ge(ld_kv, 16 * 3)
            for b in range(B):
                k4 = kv[:, b * TB:(b + 1) * TB, :]
                d4 = kvr[:, b * TB:(b + 1) * TB, 0, :]
                t4 = kvt[:, b * TB:(b + 1) * TB, :]
                H2 = CD // 2
                pool.tensor_tensor(d4, k4, cosd[:, :, :], ALU.mult).then_inc(pool_step, 1)
                pool.tensor_tensor(t4[:, :, 0:H2], k4[:, :, H2:CD], sind[:, :, 0:H2], ALU.mult,
                                   ).then_inc(pool_step, 1)
                pool.tensor_tensor(t4[:, :, H2:CD], k4[:, :, 0:H2], sind[:, :, H2:CD], ALU.mult,
                                   ).then_inc(pool_step, 1)
                pool.wait_ge(pool_step, 5 * b + 3)
                pool.tensor_tensor(d4[:, :, 0:H2], d4[:, :, 0:H2], t4[:, :, 0:H2], ALU.subtract,
                                   ).then_inc(pool_step, 1)
                pool.tensor_tensor(d4[:, :, H2:CD], d4[:, :, H2:CD], t4[:, :, H2:CD], ALU.add,
                                   ).then_inc(pool_step, 1)
            pool.wait_ge(pool_step, 5 * B)
            pool.tensor_copy(kvr[:, :, 1, :], kvr[:, :, 0, :]).then_inc(kvr_ready, 1)

            pool.wait_ge(consts_ready, 1)

            def root(count, veps_sem, rstd_sem, src=None, dst=None):
                pool.wait_ge(veps_sem, count)
                src = veps[:, :] if src is None else src
                dst = rstd[:, :] if dst is None else dst
                pool.tensor_tensor(dst, src, half[:, 0:src.shape[1]], ALU.pow).then_inc(rstd_sem, 1)

            with pool.Fori(0, B) as b:
                root(b * 2 + 1, veps_ready, rstd_ready)
                for l in range(2):
                    r = b * 2 + l
                    held = pool.to_reg(r * 4 + 4)
                    pool.wait_ge(consts_ready, 1)
                    pool.wait_ge(nb_evac, held)
                    held = pool.to_reg(r * 2 + 2)
                    pool.wait_ge(consts_ready, 1)
                    pool.wait_ge(self_evac, held)
                    for h in range(GH + 1):
                        if h < GH:
                            held = pool.to_reg(r * 16 + 2 * max(h - 1, 0) + 1)
                            pool.wait_ge(consts_ready, 1)
                            pool.wait_ge(leak_done, held)
                            for t in range(TB):
                                pool.tensor_scalar(U[:, h % 2, t, :], NB[:, h, :], 0.2, self02[:, t, h:h + 1],
                                                   ALU.mult, ALU.add).then_inc(u_ready, 1)
                        if h >= 1:
                            g = h - 1
                            held = pool.to_reg(r * 8 + (g + 1) + 1)
                            pool.wait_ge(consts_ready, 1)
                            pool.wait_ge(rinv_ready, held)
                            for t in range(TB):
                                pool.tensor_scalar(Ex[:, g % 2, t, :], Ex[:, g % 2, t, :], Ri[:, g % 2, t:t + 1], 1.0,
                                                   ALU.mult, ALU.mult).then_inc(en_ready, 1)
                root(b * 2 + 2, veps_ready, rstd_ready)

            pool.wait_ge(idx_ready, 1)
            pool.wait_ge(st_eout, 16 * E + 16)
            pool.wait_ge(st_z, 16)
            for t in range(NT):
                for k in range(TOPK):
                    pool.indirect_dma_start(out=gath[:, t * TOPK + k, :], out_offset=None, in_=eout[:, :],
                                            in_offset=bass.IndirectOffsetOnAxis(ap=idx[:, t, k:k + 1], axis=0),
                                            ).then_inc(g_ld[t], 16)

            with pool.Fori(0, B) as b:
                root(b + 1, l2_veps, l2_rstd)
                for j in range(AH // 2):
                    held = pool.to_reg(b * 8 + (j + 1) + 1)
                    pool.wait_ge(consts_ready, 1)
                    pool.wait_ge(ri2_ready, held)
                    for t in range(TB):
                        for h in range(2):
                            pool.tensor_scalar(E2[:, j % 2, t, h, :], E2[:, j % 2, t, h, :],
                                               R2[:, j % 2, t, h:h + 1], 1.0, ALU.mult,
                                               ALU.mult).then_inc(en2_ready, 1)
            with pool.Fori(0, B) as b:
                root(b + 1, f_veps, f_rstd)
                for t in range(TB):
                    root(b * TB + (t + 1), f_ms, f_rms, msq[:, :], rms[:, :])


def _layouts(inp):
    f = lambda n: np.asarray(inp[n])
    rows = lambda n: f(n).reshape(T, -1)
    pos = np.arange(S, dtype=np.float32)
    inv = (np.float32(1.0) / np.float32(10000.0) ** (np.arange(0, CD, 2, dtype=np.float32) / np.float32(CD)))
    freqs = pos[:, None] * inv.astype(np.float32)[None, :]
    block = np.zeros((2 * P, GH), np.float32)
    for h in range(GH):
        block[h * GO:(h + 1) * GO, h] = -1.0
    return {
        "x": rows("x"),
        "ctx": rows("ctx_512"),
        "ctxT": rows("ctx_512").T,
        "w0": f("L0_xattn_W0").transpose(1, 0, 2).reshape(CD, D),
        "w0T": f("L0_xattn_W0").transpose(0, 2, 1).reshape(D, CD),
        "w1": f("L0_xattn_W1").transpose(1, 0, 2).reshape(D, D),
        "w1T": f("L0_xattn_W1").transpose(0, 2, 1).reshape(D, D),
        "cols": np.stack([f(f"L0_xattn_{n}{l}").reshape(KT, P) for l in range(2) for n in ("a_self", "a_neigh", "b")],
                         ).reshape(-1, P).T,
        "gwT": f("L0_ffn_gate_w").T,
        "wg": f("L0_ffn_w_gate"), "wu": f("L0_ffn_w_up"), "wd": f("L0_ffn_w_down"),
        "swg": f("L0_ffn_sw_gate"), "swu": f("L0_ffn_sw_up"), "swd": f("L0_ffn_sw_down"),
        "wq": f("L1_xattn_Wq"),
        "kcqT": f("L1_xattn_w_kc_q").transpose(2, 0, 1).reshape(AQ, AH * AK),
        "kckv": f("L1_xattn_w_kc_kv").transpose(1, 0, 2).reshape(AK, AH * CD),
        "qrT": f("L1_xattn_W_qr").transpose(2, 0, 1).reshape(AR, AH * AQ),
        "krT": f("L1_xattn_W_kr").transpose(2, 0, 1).reshape(AR, AH * CD),
        "woT": f("L1_xattn_Wo").T,
        "w13T": f("L1_ffn_w13").T, "w2T": f("L1_ffn_w2").T, "nw": f("L1_ffn_norm_w"),
        "ident": np.eye(P, dtype=np.float32),
        "upper": np.triu(np.ones((P, P), np.float32), 1),
        "iota": np.tile(np.arange(CAP, dtype=np.float32), (P, 1)),
        "rowof": np.tile(ZROW - CAP * np.arange(E, dtype=np.float32), (P, 1)),
        "block": block,
        "cos": np.repeat(np.cos(freqs), 2, axis=-1).astype(np.float32),
        "sin": np.repeat(np.sin(freqs), 2, axis=-1).astype(np.float32),
    }


def kernel(**inputs):
    import concourse.bacc as _bacc
    from concourse.bass_utils import run_bass_kernel_spmd as _run

    nc = _bacc.Bacc("TRN2", target_bir_lowering=False, num_devices=1)
    arrays, a = {}, {}
    for name, x in _layouts(inputs).items():
        x = np.ascontiguousarray(x)
        arrays[f"in_{name}"] = x
        a[name] = nc.dram_tensor(f"in_{name}", x.shape, mybir.dt.from_np(x.dtype), kind="ExternalInput").ap()
    out = nc.dram_tensor("out_0", (T, D), F32, kind="ExternalOutput").ap()
    build(nc, a, out)
    r = _run(nc, [arrays], core_ids=[0])
    return r.results[0]["out_0"].reshape(B, S, D)
```

```python
from contextlib import ExitStack

import numpy as np

import concourse.bass as bass
from concourse import mybir

F32 = mybir.dt.float32
F16 = mybir.dt.float16
BF16 = mybir.dt.bfloat16
U32 = mybir.dt.uint32
ALU = mybir.AluOpType
ACT = mybir.ActivationFunctionType
AX_X = mybir.AxisListType.X

P = 128
B, S, D = 4, 256, 256
T = B * S
NT = T // P
TB = S // P
KT = D // P
CD = 64
GH, GO = 8, 32
E, TOPK, IE, CAP = 16, 4, 176, 128
IS = 352
AH, AK, AQ, AR = 16, 128, 192, 64
HID = 704
LN_EPS, RMS_EPS = 1e-5, 1e-5
MASK = 1e10
BIG = 3.0e38
ROUND = 1.5 * 2.0 ** 23
NO_SLOT = 200.0
ZROW = E * CAP


def build(nc, a, out):
    ctx = ExitStack()
    with ctx:
        def sb(name, shape, dt=F32):
            return ctx.enter_context(nc.sbuf_tensor(name, shape, dt))

        def sem(name):
            return ctx.enter_context(nc.semaphore(name))

        bank = [ctx.enter_context(nc.psum_tensor(f"bank{i}", [P, 512], F32)) for i in range(8)]

        X = sb("X", [P, NT, D])
        ident = sb("ident", [P, P])
        identh = sb("identh", [P, P], BF16)
        half = sb("half", [P, 2])
        xlnT = sb("xlnT", [P, KT, T])
        bnst = sb("bnst", [P, TB, 6])
        mv = sb("mv", [P, TB, 2])
        veps = sb("veps", [P, TB])
        rstd = sb("rstd", [P, TB])
        xln = sb("xln", [P, TB, D])
        Nw = sb("Nw", [P, KT, AH * CD])
        Pw = sb("Pw", [P, AH // 2, D])
        work = sb("work", [P, 19200])
        place = [0]

        def at(shape, rows=P, dt=F32):
            n = int(np.prod(shape)) * (1 if dt is F32 else 0.5)
            lo = place[0]
            place[0] += int(n)
            assert place[0] <= 19200, place[0]
            x = work[0:rows, lo:place[0]]
            x = x if dt is F32 else x.bitcast(dt)
            names = "abcd"[:len(shape)]
            return x.rearrange(f"p ({' '.join(names)}) -> p {' '.join(names)}", **dict(zip(names[1:], shape[1:])))

        ctxT = at([T], CD)
        ctxb = Nw[0:CD, 0, 0:2 * S].rearrange("p (b s) -> p b s", b=2)
        maskN = Nw[:, 1, :].rearrange("p (b t s) -> p b t s", b=2, t=TB)
        w0 = at([1, D], CD)
        w1 = at([KT, D])
        w0T = at([KT, CD])
        w1T = at([KT, D])
        cols = sb("cols", [P, 2, 3, KT])
        acol = cols[:, :, 0:2, :]
        bcol = cols[:, :, 2, :]
        blockmask = sb("blockmask", [P, KT, GH])
        abd = sb("abd", [P, 2, KT, 2 * GH])
        was = [sb("was0", [CD, 1, GH]), sb("was1", [P, KT, GH])]
        wan = [at([1, GH, P], CD), at([KT, GH, P])]
        featS = at([2, TB, D])
        selfS = sb("selfS", [P, 2, TB, GH])
        self02 = sb("self02", [P, 2, TB, GH])
        NB = at([2, GH, S])
        U = at([4, TB, S])
        L = at([2, TB, S])
        M = sb("M", [P, 2, TB])
        Ex = at([2, TB, S])
        Sm = sb("Sm", [P, 2, TB, GH])
        Ri = sb("Ri", [P, TB, GH])
        rX = at([TB, GH, GO])
        rT = at([KT, S])
        ETs = at([2, TB, S])
        y0 = at([KT, S])
        r0 = at([KT, S])
        hT = [at([KT, S]), at([KT, S])]
        place[0] = 0
        gwT = sb("gwT", [P, KT, E])
        Lp = sb("Lp", [P, NT, E + TOPK])
        top8 = sb("top8", [P, NT, 8])
        rep = sb("rep", [P, NT, E + TOPK])
        sel = sb("sel", [P, NT, E])
        selb = sb("selb", [P, NT, E], BF16)
        prob = sb("prob", [P, NT, E])
        wgt = sb("wgt", [P, NT, E])
        ssum = sb("ssum", [P, NT])
        srec = sb("srec", [P, NT])
        keep = sb("keep", [P, NT, E])
        slotf = sb("slotf", [P, NT, E])
        slotv = sb("slotv", [P, NT, E], F16)
        key = sb("key", [P, NT, E])
        rowof = sb("rowof", [P, E])
        keytop = sb("keytop", [P, NT, 8])
        idx = sb("idx", [P, NT, TOPK], U32)
        eq = sb("eq", [P, NT, TOPK, E])
        wk = sb("wk", [P, NT, TOPK])
        upper = sb("upper", [P, P], BF16)
        upperf = sb("upperf", [P, P])
        onesb = sb("onesb", [P, P], BF16)
        iotaf = sb("iotaf", [P, CAP])
        iotah = sb("iotah", [P, CAP], F16)
        xhi = sb("xhi", [P, NT, D], F16)
        xlo = sb("xlo", [P, NT, D], F16)
        arena = sb("arena", [P, 17408])
        gath = arena[:, 8192:16384].rearrange("p (j d) -> p j d", j=NT * TOPK)
        wq = arena[:, 0:4096].rearrange("p (h d) -> p h d", h=AH)
        wo = arena[:, 4096:8192].rearrange("p (h d) -> p h d", h=AH)
        kcqT = arena[0:96, 8192:12288].rearrange("p (t n) -> p t n", t=2)
        qrT = arena[0:AR, 12288:15360].rearrange("p (h q) -> p h q", h=AH)
        krT = arena[0:AR, 15360:16384].rearrange("p (h c) -> p h c", h=AH)
        kckv = arena[:, 16384:17408].rearrange("p (h c) -> p h c", h=AH)
        xgT = at([KT, E * CAP])
        kblk = xgT[:, 0, :].rearrange("p (b h s) -> p b h s", b=B, h=2)
        zrow = sb("zrow", [1, D])
        sgs = at([512])
        smid = at([3, 512])
        IH = IE // 2
        esg = sgs[0:IH, :].rearrange("p (f c) -> p f c", f=2)
        emid = smid[0:IH, 0, :].rearrange("p (f j c) -> p f j c", f=2, j=2)
        eoS = smid[:, 1, :].rearrange("p (f d) -> p f d", f=2)
        NW = 4
        wg = at([NW, KT, IE])
        wu = at([NW, KT, IE])
        wd = at([NW, 2, D], IH)
        swg = wg[:, 2:4, :, :].rearrange("p f k n -> p (f k n)").rearrange("p (k n) -> p k n", k=KT)
        swu = wu[:, 2:4, :, :].rearrange("p f k n -> p (f k n)").rearrange("p (k n) -> p k n", k=KT)
        swd = sb("swd", [P, 3, D])
        chs = xgT[0:96, 0, :]
        dhs = xgT[:, 1, 0:AH * CD]
        early = Pw[:, :, :].rearrange("p j d -> p (j d)")
        kv = early[:, 0:512].rearrange("p (t c) -> p t c", t=NT)
        kvt = early[:, 512:1024].rearrange("p (t c) -> p t c", t=NT)
        cosd = early[:, 1024:1152].rearrange("p (t c) -> p t c", t=TB)
        sind = early[:, 1152:1280].rearrange("p (t c) -> p t c", t=TB)
        kvr = sb("kvr", [P, NT, 2, CD])
        w13f = arena[:, 0:KT * 2 * HID].rearrange("p (k n) -> p k n", k=KT)
        w2f = arena[:, 2816:2816 + 6 * D].rearrange("p (k n) -> p k n", k=6)
        before = place[0]
        disp = at([NT, E, CAP], dt=F16)
        place[0] = before
        w13p = at([3, KT, 2 * HID], dt=BF16)
        w2p = at([3, 6, D], dt=BF16)
        nwb = arena[:, 4352:4352 + HID]
        spare = 4096 + 512 + 3 * 512
        qT = work[:, spare:spare + 2048].rearrange("p (j s) -> p j s", j=AH // 2)
        E2 = work[:, spare + 2048:spare + 4096].rearrange("p (f t h s) -> p f t h s", f=2, t=TB, h=2)
        ET2 = arena[:, 12288:14336].rearrange("p (f h t s) -> p f h t s", f=2, h=2, t=TB)
        cxT = arena[:, 14336:16384].rearrange("p (j s) -> p j s", j=AH // 2)
        xT3 = arena[:, 16384:16896].rearrange("p (k s) -> p k s", k=KT)
        kvb = sb("kvb", [P, TB, CD])
        nmx = sb("nmx", [P, 2, TB, 2])
        S2 = sb("S2", [P, 2, TB, 2])
        R2 = sb("R2", [P, 2, TB, 2])
        spot = [0]

        def piece(shape, dt=F32):
            n = int(np.prod(shape)) // (1 if dt is F32 else 2)
            lo = spot[0]
            spot[0] += n
            assert spot[0] <= 4352 or lo >= 4352 + HID and spot[0] <= 8192
            x = arena[:, lo:spot[0]]
            x = x if dt is F32 else x.bitcast(dt)
            names = "abcd"[:len(shape)]
            return x.rearrange(f"p ({' '.join(names)}) -> p {' '.join(names)}", **dict(zip(names[1:], shape[1:])))

        r1 = piece([HID])
        r2 = piece([HID])
        gated = piece([HID])
        tmp2 = piece([HID])
        tmp1 = piece([D])
        q1 = piece([2, D], BF16)
        q1T = piece([2, KT * P], BF16)
        q2T = piece([2, 6 * P], BF16)
        spot[0] = 4352 + HID
        q2 = piece([2, HID], BF16)
        yt = piece([2, D])
        is1 = sb("is1", [P, 2])
        is2 = sb("is2", [P, 2])
        amax = sb("amax", [P, 1])
        scl = sb("scl", [P, 1])
        ms = sb("ms", [P, 1])
        msq = sb("msq", [P, 1])
        rms = sb("rms", [P, 1])
        unround = sb("unround", [P, 1])

        eout = nc.dram_tensor("eout", (ZROW + 1, D), F32, kind="Internal").ap()

        ld_x = sem("ld_x")
        ld_ctxT = sem("ld_ctxT")
        ld_gat = sem("ld_gat")
        ld_const = sem("ld_const")
        ld_attn = sem("ld_attn")
        ld_ffn0 = sem("ld_ffn0")
        ld_w13 = sem("ld_w13")
        ld_kv = sem("ld_kv")
        st_out = [sem(f"st_out{g}") for g in range(2)]
        st_eout = [sem(f"st_eout{g}") for g in range(2)]
        st_z = sem("st_z")
        consts_ready = sem("consts_ready")
        abd_ready = sem("abd_ready")
        wa_mm = sem("wa_mm")
        wa_ready = sem("wa_ready")
        ctxb_ready = sem("ctxb_ready")
        prep_mm = sem("prep_mm")
        prep_act = sem("prep_act")
        prep_dve = sem("prep_dve")
        sums_ready = sem("sums_ready")
        sums_mm = sem("sums_mm")
        sums_evac = sem("sums_evac")
        agg_read = sem("agg_read")
        elu_ready = sem("elu_ready")
        elu_exp = sem("elu_exp")
        h_ready = sem("h_ready")
        veps_ready = sem("veps_ready")
        rstd_ready = sem("rstd_ready")
        u_ready = sem("u_ready")
        leak_done = sem("leak_done")
        e_ready = sem("e_ready")
        exp_done = sem("exp_done")
        et_mm = sem("et_mm")
        et_evac = sem("et_evac")
        agg_mm = sem("agg_mm")
        rows_mm = sem("rows_mm")
        x1_ready = sem("x1_ready")
        xln_ready = sem("xln_ready")
        lnT_mm = sem("lnT_mm")
        lnT_evac = sem("lnT_evac")
        split_ready = sem("split_ready")
        c_mm = sem("c_mm")
        c_evac = sem("c_evac")
        d_mm = sem("d_mm")
        d_evac = sem("d_evac")
        n_mm = sem("n_mm")
        n_evac = sem("n_evac")
        p_mm = sem("p_mm")
        p_evac = sem("p_evac")
        logit_mm = sem("logit_mm")
        route_exp_in = sem("route_exp_in")
        route_exp = sem("route_exp")
        sel_ready = sem("sel_ready")
        rank_mm = sem("rank_mm")
        disp_ready = sem("disp_ready")
        disp_mm = sem("disp_mm")
        disp_evac = sem("disp_evac")
        idx_ready = sem("idx_ready")
        shg_mm = sem("shg_mm")
        shs_ready = sem("shs_ready")
        shm_ready = sem("shm_ready")
        shd_mm = sem("shd_mm")
        shd_add = sem("shd_add")
        exg_mm = sem("exg_mm")
        exs_ready = sem("exs_ready")
        exm_ready = sem("exm_ready")
        exd_mm = sem("exd_mm")
        exo_ready = sem("exo_ready")
        kvr_ready = sem("kvr_ready")
        kvT_mm = sem("kvT_mm")
        kvT_ready = sem("kvT_ready")
        kvb_ready = sem("kvb_ready")
        l2_veps = sem("l2_veps")
        l2_rstd = sem("l2_rstd")
        l2_xln = sem("l2_xln")
        l2_T_mm = sem("l2_T_mm")
        l2_T_evac = sem("l2_T_evac")
        q_mm = sem("q_mm")
        q_evac = sem("q_evac")
        sc_mm = sem("sc_mm")
        mx_ready = sem("mx_ready")
        ex2_ready = sem("ex2_ready")
        ri2_ready = sem("ri2_ready")
        en2_ready = sem("en2_ready")
        et2_mm = sem("et2_mm")
        et2_act = sem("et2_act")
        et2_dve = sem("et2_dve")
        combined = sem("combined")
        cx_mm = sem("cx_mm")
        cx_evac = sem("cx_evac")
        o_mm = sem("o_mm")
        x3_ready = sem("x3_ready")
        wsplit_ready = sem("wsplit_ready")
        w13_part = sem("w13_part")
        f_veps = sem("f_veps")
        f_rstd = sem("f_rstd")
        f_q1 = sem("f_q1")
        f_q1T_mm = sem("f_q1T_mm")
        f_q1T = sem("f_q1T")
        f_a_mm = sem("f_a_mm")
        f_r_ready = sem("f_r_ready")
        f_g_ready = sem("f_g_ready")
        f_sq_ready = sem("f_sq_ready")
        f_ms = sem("f_ms")
        f_rms = sem("f_rms")
        f_t2 = sem("f_t2")
        f_q2 = sem("f_q2")
        f_q2T_mm = sem("f_q2T_mm")
        f_q2T = sem("f_q2T")
        f_o_mm = sem("f_o_mm")
        f_out = sem("f_out")
        act_step = sem("act_step")
        f_relu = sem("f_relu")
        dve_step = sem("dve_step")
        pool_step = sem("pool_step")
        zero_ready = sem("zero_ready")
        big_ready = sem("big_ready")
        ld_we = [sem(f"ld_we{i}") for i in range(NW)]
        g_ld = [sem(f"g_ld{i}") for i in range(8)]

        block = ctx.enter_context(nc.Block())

        @block.sync
        def _(sp):
            sp.sem_inc(st_out[0], 16)
            sp.sem_inc(st_out[1], 16)
            sp.sem_inc(st_eout[0], 16)
            sp.sem_inc(st_eout[1], 16)
            sp.dma_start(X[:, :, :], a["x"].rearrange("(t p) d -> p t d", p=P)).then_inc(ld_x, 16)
            sp.dma_start(ctxT[:, :], a["ctxT"]).then_inc(ld_ctxT, 16)
            sp.dma_start(w0T[:, :, :], a["w0T"].rearrange("(k p) n -> p k n", p=P)).then_inc(ld_gat, 16)
            sp.dma_start(w1T[:, :, :], a["w1T"].rearrange("(k p) n -> p k n", p=P)).then_inc(ld_gat, 16)
            sp.dma_start(cols[:, :, :, :], a["cols"].rearrange("p (l i k) -> p l i k", l=2, i=3)).then_inc(ld_gat, 16)
            sp.dma_start(blockmask[:, :, :], a["block"].rearrange("(k p) h -> p k h", p=P)).then_inc(ld_gat, 16)
            sp.dma_start(w0[:, 0, :], a["w0"]).then_inc(ld_gat, 16)
            sp.dma_start(w1[:, :, :], a["w1"].rearrange("(k p) n -> p k n", p=P)).then_inc(ld_gat, 16)
            sp.dma_start(ident[:, :], a["ident"]).then_inc(ld_const, 16)
            sp.dma_start(upperf[:, :], a["upper"]).then_inc(ld_const, 16)
            sp.dma_start(iotaf[:, :], a["iota"]).then_inc(ld_const, 16)
            sp.dma_start(rowof[:, :], a["rowof"]).then_inc(ld_const, 16)
            sp.dma_start(kv[:, :, :], a["ctx"].rearrange("(t p) c -> p t c", p=P)).then_inc(ld_kv, 16)
            sp.dma_start(cosd[:, :, :], a["cos"].rearrange("(t p) c -> p t c", p=P)).then_inc(ld_kv, 16)
            sp.dma_start(sind[:, :, :], a["sin"].rearrange("(t p) c -> p t c", p=P)).then_inc(ld_kv, 16)
            sp.dma_start(gwT[:, :, :], a["gwT"].rearrange("(k p) e -> p k e", p=P)).then_inc(ld_ffn0, 16)
            sp.dma_start(swd[:, 0:2, :], a["swd"][0:2 * P, :].rearrange("(k p) n -> p k n", p=P),
                         ).then_inc(ld_ffn0, 16)
            sp.dma_start(swd[0:IS - 2 * P, 2, :], a["swd"][2 * P:IS, :]).then_inc(ld_ffn0, 16)
            sp.dma_start(wq, a["wq"].rearrange("(h k) d -> k h d", k=P)).then_inc(ld_attn, 16)
            sp.dma_start(wo, a["woT"].rearrange("(h k) d -> k h d", k=P)).then_inc(ld_attn, 16)
            sp.dma_start(kcqT, a["kcqT"].rearrange("(t q) n -> q t n", q=96)).then_inc(ld_attn, 16)
            sp.dma_start(qrT, a["qrT"].rearrange("r (h q) -> r h q", h=AH)).then_inc(ld_attn, 16)
            sp.dma_start(krT, a["krT"].rearrange("r (h c) -> r h c", h=AH)).then_inc(ld_attn, 16)
            sp.dma_start(kckv, a["kckv"].rearrange("k (h c) -> k h c", h=AH)).then_inc(ld_attn, 16)

            def load_expert(e, f):
                gw, uw = (a[n][bass.ds(e, 1), :, :].rearrange("o (k p) n -> p (o k) n", p=P) for n in ("wg", "wu"))
                dw = a["wd"][bass.ds(e, 1), :, :].rearrange("o (j p) n -> p (o j) n", p=IH)
                sp.dma_start(wg[:, f, :, :], gw).then_inc(ld_we[f], 16)
                sp.dma_start(wu[:, f, :, :], uw).then_inc(ld_we[f], 16)
                sp.dma_start(wd[:, f, :, :], dw).then_inc(ld_we[f], 16)

            sp.wait_ge(rows_mm, B)
            sp.wait_ge(h_ready, 2 * B)
            sp.dma_start(swg[:, :, :], a["swg"].rearrange("(k p) n -> p k n", p=P)).then_inc(ld_ffn0, 16)
            sp.dma_start(swu[:, :, :], a["swu"].rearrange("(k p) n -> p k n", p=P)).then_inc(ld_ffn0, 16)
            for f in range(2):
                load_expert(f, f)
            sp.wait_ge(zero_ready, 1)
            sp.dma_start(eout[ZROW:ZROW + 1, :], zrow[:, :]).then_inc(st_z, 16)

            sp.wait_ge(n_evac, 4)
            sp.wait_ge(p_evac, 4)
            sp.dma_start(nwb[:, :], a["nw"].partition_broadcast(P)).then_inc(ld_w13, 16)
            sp.dma_start(w13f, a["w13T"].rearrange("(k p) n -> p k n", p=P)).then_inc(ld_w13, 16)
            sp.dma_start(w2f[:, 0:5, :], a["w2T"][0:5 * P, :].rearrange("(k p) n -> p k n", p=P),
                         ).then_inc(ld_w13, 16)
            sp.dma_start(w2f[0:HID - 5 * P, 5, :], a["w2T"][5 * P:HID, :]).then_inc(ld_w13, 16)
            sp.wait_ge(shd_mm, NT)
            for f in range(2, NW):
                load_expert(f, f)
            with sp.Fori(0, E // NW - 1) as i:
                for f in range(NW):
                    sp.wait_ge(exo_ready, i * NW + (f + 1) + 1)
                    sp.dma_start(eout[bass.ds(i * (NW * CAP) + f * CAP, CAP), :], eoS[:, f % 2, :],
                                 ).then_inc(st_eout[f % 2], 16)
                    load_expert(i * NW + (NW + f), f)
            for f in range(NW):
                sp.wait_ge(exo_ready, E - NW + f + 1 + 1)
                sp.dma_start(eout[(E - NW + f) * CAP:(E - NW + f + 1) * CAP, :], eoS[:, f % 2, :],
                             ).then_inc(st_eout[f % 2], 16)
            with sp.Fori(0, B) as b:
                for t in range(TB):
                    sp.wait_ge(f_out, b * TB + (t + 1) + 1)
                    sp.dma_start(out[bass.ds(b * S + t * P, P), :], yt[:, t, :]).then_inc(st_out[t], 16)
            sp.wait_ge(st_out[0], 16 * B + 16)
            sp.wait_ge(st_out[1], 16 * B + 16)
            sp.wait_ge(st_eout[0], 16 * (E // 2) + 16)
            sp.wait_ge(st_eout[1], 16 * (E // 2) + 16)
            sp.wait_ge(st_z, 16)

        @block.tensor
        def _(pe):
            pe.sem_inc(agg_mm, 1)
            pe.sem_inc(et_mm, 1)
            pe.sem_inc(q_mm, 1)
            pe.sem_inc(et2_mm, 1)
            pe.sem_inc(cx_mm, 1)
            pe.sem_inc(exd_mm, 1)
            pe.sem_inc(o_mm, 1)
            pe.sem_inc(f_q2T_mm, 1)
            pe.sem_inc(f_o_mm, 1)
            pe.sem_inc(prep_mm, 1)
            pe.wait_ge(ld_gat, 16 * 6)
            pe.wait_ge(abd_ready, 4)
            for k in range(KT):
                mm = pe.matmul(bank[0][0:CD, 0:16], w0T[:, k, :], abd[:, 0, k, :], start=k == 0, stop=k == 1)
            mm.then_inc(wa_mm, 1)
            for f in range(KT):
                for k in range(KT):
                    mm = pe.matmul(bank[1 + f][:, 0:16], w1T[:, k, f * P:(f + 1) * P], abd[:, 1, k, :],
                                   start=k == 0, stop=k == 1)
            mm.then_inc(wa_mm, 1)
            pe.wait_ge(wa_ready, 6)
            pe.wait_ge(ld_const, 16 * 4)
            def prep(p, k, j):
                l, bb = k // 2, k % 2
                nk = l + 1
                ft = [ctxb[:, bb, :]] if l == 0 else [hT[bb][:, 0, :], hT[bb][:, 1, :]]
                if j == 0:
                    if l == 0:
                        pe.wait_ge(ctxb_ready, p * 2 + (bb + 1))
                    else:
                        pe.wait_ge(h_ready, p * 4 + (k - 1))
                if j == 2:
                    pe.wait_ge(sums_evac, p * 4 + max(k - 1, 0) + 1)
                elif j == 3:
                    pe.wait_ge(lnT_evac, p * 2 + 1)
                elif j % 2 == 0:
                    pe.wait_ge(prep_dve, p * 12 + (k * 3 + j // 4) + 1)
                else:
                    pe.wait_ge(prep_act, p * 12 + (k * 3 + j // 4) + 1)
                bk = bank[j % 4]
                if j < 2:
                    for t in range(TB):
                        for i in range(nk):
                            rhs, c = ((was[l][:, i, :], GH), ((w1 if l else w0)[:, i, :], D))[j]
                            mm = pe.matmul(bk[:, t * c:(t + 1) * c], ft[i][:, t * P:(t + 1) * P], rhs,
                                           start=i == 0, stop=i == nk - 1)
                else:
                    for h in (2 * j - 4, 2 * j - 3):
                        for i in range(nk):
                            mm = pe.matmul(bk[:, (h % 2) * S:(h % 2 + 1) * S], wan[l][:, i, h, :], ft[i],
                                           start=i == 0, stop=i == nk - 1)
                mm.then_inc(prep_mm, 1)

            def head_transposes(p, i):
                n = p * 32 + i
                pe.wait_ge(exp_done, p * 64 + (2 * i + 2) + 1)
                pe.wait_ge(et_evac, p * 32 + max(i - 1, 0) + 1)
                for t in range(TB):
                    for m in range(TB):
                        c = m * S + t * P
                        mm = pe.transpose(bank[4 + i % 2][:, c:c + P], Ex[:, i % 2, t, m * P:(m + 1) * P], ident[:, :])
                mm.then_inc(et_mm, 1)

            def head_sum(p, i):
                k, h = i // GH, i % GH
                if h == 0:
                    pe.wait_ge(prep_act, p * 12 + (3 * k + 1) + 1)
                    pe.wait_ge(agg_read, p * 4 + max(k - 1, 0) + 1)
                pe.wait_ge(et_evac, p * 32 + (i + 1) + 1)
                j = h % 4
                for m in range(TB):
                    mm = pe.matmul(bank[6 + k % 2][32 * j:32 * j + 32, (h // 4) * S:(h // 4 + 1) * S],
                                   featS[:, k % 2, m, h * GO:(h + 1) * GO], ETs[:, i % 2, m, :],
                                   start=m == 0, stop=m == 1, tile_position=(0, 32 * j))
                mm.then_inc(agg_mm, 1)

            def spread_sums(p, k):
                pe.wait_ge(sums_ready, p * 4 + (k + 1))
                pe.wait_ge(sums_evac, p * 4 + k + 1)
                if k < 3:
                    pe.wait_ge(prep_dve, p * 12 + (3 * k + 5) + 1)
                for g in range(KT):
                    for t in range(TB):
                        c = g * S + t * P
                        mm = pe.transpose(bank[2][:, c:c + P],
                                          rX[:, t, 4 * g:4 * g + 4, :].rearrange("p h o -> p (h o)"), ident[:, :])
                mm.then_inc(sums_mm, 1)

            def to_rows(p, bb):
                pe.wait_ge(h_ready, p * 4 + (bb + 3))
                pe.wait_ge(lnT_evac, p * 2 + bb + 1)
                for t in range(TB):
                    for g in range(KT):
                        c = t * D + g * P
                        mm = pe.transpose(bank[3][:, c:c + P], hT[bb][:, g, t * P:(t + 1) * P], ident[:, :])
                mm.then_inc(rows_mm, 1)

            def ln_transposes(p, bb):
                pe.wait_ge(xln_ready, p * 2 + (bb + 1))
                for k in range(KT):
                    for t in range(TB):
                        c = k * S + t * P
                        mm = pe.transpose(bank[3][:, c:c + P], xln[:, t, k * P:(k + 1) * P], ident[:, :])
                mm.then_inc(lnT_mm, 1)

            with pe.Fori(0, B // 2) as p:
                for j in range(6):
                    prep(p, 0, j)
                for i in range(4 * GH + 1):
                    k, h = i // GH, i % GH
                    if i < 4 * GH:
                        head_transposes(p, i)
                    if i > 0:
                        head_sum(p, i - 1)
                        if h == 0:
                            spread_sums(p, k - 1)
                    if k < 3 and h >= 3:
                        if h == 3:
                            prep(p, k + 1, 0)
                        prep(p, k + 1, h - 2)
                    if k == 3 and h == 4:
                        to_rows(p, 0)
                    if i == 4 * GH:
                        ln_transposes(p, 0)
                to_rows(p, 1)
                ln_transposes(p, 1)

            pe.wait_ge(lnT_evac, B + 1)
            pe.wait_ge(ld_ffn0, 16 * 5)
            for t in range(NT):
                for k in range(KT):
                    mm = pe.matmul(bank[7][:, t * E:(t + 1) * E], xlnT[:, k, t * P:(t + 1) * P], gwT[:, k, :],
                                   start=k == 0, stop=k == 1)
            mm.then_inc(logit_mm, 1)

            pe.wait_ge(ld_attn, 16 * 6)
            for q in range(4):
                for h in range(4 * q, 4 * q + 4):
                    for t in range(2):
                        c = (h % 4 * 2 + t) * CD
                        mm = pe.matmul(bank[q][0:96, c:c + CD], qrT[:, h, t * 96:(t + 1) * 96], krT[:, h, :],
                                       start=True, stop=True)
                mm.then_inc(c_mm, 1)

            pe.wait_ge(sel_ready, 1)
            mm = pe.matmul(bank[6][:, 0:P], upper[:, :], selb[:, :, :].rearrange("p t e -> p (t e)"),
                           start=True, stop=True)
            for k in range(1, NT):
                mm = pe.matmul(bank[6][:, k * E:P], onesb[:, :], selb[:, 0:NT - k, :].rearrange("p t e -> p (t e)"),
                               start=False, stop=True, skip_group_check=True)
            mm.then_inc(rank_mm, 1)

            for q in range(2):
                pe.wait_ge(c_evac, 2 * q + 2)
                for h in range(8 * q, 8 * q + 8):
                    for t in range(2):
                        mm = pe.matmul(bank[4 + q][:, h % 8 * CD:(h % 8 + 1) * CD], kcqT[:, t, h * AK:(h + 1) * AK],
                                       chs[:, (h * 2 + t) * CD:(h * 2 + t + 1) * CD], start=t == 0, stop=t == 1)
                mm.then_inc(d_mm, 1)
            for q in range(4):
                pe.wait_ge(d_evac, q // 2 + 1)
                for h in range(4 * q, 4 * q + 4):
                    for t in range(2):
                        c = (h % 4 * 2 + t) * CD
                        mm = pe.matmul(bank[q][:, c:c + CD], wq[:, h, t * P:(t + 1) * P],
                                       dhs[:, h * CD:(h + 1) * CD], start=True, stop=True)
                mm.then_inc(n_mm, 1)
            for q in range(4):
                pe.wait_ge(d_evac, 2)
                pe.wait_ge(p_evac, max(q - 1, 0))
                for h in range(4 * q, 4 * q + 4):
                    mm = pe.matmul(bank[4 + q % 2][h % 2 * CD:(h % 2 + 1) * CD, h % 4 // 2 * D:(h % 4 // 2 + 1) * D],
                                   kckv[:, h, :], wo[:, h, :], start=True, stop=True,
                                   tile_position=(0, h % 2 * CD))
                mm.then_inc(p_mm, 1)
            n = 0
            for c in range(2):
                for i in range(3):
                    m = min(P, IS - i * P)
                    pe.wait_ge(shm_ready, max(n - 1, 0))
                    if n == 0:
                        pe.wait_ge(n_evac, 4)
                        pe.wait_ge(p_evac, 4)
                    for wt, bk in ((swg, 0), (swu, 2)):
                        for k in range(KT):
                            mm = pe.matmul(bank[bk + n % 2][0:m, :], wt[:, k, i * P:i * P + m],
                                           xlnT[:, k, c * 512:(c + 1) * 512], start=k == 0, stop=k == 1)
                    mm.then_inc(shg_mm, 1)
                    n += 1
                pe.wait_ge(shm_ready, n)
                for t in range(4):
                    pe.wait_ge(shd_add, max(c * 4 + t - 1, 0))
                    for i in range(3):
                        m = min(P, IS - i * P)
                        mm = pe.matmul(bank[4 + t % 2][:, 0:D], smid[0:m, i, t * P:(t + 1) * P], swd[0:m, i, :],
                                       start=i == 0, stop=i == 2)
                    mm.then_inc(shd_mm, 1)

            pe.wait_ge(disp_ready, NT)
            n = 0
            for g in range(4):
                for k in range(KT):
                    pe.wait_ge(disp_evac, max(n - 1, 0))
                    for t in range(NT):
                        for i, part in enumerate((xhi, xlo)):
                            mm = pe.matmul(bank[n % 2][:, :], part[:, t, k * P:(k + 1) * P],
                                           disp[:, t, 4 * g:4 * g + 4, :].rearrange("p e s -> p (e s)"),
                                           start=t == 0 and i == 0, stop=t == NT - 1 and i == 1)
                    mm.then_inc(disp_mm, 1)
                    n += 1
            pe.wait_ge(disp_evac, 8)

            with pe.Fori(0, E // NW) as i:
                for f in range(NW + 1):
                    if f < NW:
                        g = f % 2
                        pe.wait_ge(ld_we[f], i * 48 + 48)
                        pe.wait_ge(exm_ready, i * NW + max(f, 1))
                        for wt, bk in ((wg, 0), (wu, 2)):
                            for j in range(2):
                                for k in range(KT):
                                    mm = pe.matmul(bank[bk + g][0:IH, j * CAP:(j + 1) * CAP],
                                                   wt[:, f, k, j * IH:(j + 1) * IH],
                                                   xgT[:, k, bass.ds(i * (NW * CAP) + f * CAP, CAP)],
                                                   start=k == 0, stop=k == 1)
                        mm.then_inc(exg_mm, 1)
                    if f > 0:
                        g = (f - 1) % 2
                        pe.wait_ge(exm_ready, i * NW + f + 1)
                        pe.wait_ge(exo_ready, i * NW + max(f - 1, 1))
                        for j in range(2):
                            mm = pe.matmul(bank[4 + g][:, 0:D], emid[:, g, j, :], wd[:, f - 1, j, :],
                                           start=j == 0, stop=j == 1)
                        mm.then_inc(exd_mm, 1)

            pe.wait_ge(exo_ready, E + 1)
            pe.wait_ge(shd_add, NT)
            pe.wait_ge(kvr_ready, 1)
            for b in range(B):
                pe.wait_ge(kvT_ready, 2 * b)
                for t in range(TB):
                    mm = pe.transpose(bank[6][:, t * P:(t + 1) * P],
                                      kvr[:, b * TB + t, :, :].rearrange("p a c -> p (a c)"), ident[:, :])
                mm.then_inc(kvT_mm, 1)
            pe.wait_ge(kvT_ready, 2 * B)
            def att_ln_transposes(b):
                pe.wait_ge(l2_xln, b * 2 + 2)
                pe.wait_ge(q_evac, b * 8 + 1)
                for k in range(KT):
                    for t in range(TB):
                        c = k * S + t * P
                        mm = pe.transpose(bank[6][:, c:c + P], xln[:, t, k * P:(k + 1) * P], ident[:, :])
                mm.then_inc(l2_T_mm, 1)

            def att_queries(b, j, first=False):
                pe.wait_ge(l2_T_evac, b + 1)
                pe.wait_ge(q_evac, b * 8 + max(j, 1))
                if j % 2 == 1 and not first:
                    pe.wait_ge(x3_ready, b)
                for k in range(KT):
                    mm = pe.matmul(bank[6 + j % 2][:, 0:S], Nw[:, k, j * P:(j + 1) * P], xT3[:, k, :],
                                   start=k == 0, stop=k == 1)
                mm.then_inc(q_mm, 1)

            def att_back_transposes(b, j):
                pe.wait_ge(en2_ready, b * 32 + (4 * j + 4) + 1)
                for h in range(2):
                    if h == 0:
                        pe.wait_ge(et2_act, b * 8 + j + 1)
                    else:
                        pe.wait_ge(et2_dve, b * 8 + j + 1)
                    for t in range(TB):
                        for m in range(TB):
                            c = m * S + t * P
                            mm = pe.transpose(bank[2 + h][:, c:c + P], E2[:, j % 2, t, h, m * P:(m + 1) * P],
                                              ident[:, :])
                    mm.then_inc(et2_mm, 1)

            def att_scores(b, j, first=False):
                pe.wait_ge(q_evac, b * 8 + (j + 1) + 1)
                for t in range(TB):
                    if not first:
                        pe.wait_ge(ex2_ready, b * 32 + (4 * j + 2 * t - 1))
                    mm = pe.matmul(bank[t][:, :], qT[:, j, t * P:(t + 1) * P],
                                   kblk[:, bass.ds(b, 1), :, :].rearrange("p b h s -> p (b h s)"),
                                   start=True, stop=True)
                    mm.then_inc(sc_mm, 1)

            def att_context(b, j):
                pe.wait_ge(cx_evac, b * 8 + max(j, 1))
                pe.wait_ge(kvb_ready, b + 1)
                pe.wait_ge(et2_act, b * 8 + (j + 1) + 1)
                pe.wait_ge(et2_dve, b * 8 + (j + 1) + 1)
                for h in range(2):
                    for m in range(TB):
                        mm = pe.matmul(bank[4 + j % 2][h * CD:(h + 1) * CD, 0:S], kvb[:, m, :],
                                       ET2[:, j % 2, h, m, :], start=m == 0, stop=m == 1,
                                       tile_position=(0, h * CD))
                mm.then_inc(cx_mm, 1)

            def att_output(b, last=False):
                pe.wait_ge(cx_evac, b * 8 + 8 + 1)
                pe.wait_ge(q_evac, b * 8 + (8 if last else 16) + 1)
                for t in range(TB):
                    for j in range(AH // 2):
                        mm = pe.matmul(bank[7][:, t * D:(t + 1) * D], cxT[:, j, t * P:(t + 1) * P], Pw[:, j, :],
                                       start=j == 0, stop=j == AH // 2 - 1)
                mm.then_inc(o_mm, 1)

            att_ln_transposes(0)
            for j in range(AH // 2):
                att_queries(0, j, first=True)
            att_scores(0, 0, first=True)
            att_scores(0, 1)
            with pe.Fori(0, B - 1) as b:
                for j in range(2, AH // 2):
                    att_back_transposes(b, j - 2)
                    att_scores(b, j)
                    att_context(b, j - 2)
                    if j == 3:
                        att_ln_transposes(b + 1)
                    if j >= 4:
                        att_queries(b + 1, 2 * j - 8)
                        att_queries(b + 1, 2 * j - 7)
                for j in range(2):
                    att_back_transposes(b, j + 6)
                    att_scores(b + 1, j)
                    att_context(b, j + 6)
                att_output(b)
            for j in range(2, AH // 2 + 2):
                att_back_transposes(B - 1, j - 2)
                if j < AH // 2:
                    att_scores(B - 1, j)
                att_context(B - 1, j - 2)
            att_output(B - 1, last=True)
            pe.wait_ge(x3_ready, B + 1)

            pe.wait_ge(wsplit_ready, 1)
            pe.wait_ge(w13_part, 3)
            trs = bank[6][:, :].bitcast(BF16)

            def ff_in_transposes(n, g, first=False):
                pe.wait_ge(f_q1, n + 1)
                if not first:
                    pe.wait_ge(f_q1T, n)
                    pe.wait_ge(f_q2T, n - 1)
                for k in range(KT):
                    mm = pe.transpose(trs[:, k * P:(k + 1) * P], q1[:, g, k * P:(k + 1) * P], identh[:, :])
                mm.then_inc(f_q1T_mm, 1)

            def ff_in(n, g):
                pe.wait_ge(f_q1T, n + 1)
                pe.wait_ge(f_g_ready, max(n, 1) if isinstance(n, int) else n)
                for u in range(2):
                    for lo, w, bk, c in ((0, 512, u, 0), (512, HID - 512, 2, u * (HID - 512))):
                        i = 0
                        for part in range(3):
                            for k in range(KT):
                                mm = pe.matmul(bank[3 * g + bk][:, c:c + w], q1T[:, g, k * P:(k + 1) * P],
                                               w13p[:, part, k, u * HID + lo:u * HID + lo + w],
                                               start=i == 0, stop=i == 5)
                                i += 1
                mm.then_inc(f_a_mm, 1)

            def ff_back_transposes(n, g):
                pe.wait_ge(f_q2, n + 1 + 1)
                pe.wait_ge(f_q1T, min(n + 3, NT) if isinstance(n, int) else n + 3)
                for k in range(6):
                    m = min(P, HID - k * P)
                    mm = pe.transpose(trs[0:m, k * P:(k + 1) * P], q2[:, g, k * P:k * P + m], identh[:, :])
                mm.then_inc(f_q2T_mm, 1)

            def ff_out(n, g):
                pe.wait_ge(f_q2T, n + 1 + 1)
                pe.wait_ge(f_out, n + 1)
                for k in range(6):
                    m = min(P, HID - k * P)
                    for part in range(3):
                        mm = pe.matmul(bank[7][:, 0:D], q2T[0:m, g, k * P:(k + 1) * P], w2p[0:m, part, k, :],
                                       start=k == 0 and part == 0, stop=k == 5 and part == 2)
                mm.then_inc(f_o_mm, 1)

            ff_in_transposes(0, 0, first=True)
            pe.wait_ge(f_q1T, 1)
            ff_in_transposes(1, 1, first=True)
            ff_in(0, 0)
            ff_in(1, 1)
            ff_in_transposes(2, 0)
            ff_back_transposes(0, 0)
            ff_in(2, 0)
            ff_in_transposes(3, 1)
            ff_out(0, 0)
            with pe.Fori(1, B - 1) as b:
                for t in range(TB):
                    n = b * TB + t
                    ff_back_transposes(b * TB + (t - 1), 1 - t)
                    ff_in(b * TB + (t + 1), 1 - t)
                    ff_in_transposes(b * TB + (t + 2), t)
                    ff_out(b * TB + (t - 1), 1 - t)
            ff_back_transposes(NT - 3, 1)
            ff_in(NT - 1, 1)
            ff_out(NT - 3, 1)
            ff_back_transposes(NT - 2, 0)
            ff_out(NT - 2, 0)
            ff_back_transposes(NT - 1, 1)
            ff_out(NT - 1, 1)

        @block.scalar
        def _(act):
            act.sem_inc(prep_act, 1)
            act.sem_inc(sums_evac, 1)
            act.sem_inc(elu_exp, 1)
            act.sem_inc(et_evac, 1)
            act.sem_inc(lnT_evac, 1)
            act.sem_inc(exo_ready, 1)
            act.sem_inc(q_evac, 1)
            act.sem_inc(ex2_ready, 1)
            act.sem_inc(et2_act, 1)
            act.sem_inc(exp_done, 1)
            act.sem_inc(f_q2, 1)
            act.sem_inc(f_q2T, 1)
            def prep_copy(p, k, j):
                act.wait_ge(prep_mm, p * 24 + (6 * k + j + 1) + 1)
                if j == 1:
                    act.wait_ge(agg_mm, p * 32 + max(8 * (k - 1), 0) + 1)
                    dst = featS[:, k % 2, :, :].rearrange("p t d -> p (t d)")
                else:
                    act.wait_ge(leak_done, p * 64 + max(16 * (k - 1), 0) + 1)
                    dst = NB[:, k % 2, 2 * j - 4:2 * j - 2, :].rearrange("p h s -> p (h s)")
                act.activation(dst, bank[j % 4][:, :], ACT.Copy).then_inc(prep_act, 1)

            with act.Fori(0, B // 2) as p:
                act.wait_ge(ld_ctxT, 16)
                act.wait_ge(prep_mm, p * 24 + 1)
                for bb in range(2):
                    act.activation(ctxb[:, bb, :], ctxT[:, bass.ds(p * (2 * S) + bb * S, S)],
                                   ACT.Copy).then_inc(ctxb_ready, 1)
                for j in (1, 3):
                    prep_copy(p, 0, j)
                for i in range(4 * GH + 1):
                    k, h = i // GH, i % GH
                    if i < 4 * GH:
                        act.wait_ge(et_mm, p * 32 + max(i - 1, 0) + 1)
                        for t in range(TB):
                            act.wait_ge(e_ready, p * 64 + (2 * i + t + 1))
                            act.activation(Ex[:, i % 2, t, :], L[:, i % 2, t, :], ACT.Exp,
                                           bias=M[:, i % 2, t:t + 1], scale=-1.0,
                                           accum_out=Sm[:, k % 2, t, h:h + 1]).then_inc(exp_done, 1)
                    if i > 0:
                        act.wait_ge(et_mm, p * 32 + i + 1)
                        act.wait_ge(agg_mm, p * 32 + max(i - 2, 0) + 1)
                        act.activation(ETs[:, (i - 1) % 2, :, :].rearrange("p t s -> p (t s)"),
                                       bank[4 + (i - 1) % 2][:, :], ACT.Copy).then_inc(et_evac, 1)
                    if h == 0 and i > 0:
                        act.wait_ge(sums_mm, p * 4 + k)
                        act.wait_ge(agg_read, p * 4 + (k - 1) + 1)
                        act.activation(rT[:, :, :].rearrange("p g s -> p (g s)"), bank[2][:, :],
                                       ACT.Copy).then_inc(sums_evac, 1)
                    if (h == 2 and i > 2) or i == 4 * GH:
                        n = k - 1
                        act.wait_ge(elu_ready, p * 4 + (n + 1))
                        act.activation(y0[:, :, :], y0[:, :, :], ACT.Exp).then_inc(elu_exp, 1)
                    if k < 4 and h == 1:
                        prep_copy(p, k, 5)
                    if k < 3 and h in (5, 7):
                        prep_copy(p, k + 1, h - 4)
                    if i == 4 * GH:
                        act.wait_ge(lnT_mm, p * 2 + 1)
                        act.activation(xlnT[:, :, bass.ds(p * (2 * S), S)],
                                       bank[3][:, :].rearrange("p (k s) -> p k s", k=KT),
                                       ACT.Copy).then_inc(lnT_evac, 1)
                act.wait_ge(lnT_mm, p * 2 + 2)
                act.activation(xlnT[:, :, bass.ds(p * (2 * S) + S, S)],
                               bank[3][:, :].rearrange("p (k s) -> p k s", k=KT), ACT.Copy).then_inc(lnT_evac, 1)

            act.wait_ge(route_exp_in, 1)
            act.activation(prob[:, :, :], prob[:, :, :], ACT.Exp).then_inc(route_exp, 1)

            for q in range(4):
                act.wait_ge(c_mm, q + 1)
                act.activation(chs[:, q * 512:(q + 1) * 512], bank[q][0:96, :], ACT.Copy).then_inc(c_evac, 1)
            for q in range(2):
                act.wait_ge(d_mm, q + 1)
                act.activation(dhs[:, q * 512:(q + 1) * 512], bank[4 + q][:, :], ACT.Copy).then_inc(d_evac, 1)
            for q in range(4):
                act.wait_ge(n_mm, q + 1)
                src = bank[q][:, :].rearrange("p (h t c) -> p h t c", h=4, t=2)
                dst = Nw[:, :, q * 4 * CD:(q + 1) * 4 * CD].rearrange("p t (h c) -> p t h c", h=4)
                for t in range(2):
                    ins = act.activation(dst[:, t, :, :], src[:, :, t, :], ACT.Copy)
                    if t == 0:
                        ins.then_inc(act_step, 1)
                ins.then_inc(n_evac, 1)
            for q in range(4):
                act.wait_ge(p_mm, q + 1)
                act.activation(Pw[:, 2 * q:2 * q + 2, :].rearrange("p j d -> p (j d)"), bank[4 + q % 2][:, :],
                               ACT.Copy).then_inc(p_evac, 1)
            n = 0
            for c in range(2):
                for i in range(3):
                    m = min(P, IS - i * P)
                    act.wait_ge(shg_mm, n + 1)
                    act.wait_ge(shm_ready, n)
                    act.activation(sgs[0:m, :], bank[n % 2][0:m, :], ACT.Silu).then_inc(shs_ready, 1)
                    n += 1

            for n in range(0, 8, 2):
                act.wait_ge(disp_mm, n + 1)
                act.activation(xgT[:, 0, n // 2 * 512:(n // 2 + 1) * 512], bank[n % 2][:, :],
                               ACT.Copy).then_inc(disp_evac, 1)
                act.wait_ge(disp_mm, n + 2)
                act.activation(xgT[:, 1, n // 2 * 512:(n // 2 + 1) * 512], bank[1][:, :],
                               ACT.Copy).then_inc(disp_evac, 1)
            with act.Fori(0, E // NW) as i:
                for f in range(NW + 1):
                    if f < NW:
                        act.wait_ge(exg_mm, i * NW + (f + 1))
                        act.wait_ge(exm_ready, i * NW + max(f, 1))
                        act.activation(esg[:, f % 2, :], bank[f % 2][0:IH, 0:2 * CAP],
                                       ACT.Silu).then_inc(exs_ready, 1)
                    if f > 0:
                        act.wait_ge(exd_mm, i * NW + f + 1)
                        act.wait_ge(st_eout[(f - 1) % 2], i * (NW * 8) + (f - 1) // 2 * 16 + 16)
                        act.activation(eoS[:, (f - 1) % 2, :], bank[4 + (f - 1) % 2][:, 0:D],
                                       ACT.Copy).then_inc(exo_ready, 1)

            act.wait_ge(zero_ready, 2)
            for b in range(B):
                act.wait_ge(kvT_mm, b + 1)
                for h in range(2):
                    act.activation(kblk[h * CD:(h + 1) * CD, b, h, :], bank[6][h * CD:(h + 1) * CD, 0:S],
                                   ACT.Copy).then_inc(kvT_ready, 1)

            def att_ln_evac(b):
                act.wait_ge(l2_T_mm, b + 1)
                act.wait_ge(q_mm, b * 8 + 1)
                act.activation(xT3[:, :, :].rearrange("p k s -> p (k s)"), bank[6][:, :],
                               ACT.Copy).then_inc(l2_T_evac, 1)

            def att_query_evac(b, j, first=False):
                act.wait_ge(q_mm, b * 8 + (j + 1) + 1)
                if not first:
                    act.wait_ge(sc_mm, b * 16 + (2 * j + 2 - 16))
                act.activation(qT[:, j, :], bank[6 + j % 2][:, 0:S], ACT.Copy).then_inc(q_evac, 1)

            def att_back_evac(b, j):
                act.wait_ge(et2_mm, b * 16 + (2 * j + 1) + 1)
                act.wait_ge(cx_mm, b * 8 + max(j, 1))
                act.activation(ET2[:, j % 2, 0, :, :].rearrange("p t s -> p (t s)"), bank[2][:, :],
                               ACT.Copy).then_inc(et2_act, 1)

            def att_exp(b, j, first=False):
                if not first:
                    act.wait_ge(et2_mm, b * 16 + (2 * j - 2) + 1)
                    act.wait_ge(ri2_ready, b * 8 + j)
                for t in range(TB):
                    act.wait_ge(mx_ready, b * 16 + (2 * j + t + 1))
                    for h in range(2):
                        act.activation(E2[:, j % 2, t, h, :], bank[t][:, h * S:(h + 1) * S], ACT.Exp,
                                       bias=nmx[:, j % 2, t, h:h + 1],
                                       accum_out=S2[:, j % 2, t, h:h + 1]).then_inc(ex2_ready, 1)

            att_ln_evac(0)
            for j in range(AH // 2):
                att_query_evac(0, j, first=True)
            att_exp(0, 0, first=True)
            att_exp(0, 1, first=True)
            act.wait_ge(combined, 1)
            with act.Fori(0, B - 1) as b:
                for j in range(2, AH // 2):
                    att_back_evac(b, j - 2)
                    att_exp(b, j)
                    if j == 3:
                        att_ln_evac(b + 1)
                    if j >= 4:
                        att_query_evac(b + 1, 2 * j - 8)
                        att_query_evac(b + 1, 2 * j - 7)
                for j in range(2):
                    att_back_evac(b, j + 6)
                    att_exp(b + 1, j)
            for j in range(2, AH // 2 + 2):
                att_back_evac(B - 1, j - 2)
                if j < AH // 2:
                    att_exp(B - 1, j)

            trs = bank[6][:, :].bitcast(BF16)

            def ff_in_evac(n, g, first=False):
                act.wait_ge(f_q1T_mm, n + 1)
                if not first:
                    act.wait_ge(f_a_mm, n - 1)
                act.activation(q1T[:, g, :], trs[:, 0:KT * P], ACT.Copy).then_inc(f_q1T, 1)

            def ff_relu(n, g, first=False):
                if not first:
                    act.wait_ge(f_sq_ready, n)
                act.wait_ge(f_a_mm, n + 1)
                act.wait_ge(f_g_ready, n + 1)
                for lo, w, bk in ((0, 512, 0), (512, HID - 512, 2)):
                    act.activation(r1[:, lo:lo + w], bank[3 * g + bk][:, 0:w], ACT.Relu,
                                   scale=is1[:, g:g + 1]).then_inc(f_relu, 1)
                act.wait_ge(f_relu, n * 2 + 2)
                act.activation(r2[:, :], r1[:, :], ACT.Square).then_inc(f_r_ready, 1)

            def ff_square(n):
                act.wait_ge(f_g_ready, n + 1 + 1)
                act.activation(r1[:, :], gated[:, :], ACT.Square, accum_out=ms[:, :]).then_inc(f_sq_ready, 1)

            def ff_integers(n, g):
                act.wait_ge(f_t2, n + 1)
                act.activation(q2[:, g, :], tmp2[:, :], ACT.Identity, bias=unround[:, :]).then_inc(f_q2, 1)

            def ff_back_evac(n, g):
                act.wait_ge(f_q2T_mm, n + 1 + 1)
                act.activation(q2T[:, g, 0:5 * P], trs[:, 0:5 * P], ACT.Copy).then_inc(act_step, 1)
                act.activation(q2T[0:HID - 5 * P, g, 5 * P:6 * P], trs[0:HID - 5 * P, 5 * P:6 * P],
                               ACT.Copy).then_inc(f_q2T, 1)

            ff_in_evac(0, 0, first=True)
            ff_in_evac(1, 1, first=True)
            ff_relu(0, 0, first=True)
            ff_square(0)
            ff_relu(1, 1)
            ff_in_evac(2, 0)
            ff_integers(0, 0)
            ff_back_evac(0, 0)
            ff_square(1)
            ff_relu(2, 0)
            ff_in_evac(3, 1)
            ff_integers(1, 1)
            with act.Fori(1, B - 1) as b:
                for t in range(TB):
                    n = b * TB + t
                    ff_back_evac(b * TB + (t - 1), 1 - t)
                    ff_square(n)
                    ff_relu(b * TB + (t + 1), 1 - t)
                    ff_in_evac(b * TB + (t + 2), t)
                    ff_integers(n, t)
            ff_back_evac(NT - 3, 1)
            ff_square(NT - 2)
            ff_relu(NT - 1, 1)
            ff_integers(NT - 2, 0)
            ff_back_evac(NT - 2, 0)
            ff_square(NT - 1)
            ff_integers(NT - 1, 1)
            ff_back_evac(NT - 1, 1)

        @block.vector
        def _(dve):
            dve.sem_inc(prep_dve, 1)
            dve.sem_inc(agg_read, 1)
            dve.sem_inc(x1_ready, 1)
            dve.sem_inc(x3_ready, 1)
            dve.sem_inc(et2_dve, 1)
            dve.sem_inc(exm_ready, 1)
            dve.sem_inc(cx_evac, 1)
            dve.sem_inc(f_g_ready, 1)
            dve.sem_inc(f_out, 1)
            dve.sem_inc(leak_done, 1)
            dve.sem_inc(ri2_ready, 1)
            steps = [0]

            def link(ins, base=0, alone=False):
                steps[0] += 1
                ins.then_inc(dve_step, 1)
                count = base + steps[0]
                if alone:
                    count = dve.to_reg(count)
                    dve.wait_ge(consts_ready, 1)
                dve.wait_ge(dve_step, count)

            def row(b, t):
                return X[:, bass.ds(b * TB + t, 1), :].rearrange("p o d -> p (o d)")

            def layernorm_stats(b, base, veps_sem):
                for t in range(TB):
                    link(dve.bn_stats(bnst[:, t, :], row(b, t)), base, True)
                link(dve.bn_aggr(mv[:, 0, :], bnst[:, 0, :]), base, True)
                link(dve.bn_aggr(mv[:, 1, :], bnst[:, 1, :]), base)
                dve.tensor_scalar(veps[:, :], mv[:, :, 1], LN_EPS, None, ALU.add).then_inc(veps_sem, 1)

            def layernorm_apply(b, base, rstd_sem, count, dst):
                dve.wait_ge(rstd_sem, count)
                for t in range(TB):
                    link(dve.tensor_scalar(dst[:, t, :], row(b, t), mv[:, t, 0:1], rstd[:, t:t + 1],
                                           ALU.subtract, ALU.mult), base)

            def layernorm(b, base, veps_sem, rstd_sem, count, dst):
                layernorm_stats(b, base, veps_sem)
                layernorm_apply(b, base, rstd_sem, count, dst)

            dve.memset(unround[:, :], -ROUND).then_inc(big_ready, 1)
            dve.memset(half[:, :], -0.5).then_inc(consts_ready, 1)
            dve.memset(zrow[:, :], 0.0).then_inc(zero_ready, 1)
            dve.memset(onesb[:, :], 1.0).then_inc(big_ready, 1)
            dve.memset(Lp[:, :, E:E + TOPK], BIG).then_inc(big_ready, 1)
            dve.wait_ge(ld_gat, 16 * 6)
            for l in range(2):
                for i in range(2):
                    dve.tensor_tensor(abd[:, l, :, i * GH:(i + 1) * GH], blockmask[:, :, :],
                                      acol[:, l, i, :].unsqueeze(2).to_broadcast([P, KT, GH]),
                                      ALU.mult).then_inc(abd_ready, 1)
            dve.wait_ge(ld_const, 16 * 4)
            dve.tensor_copy(identh[:, :], ident[:, :]).then_inc(big_ready, 1)
            dve.tensor_copy(upper[:, :], upperf[:, :]).then_inc(big_ready, 1)
            dve.tensor_copy(iotah[:, :], iotaf[:, :]).then_inc(big_ready, 1)
            dve.wait_ge(wa_mm, 1)
            dve.tensor_copy(was[0][:, 0, :], bank[0][0:CD, 0:GH]).then_inc(wa_ready, 1)
            dve.tensor_copy(wan[0][:, 0, :, :], bank[0][0:CD, GH:2 * GH].unsqueeze(2).to_broadcast([CD, GH, P]),
                            ).then_inc(wa_ready, 1)
            dve.wait_ge(wa_mm, 2)
            for f in range(KT):
                dve.tensor_copy(was[1][:, f, :], bank[1 + f][:, 0:GH]).then_inc(wa_ready, 1)
                dve.tensor_copy(wan[1][:, f, :, :], bank[1 + f][:, GH:2 * GH].unsqueeze(2).to_broadcast([P, GH, P]),
                                ).then_inc(wa_ready, 1)

            dve.wait_ge(ld_x, 16)
            GAT_STEPS = 48

            def prep_copy(p, k, j):
                dve.wait_ge(prep_mm, p * 24 + (6 * k + j + 1) + 1)
                if j == 0:
                    selfp = bank[0][:, 0:TB * GH].rearrange("p (t h) -> p t h", t=TB)
                    link(dve.tensor_copy(selfS[:, k % 2, :, :], selfp), p * GAT_STEPS)
                    dve.tensor_scalar(self02[:, k % 2, :, :], selfp, 0.2, None, ALU.mult).then_inc(prep_dve, 1)
                else:
                    dve.tensor_copy(NB[:, k % 2, 2 * j - 4:2 * j - 2, :].rearrange("p h s -> p (h s)"),
                                    bank[j % 4][:, :]).then_inc(prep_dve, 1)

            def elu_first(p, k):
                base = p * GAT_STEPS
                l = k // 2
                dve.wait_ge(sums_evac, p * 4 + (k + 1) + 1)
                dve.wait_ge(agg_mm, p * 32 + (8 * k + 8) + 1)
                dve.wait_ge(elu_exp, p * 4 + k + 1)
                dve.tensor_tensor(y0[:, :, :].rearrange("p g s -> p (g s)"), bank[6 + k % 2][:, :],
                                  rT[:, :, :].rearrange("p g s -> p (g s)"), ALU.mult).then_inc(agg_read, 1)
                dve.wait_ge(agg_read, p * 4 + (k + 1) + 1)
                for g in range(KT):
                    link(dve.tensor_scalar(r0[:, g, :], y0[:, g, :], bcol[:, l, g:g + 1], 0.0, ALU.add, ALU.max), base)
                link(dve.tensor_scalar(y0[:, 0, :], y0[:, 0, :], bcol[:, l, 0:1], 0.0, ALU.add, ALU.min), base)
                dve.tensor_scalar(y0[:, 1, :], y0[:, 1, :], bcol[:, l, 1:2], 0.0, ALU.add,
                                  ALU.min).then_inc(elu_ready, 1)

            def elu_last(p, k):
                dve.wait_ge(elu_exp, p * 4 + (k + 1) + 1)
                dve.scalar_tensor_tensor(hT[k % 2][:, :, :], y0[:, :, :], -1.0, r0[:, :, :], ALU.add,
                                         ALU.add).then_inc(h_ready, 1)

            def add_rows(p, bb):
                dve.wait_ge(rows_mm, p * 2 + (bb + 1))
                xb = X[:, bass.ds(p * (2 * TB) + bb * TB, TB), :].rearrange("p t d -> p (t d)")
                dve.tensor_tensor(xb, xb, bank[3][:, :], ALU.add).then_inc(x1_ready, 1)
                held = dve.to_reg(p * 2 + (bb + 1) + 1)
                dve.wait_ge(consts_ready, 1)
                dve.wait_ge(x1_ready, held)

            def keep_rows(p, bb):
                t0 = p * (2 * TB) + bb * TB
                xh = xhi[:, bass.ds(t0, TB), :]
                dve.tensor_copy(xh, xln[:, :, :]).then_inc(xln_ready, 1)
                dve.wait_ge(xln_ready, p * 2 + (bb + 1))
                link(dve.tensor_tensor(xlo[:, bass.ds(t0, TB), :], xln[:, :, :], xh, ALU.subtract), p * GAT_STEPS)

            def adjacency(p, bb):
                layernorm_apply(p * 2 + bb, p * GAT_STEPS, rstd_ready, p * 4 + (bb + 1), maskN[:, bb, :, :])
                link(dve.tensor_scalar(maskN[:, bb, :, :], maskN[:, bb, :, :], 1.0, -MASK, ALU.subtract,
                                       ALU.mult), p * GAT_STEPS)

            with dve.Fori(0, B // 2) as p:
                base = p * GAT_STEPS
                steps[0] = 0
                prep_copy(p, 0, 0)
                layernorm_stats(p * 2, base, veps_ready)
                prep_copy(p, 0, 2)
                adjacency(p, 0)
                for i in range(4 * GH + 1):
                    k, h = i // GH, i % GH
                    if i < 4 * GH:
                        if h in (0, 4):
                            dve.wait_ge(prep_dve, p * 12 + (3 * k + 2 + h // 4) + 1)
                        if h in (2, 6):
                            dve.wait_ge(prep_act, p * 12 + (3 * k + 2 + h // 4) + 1)
                        dve.wait_ge(u_ready, p * 64 + (2 * i + 2) + 1)
                        dve.wait_ge(exp_done, p * 64 + max(2 * i - 2, 0) + 1)
                        for t in range(TB):
                            dve.scalar_tensor_tensor(L[:, i % 2, t, :], NB[:, k % 2, h, :],
                                                     selfS[:, k % 2, t, h:h + 1], U[:, i % 4, t, :],
                                                     ALU.add, ALU.min).then_inc(leak_done, 1)
                        for t in range(TB):
                            held = dve.to_reg(p * 64 + (2 * i + t + 1) + 1)
                            dve.wait_ge(consts_ready, 1)
                            dve.wait_ge(leak_done, held)
                            dve.tensor_tensor_reduce(L[:, i % 2, t, :], L[:, i % 2, t, :], maskN[:, k % 2, t, :],
                                                     1.0, 3.4e38, ALU.add, ALU.min, M[:, i % 2, t:t + 1],
                                                     ).then_inc(e_ready, 1)
                    if h == 0 and i > 0:
                        dve.wait_ge(exp_done, p * 64 + 2 * i + 1)
                        link(dve.reciprocal(Ri[:, :, :], Sm[:, (k - 1) % 2, :, :]), base)
                        if k > 1:
                            dve.wait_ge(sums_mm, p * 4 + k - 1)
                        dve.tensor_copy(rX[:, :, :, :], Ri[:, :, :].unsqueeze(3).to_broadcast([P, TB, GH, GO]),
                                        ).then_inc(sums_ready, 1)
                    if (h == 2 and i > 2) or i == 4 * GH:
                        elu_first(p, k - 1)
                    if (h == 3 and i > 3) or i == 4 * GH:
                        elu_last(p, k - 1)
                    if k < 4 and h == 0:
                        prep_copy(p, k, 4)
                    if k < 3 and h in (5, 6):
                        prep_copy(p, k + 1, 2 * h - 10)
                    if i == 2:
                        layernorm_stats(p * 2 + 1, base, veps_ready)
                    if i == 4:
                        adjacency(p, 1)
                    if k == 3 and h == 6:
                        add_rows(p, 0)
                        layernorm_stats(p * 2, base, veps_ready)
                    if k == 3 and h == 7:
                        layernorm_apply(p * 2, base, rstd_ready, p * 4 + 3, xln)
                        keep_rows(p, 0)
                add_rows(p, 1)
                layernorm_stats(p * 2 + 1, base, veps_ready)
                dve.wait_ge(lnT_mm, p * 2 + 1)
                layernorm_apply(p * 2 + 1, base, rstd_ready, p * 4 + 4, xln)
                keep_rows(p, 1)
                assert steps[0] == GAT_STEPS, steps[0]
            dve.wait_ge(lnT_mm, B)
            base = (B // 2) * GAT_STEPS
            steps[0] = 0

            dve.wait_ge(big_ready, 6)
            dve.wait_ge(logit_mm, 1)
            link(dve.tensor_copy(Lp[:, :, 0:E], bank[7][:, 0:NT * E].rearrange("p (t e) -> p t e", t=NT)), base)
            for t in range(NT):
                link(dve.max(top8[:, t, :], Lp[:, t, :]), base)
            dve.tensor_tensor(prob[:, :, :], Lp[:, :, 0:E], top8[:, :, 4:5].to_broadcast([P, NT, E]),
                              ALU.subtract).then_inc(route_exp_in, 1)
            for t in range(NT):
                link(dve.match_replace(rep[:, t, :], top8[:, t, :], Lp[:, t, :], -BIG), base)
            link(dve.tensor_scalar(sel[:, :, :], rep[:, :, 0:E], -BIG, None, ALU.is_equal), base)
            dve.tensor_copy(selb[:, :, :], sel[:, :, :]).then_inc(sel_ready, 1)
            dve.wait_ge(route_exp, 1)
            link(dve.tensor_reduce(ssum[:, :], prob[:, :, :], AX_X, ALU.add), base)
            link(dve.reciprocal(srec[:, :], ssum[:, :]), base)
            link(dve.tensor_tensor(prob[:, :, :], prob[:, :, :], srec[:, :].unsqueeze(2).to_broadcast([P, NT, E]),
                                   ALU.mult), base)
            link(dve.tensor_tensor(wgt[:, :, :], prob[:, :, :], sel[:, :, :], ALU.mult), base)
            link(dve.tensor_reduce(ssum[:, :], wgt[:, :, :], AX_X, ALU.add), base)
            link(dve.tensor_scalar(ssum[:, :], ssum[:, :], 1e-20, None, ALU.add), base)
            link(dve.reciprocal(srec[:, :], ssum[:, :]), base)
            link(dve.tensor_tensor(wgt[:, :, :], wgt[:, :, :], srec[:, :].unsqueeze(2).to_broadcast([P, NT, E]),
                                   ALU.mult), base)

            dve.wait_ge(rank_mm, 1)
            rank = bank[6][:, 0:NT * E].rearrange("p (t e) -> p t e", t=NT)
            link(dve.scalar_tensor_tensor(keep[:, :, :], rank, float(CAP), sel[:, :, :], ALU.is_lt, ALU.mult), base)
            link(dve.scalar_tensor_tensor(slotf[:, :, :], rank, NO_SLOT, keep[:, :, :], ALU.subtract, ALU.mult), base)
            link(dve.tensor_scalar(slotv[:, :, :], slotf[:, :, :], NO_SLOT, None, ALU.add), base)
            for t in range(NT):
                dve.tensor_tensor(disp[:, t, :, :], iotah[:, :].unsqueeze(1).to_broadcast([P, E, CAP]),
                                  slotv[:, t, :].unsqueeze(2).to_broadcast([P, E, CAP]),
                                  ALU.is_equal).then_inc(disp_ready, 1)
            link(dve.tensor_tensor(key[:, :, :], rowof[:, :].unsqueeze(1).to_broadcast([P, NT, E]), rank,
                                   ALU.subtract), base)
            link(dve.tensor_tensor(key[:, :, :], key[:, :, :], keep[:, :, :], ALU.mult), base)
            for t in range(NT):
                link(dve.max(keytop[:, t, :], key[:, t, :]), base)
            dve.tensor_scalar(idx[:, :, :], keytop[:, :, 0:TOPK], -1.0, float(ZROW), ALU.mult,
                              ALU.add).then_inc(idx_ready, 1)
            link(dve.tensor_tensor(eq[:, :, :, :], key[:, :, :].unsqueeze(2).to_broadcast([P, NT, TOPK, E]),
                                   keytop[:, :, 0:TOPK].unsqueeze(3).to_broadcast([P, NT, TOPK, E]),
                                   ALU.is_equal), base)
            link(dve.tensor_tensor(eq[:, :, :, :], eq[:, :, :, :],
                                   wgt[:, :, :].unsqueeze(2).to_broadcast([P, NT, TOPK, E]), ALU.mult), base)
            link(dve.tensor_reduce(wk[:, :, :], eq[:, :, :, :], AX_X, ALU.add), base)

            n = 0
            m = 0
            for c in range(2):
                for i in range(3):
                    rows = min(P, IS - i * P)
                    dve.wait_ge(shs_ready, n + 1)
                    dve.wait_ge(shd_mm, c * 4)
                    dve.tensor_tensor(smid[0:rows, i, :], sgs[0:rows, :], bank[2 + n % 2][0:rows, :],
                                      ALU.mult).then_inc(shm_ready, 1)
                    n += 1
                for t in range(4):
                    dve.wait_ge(shd_mm, c * 4 + t + 1)
                    dve.tensor_tensor(X[:, c * 4 + t, :], X[:, c * 4 + t, :], bank[4 + t % 2][:, 0:D],
                                      ALU.add).then_inc(shd_add, 1)

            with dve.Fori(0, E // NW) as i:
                for f in range(NW):
                    dve.wait_ge(exs_ready, i * NW + (f + 1))
                    dve.wait_ge(exd_mm, i * NW + max(f, 1))
                    dve.tensor_tensor(emid[:, f % 2, :, :].rearrange("p j c -> p (j c)"), esg[:, f % 2, :],
                                      bank[2 + f % 2][0:IH, 0:2 * CAP], ALU.mult).then_inc(exm_ready, 1)

            dve.wait_ge(exg_mm, E)
            dve.memset(kblk[:, :, :, :], 0.0).then_inc(zero_ready, 1)

            dve.wait_ge(ld_w13, 16 * 4)
            for rows, ks in ((P, slice(0, 5)), (HID - 5 * P, slice(5, 6))):
                x = w2f[0:rows, ks, :]
                for part in range(3):
                    y = w2p[0:rows, part, ks, :]
                    link(dve.tensor_copy(y, x), base)
                    if part < 2:
                        link(dve.tensor_tensor(x, x, y, ALU.subtract), base)
            dve.engine_nop().then_inc(wsplit_ready, 1)

            def combine(t):
                dve.wait_ge(g_ld[t], 16 * TOPK)
                for k in range(TOPK):
                    link(dve.scalar_tensor_tensor(X[:, t, :], gath[:, t * TOPK + k, :], wk[:, t, k:k + 1],
                                                  X[:, t, :], ALU.mult, ALU.add), base)

            def att_ln_apply(b):
                dve.wait_ge(l2_rstd, b + 1)
                for t in range(TB):
                    dve.tensor_scalar(xln[:, t, :], row(b, t), mv[:, t, 0:1], rstd[:, t:t + 1], ALU.subtract,
                                      ALU.mult).then_inc(l2_xln, 1)

            def att_keys(b):
                dve.tensor_copy(kvb[:, :, :], kvr[:, bass.ds(b * TB, TB), 0, :]).then_inc(kvb_ready, 1)

            def att_back_evac(b, j):
                dve.wait_ge(et2_mm, b * 16 + (2 * j + 2) + 1)
                dve.wait_ge(cx_mm, b * 8 + max(j, 1))
                dve.tensor_copy(ET2[:, j % 2, 1, :, :].rearrange("p t s -> p (t s)"),
                                bank[3][:, :]).then_inc(et2_dve, 1)

            def att_max(b, j, first=False):
                if not first:
                    dve.wait_ge(ex2_ready, b * 32 + (4 * j - 4) + 1)
                for t in range(TB):
                    dve.wait_ge(sc_mm, b * 16 + (2 * j + t + 1))
                    dve.tensor_reduce(nmx[:, j % 2, t, :], bank[t][:, :].rearrange("p (h s) -> p h s", h=2),
                                      AX_X, ALU.max, negate=True).then_inc(mx_ready, 1)

            def att_context_evac(b, j):
                dve.wait_ge(cx_mm, b * 8 + (j + 1) + 1)
                dve.wait_ge(o_mm, b + 1)
                dve.tensor_copy(cxT[:, j, :], bank[4 + j % 2][:, 0:S]).then_inc(cx_evac, 1)

            def att_inverse(b, j, first=False):
                dve.wait_ge(ex2_ready, b * 32 + (4 * j + 4) + 1)
                if not first:
                    dve.wait_ge(en2_ready, b * 32 + (4 * j - 4) + 1)
                dve.reciprocal(R2[:, j % 2, :, :], S2[:, j % 2, :, :]).then_inc(ri2_ready, 1)

            def att_add(b):
                dve.wait_ge(o_mm, b + 1 + 1)
                xb = X[:, bass.ds(b * TB, TB), :].rearrange("p t d -> p (t d)")
                dve.tensor_tensor(xb, xb, bank[7][:, :], ALU.add).then_inc(x3_ready, 1)

            combine(0)
            combine(1)
            layernorm_stats(0, base, l2_veps)
            att_ln_apply(0)
            att_keys(0)
            att_max(0, 0, first=True)
            att_inverse(0, 0, first=True)
            att_max(0, 1, first=True)
            att_inverse(0, 1, first=True)
            for t in range(2, NT):
                combine(t)
            dve.engine_nop().then_inc(combined, 1)
            base += steps[0]
            ATT_STEPS = 4
            with dve.Fori(0, B - 1) as b:
                base2 = b * ATT_STEPS + base
                steps[0] = 0
                for j in range(2, AH // 2):
                    att_back_evac(b, j - 2)
                    att_max(b, j)
                    att_context_evac(b, j - 2)
                    if j == 2:
                        layernorm_stats(b + 1, base2, l2_veps)
                    if j == 3:
                        dve.wait_ge(l2_T_mm, b + 1)
                        att_ln_apply(b + 1)
                    att_inverse(b, j)
                for j in range(2):
                    att_back_evac(b, j + 6)
                    att_max(b + 1, j)
                    att_context_evac(b, j + 6)
                    att_inverse(b + 1, j)
                att_keys(b + 1)
                att_add(b)
                assert steps[0] == ATT_STEPS, steps[0]
            base += (B - 1) * ATT_STEPS
            for j in range(2, AH // 2 + 2):
                att_back_evac(B - 1, j - 2)
                if j < AH // 2:
                    att_max(B - 1, j)
                att_context_evac(B - 1, j - 2)
                if j < AH // 2:
                    att_inverse(B - 1, j)
            att_add(B - 1)
            dve.wait_ge(x3_ready, B + 1)

            def quantise(x, tmp, inv, base):
                link(dve.tensor_reduce(amax[:, :], x, AX_X, ALU.max, apply_absolute_value=True), base)
                link(dve.tensor_scalar(inv, amax[:, :], 1e-5, 1.0 / 127.0, ALU.max, ALU.mult), base)
                link(dve.reciprocal(scl[:, :], inv), base)
                link(dve.tensor_scalar(tmp, x, scl[:, 0:1], ROUND, ALU.mult, ALU.add), base)
                return dve.tensor_scalar(tmp, tmp, ROUND - 128.0, ROUND + 127.0, ALU.max, ALU.min)

            def ff_first(n, b, t, base, first=False):
                dve.wait_ge(f_rstd, b + 1)
                link(dve.tensor_scalar(xln[:, t, :], row(b, t), mv[:, t, 0:1], rstd[:, t:t + 1],
                                       ALU.subtract, ALU.mult), base)
                link(quantise(xln[:, t, :], tmp1[:, :], is1[:, t:t + 1], base), base)
                if not first:
                    dve.wait_ge(f_q1T_mm, n - 1)
                dve.tensor_scalar(q1[:, t, :], tmp1[:, :], ROUND, None, ALU.subtract).then_inc(f_q1, 1)

            def ff_gate(n, g, base):
                dve.wait_ge(f_r_ready, n + 1)
                link(dve.scalar_tensor_tensor(gated[:, 0:512], bank[3 * g + 1][:, :], is1[:, g:g + 1],
                                              r2[:, 0:512], ALU.mult, ALU.mult), base)
                dve.scalar_tensor_tensor(gated[:, 512:HID], bank[3 * g + 2][:, HID - 512:2 * (HID - 512)],
                                         is1[:, g:g + 1], r2[:, 512:HID], ALU.mult, ALU.mult,
                                         ).then_inc(f_g_ready, 1)

            def ff_mean(n):
                dve.wait_ge(f_sq_ready, n + 1)
                dve.tensor_scalar(msq[:, :], ms[:, :], 1.0 / HID, RMS_EPS, ALU.mult, ALU.add,
                                  ).then_inc(f_ms, 1)

            def ff_second(n, g, base):
                dve.wait_ge(f_rms, n + 1)
                link(dve.scalar_tensor_tensor(gated[:, :], gated[:, :], rms[:, 0:1], nwb[:, :], ALU.mult,
                                              ALU.mult), base)
                dve.wait_ge(f_q2, n + 1)
                quantise(gated[:, :], tmp2[:, :], is2[:, g:g + 1], base).then_inc(f_t2, 1)

            def ff_result(n, b, t):
                dve.wait_ge(f_o_mm, n + 1 + 1)
                dve.wait_ge(st_out[t], b * 16 + 16)
                dve.scalar_tensor_tensor(yt[:, t, :], bank[7][:, 0:D], is2[:, t:t + 1], row(b, t), ALU.mult,
                                         ALU.add).then_inc(f_out, 1)

            steps[0] = 0
            layernorm_stats(0, base, f_veps)
            ff_first(0, 0, 0, base, first=True)
            ff_first(1, 0, 1, base, first=True)
            ff_gate(0, 0, base)
            layernorm_stats(1, base, f_veps)
            ff_mean(0)
            ff_first(2, 1, 0, base)
            ff_second(0, 0, base)
            ff_gate(1, 1, base)
            ff_mean(1)
            ff_first(3, 1, 1, base)
            ff_second(1, 1, base)
            base += steps[0]
            FF_STEPS = 28
            with dve.Fori(1, B - 1) as b:
                base3 = b * FF_STEPS + (base - FF_STEPS)
                steps[0] = 0
                for t in range(TB):
                    n = b * TB + t
                    ff_gate(n, t, base3)
                    ff_result(b * TB + (t - 2), b - 1, t)
                    if t == 0:
                        layernorm_stats(b + 1, base3, f_veps)
                    ff_mean(n)
                    ff_first(b * TB + (t + 2), b + 1, t, base3)
                    ff_second(n, t, base3)
                assert steps[0] == FF_STEPS, steps[0]
            base += (B - 2) * FF_STEPS
            steps[0] = 0
            for n in range(NT - 2, NT):
                ff_gate(n, n % 2, base)
                ff_result(n - 2, n // 2 - 1, n % 2)
                ff_mean(n)
                ff_second(n, n % 2, base)
            for n in range(NT - 2, NT):
                ff_result(n, n // 2, n % 2)

        @block.gpsimd
        def _(pool):
            pool.sem_inc(u_ready, 1)
            pool.sem_inc(en2_ready, 1)
            pool.wait_ge(ld_kv, 16 * 3)
            for b in range(B):
                k4 = kv[:, b * TB:(b + 1) * TB, :]
                d4 = kvr[:, b * TB:(b + 1) * TB, 0, :]
                t4 = kvt[:, b * TB:(b + 1) * TB, :]
                H2 = CD // 2
                pool.tensor_tensor(d4, k4, cosd[:, :, :], ALU.mult).then_inc(pool_step, 1)
                pool.tensor_tensor(t4[:, :, 0:H2], k4[:, :, H2:CD], sind[:, :, 0:H2], ALU.mult,
                                   ).then_inc(pool_step, 1)
                pool.tensor_tensor(t4[:, :, H2:CD], k4[:, :, 0:H2], sind[:, :, H2:CD], ALU.mult,
                                   ).then_inc(pool_step, 1)
                pool.wait_ge(pool_step, 5 * b + 3)
                pool.tensor_tensor(d4[:, :, 0:H2], d4[:, :, 0:H2], t4[:, :, 0:H2], ALU.subtract,
                                   ).then_inc(pool_step, 1)
                pool.tensor_tensor(d4[:, :, H2:CD], d4[:, :, H2:CD], t4[:, :, H2:CD], ALU.add,
                                   ).then_inc(pool_step, 1)
            pool.wait_ge(pool_step, 5 * B)
            pool.tensor_copy(kvr[:, :, 1, :], kvr[:, :, 0, :]).then_inc(kvr_ready, 1)

            pool.wait_ge(consts_ready, 1)

            def root(count, veps_sem, rstd_sem, src=None, dst=None):
                pool.wait_ge(veps_sem, count)
                src = veps[:, :] if src is None else src
                dst = rstd[:, :] if dst is None else dst
                pool.tensor_tensor(dst, src, half[:, 0:src.shape[1]], ALU.pow).then_inc(rstd_sem, 1)

            with pool.Fori(0, B // 2) as p:
                root(p * 4 + 1, veps_ready, rstd_ready)
                for i in range(4 * GH):
                    k, h = i // GH, i % GH
                    if i == 4:
                        root(p * 4 + 2, veps_ready, rstd_ready)
                    if h % 2 == 0:
                        held = pool.to_reg(p * 12 + (3 * k + 2 + h // 4) + 1)
                        pool.wait_ge(consts_ready, 1)
                    if h in (0, 4):
                        pool.wait_ge(prep_dve, held)
                    if h in (2, 6):
                        pool.wait_ge(prep_act, held)
                    held = pool.to_reg(p * 64 + 2 * max(i - 3, 0) + 1)
                    pool.wait_ge(consts_ready, 1)
                    pool.wait_ge(leak_done, held)
                    for t in range(TB):
                        pool.tensor_scalar(U[:, i % 4, t, :], NB[:, k % 2, h, :], 0.2, self02[:, k % 2, t, h:h + 1],
                                           ALU.mult, ALU.add).then_inc(u_ready, 1)
                root(p * 4 + 3, veps_ready, rstd_ready)
                root(p * 4 + 4, veps_ready, rstd_ready)

            pool.wait_ge(ld_w13, 16 * 4)
            pool.wait_ge(disp_mm, 8)
            for part in range(3):
                y = w13p[:, part, :, :]
                pool.wait_ge(pool_step, 5 * B + part)
                pool.tensor_copy(y, w13f).then_inc(w13_part, 1)
                pool.wait_ge(w13_part, part + 1)
                if part < 2:
                    pool.tensor_tensor(w13f, w13f, y, ALU.subtract).then_inc(pool_step, 1)

            pool.wait_ge(idx_ready, 1)
            pool.wait_ge(st_eout[0], 16 * (E // 2) + 16)
            pool.wait_ge(st_eout[1], 16 * (E // 2) + 16)
            pool.wait_ge(st_z, 16)
            for t in range(NT):
                if t == 4:
                    root(1, l2_veps, l2_rstd)
                for k in range(TOPK):
                    pool.indirect_dma_start(out=gath[:, t * TOPK + k, :], out_offset=None, in_=eout[:, :],
                                            in_offset=bass.IndirectOffsetOnAxis(ap=idx[:, t, k:k + 1], axis=0),
                                            ).then_inc(g_ld[t], 16)

            def normalise(b, j):
                held = pool.to_reg(b * 8 + (j + 1) + 1)
                pool.wait_ge(consts_ready, 1)
                pool.wait_ge(ri2_ready, held)
                for t in range(TB):
                    for h in range(2):
                        pool.tensor_scalar(E2[:, j % 2, t, h, :], E2[:, j % 2, t, h, :],
                                           R2[:, j % 2, t, h:h + 1], 1.0, ALU.mult,
                                           ALU.mult).then_inc(en2_ready, 1)

            normalise(0, 0)
            normalise(0, 1)
            with pool.Fori(0, B - 1) as b:
                root(b + 2, l2_veps, l2_rstd)
                for j in range(2, AH // 2):
                    normalise(b, j)
                for j in range(2):
                    normalise(b + 1, j)
            for j in range(2, AH // 2):
                normalise(B - 1, j)
            root(1, f_veps, f_rstd)
            root(2, f_veps, f_rstd)
            root(1, f_ms, f_rms, msq[:, :], rms[:, :])
            root(2, f_ms, f_rms, msq[:, :], rms[:, :])
            with pool.Fori(1, B - 1) as b:
                root(b + 2, f_veps, f_rstd)
                for t in range(TB):
                    root(b * TB + (t + 1), f_ms, f_rms, msq[:, :], rms[:, :])
            for n in range(NT - 2, NT):
                root(n + 1, f_ms, f_rms, msq[:, :], rms[:, :])


def _layouts(inp):
    f = lambda n: np.asarray(inp[n])
    rows = lambda n: f(n).reshape(T, -1)
    pos = np.arange(S, dtype=np.float32)
    inv = (np.float32(1.0) / np.float32(10000.0) ** (np.arange(0, CD, 2, dtype=np.float32) / np.float32(CD)))
    freqs = pos[:, None] * inv.astype(np.float32)[None, :]
    block = np.zeros((2 * P, GH), np.float32)
    for h in range(GH):
        block[h * GO:(h + 1) * GO, h] = -1.0
    return {
        "x": rows("x"),
        "ctx": rows("ctx_512"),
        "ctxT": rows("ctx_512").T,
        "w0": f("L0_xattn_W0").transpose(1, 0, 2).reshape(CD, D),
        "w0T": f("L0_xattn_W0").transpose(0, 2, 1).reshape(D, CD),
        "w1": f("L0_xattn_W1").transpose(1, 0, 2).reshape(D, D),
        "w1T": f("L0_xattn_W1").transpose(0, 2, 1).reshape(D, D),
        "cols": np.stack([f(f"L0_xattn_{n}{l}").reshape(KT, P) for l in range(2) for n in ("a_self", "a_neigh", "b")],
                         ).reshape(-1, P).T,
        "gwT": f("L0_ffn_gate_w").T,
        "wg": f("L0_ffn_w_gate"), "wu": f("L0_ffn_w_up"), "wd": f("L0_ffn_w_down"),
        "swg": f("L0_ffn_sw_gate"), "swu": f("L0_ffn_sw_up"), "swd": f("L0_ffn_sw_down"),
        "wq": f("L1_xattn_Wq"),
        "kcqT": f("L1_xattn_w_kc_q").transpose(2, 0, 1).reshape(AQ, AH * AK),
        "kckv": f("L1_xattn_w_kc_kv").transpose(1, 0, 2).reshape(AK, AH * CD),
        "qrT": f("L1_xattn_W_qr").transpose(2, 0, 1).reshape(AR, AH * AQ),
        "krT": f("L1_xattn_W_kr").transpose(2, 0, 1).reshape(AR, AH * CD),
        "woT": f("L1_xattn_Wo").T,
        "w13T": f("L1_ffn_w13").T, "w2T": f("L1_ffn_w2").T, "nw": f("L1_ffn_norm_w"),
        "ident": np.eye(P, dtype=np.float32),
        "upper": np.triu(np.ones((P, P), np.float32), 1),
        "iota": np.tile(np.arange(CAP, dtype=np.float32), (P, 1)),
        "rowof": np.tile(ZROW - CAP * np.arange(E, dtype=np.float32), (P, 1)),
        "block": block,
        "cos": np.repeat(np.cos(freqs), 2, axis=-1).astype(np.float32),
        "sin": np.repeat(np.sin(freqs), 2, axis=-1).astype(np.float32),
    }


def kernel(**inputs):
    import concourse.bacc as _bacc
    from concourse.bass_utils import run_bass_kernel_spmd as _run

    nc = _bacc.Bacc("TRN2", target_bir_lowering=False, num_devices=1)
    arrays, a = {}, {}
    for name, x in _layouts(inputs).items():
        x = np.ascontiguousarray(x)
        arrays[f"in_{name}"] = x
        a[name] = nc.dram_tensor(f"in_{name}", x.shape, mybir.dt.from_np(x.dtype), kind="ExternalInput").ap()
    out = nc.dram_tensor("out_0", (T, D), F32, kind="ExternalOutput").ap()
    build(nc, a, out)
    r = _run(nc, [arrays], core_ids=[0])
    return r.results[0]["out_0"].reshape(B, S, D)
```

```python
from contextlib import ExitStack

import numpy as np

import concourse.bass as bass
from concourse import mybir

F32 = mybir.dt.float32
F16 = mybir.dt.float16
BF16 = mybir.dt.bfloat16
U32 = mybir.dt.uint32
ALU = mybir.AluOpType
ACT = mybir.ActivationFunctionType
AX_X = mybir.AxisListType.X

P = 128
B, S, D = 4, 256, 256
T = B * S
NT = T // P
TB = S // P
KT = D // P
CD = 64
GH, GO = 8, 32
E, TOPK, IE, CAP = 16, 4, 176, 128
IS = 352
AH, AK, AQ, AR = 16, 128, 192, 64
HID = 704
LN_EPS, RMS_EPS = 1e-5, 1e-5
MASK = 1e10
BIG = 3.0e38
ROUND = 1.5 * 2.0 ** 23
NO_SLOT = 200.0
ZROW = E * CAP


def build(nc, a, out):
    ctx = ExitStack()
    with ctx:
        def sb(name, shape, dt=F32):
            return ctx.enter_context(nc.sbuf_tensor(name, shape, dt))

        def sem(name):
            return ctx.enter_context(nc.semaphore(name))

        bank = [ctx.enter_context(nc.psum_tensor(f"bank{i}", [P, 512], F32)) for i in range(8)]

        X = sb("X", [P, NT, D])
        ident = sb("ident", [P, P])
        identh = sb("identh", [P, P], BF16)
        half = sb("half", [P, 2])
        xlnT = sb("xlnT", [P, KT, T])
        bnst = sb("bnst", [P, TB, 6])
        mv = sb("mv", [P, TB, 2])
        veps = sb("veps", [P, TB])
        rstd = sb("rstd", [P, TB])
        xln = sb("xln", [P, TB, D])
        Nw = sb("Nw", [P, KT, AH * CD])
        Pw = sb("Pw", [P, AH // 2, D])
        work = sb("work", [P, 19200])
        place = [0]

        def at(shape, rows=P, dt=F32):
            n = int(np.prod(shape)) * (1 if dt is F32 else 0.5)
            lo = place[0]
            place[0] += int(n)
            assert place[0] <= 19200, place[0]
            x = work[0:rows, lo:place[0]]
            x = x if dt is F32 else x.bitcast(dt)
            names = "abcd"[:len(shape)]
            return x.rearrange(f"p ({' '.join(names)}) -> p {' '.join(names)}", **dict(zip(names[1:], shape[1:])))

        ctxT = at([T], CD)
        ctxb = Nw[0:CD, 0, 0:2 * S].rearrange("p (b s) -> p b s", b=2)
        maskN = Nw[:, 1, :].rearrange("p (b t s) -> p b t s", b=2, t=TB)
        w0 = at([1, D], CD)
        w1 = at([KT, D])
        w0T = at([KT, CD])
        w1T = at([KT, D])
        cols = sb("cols", [P, 2, 3, KT])
        acol = cols[:, :, 0:2, :]
        bcol = cols[:, :, 2, :]
        blockmask = sb("blockmask", [P, KT, GH])
        abd = sb("abd", [P, 2, KT, 2 * GH])
        was = [sb("was0", [CD, 1, GH]), sb("was1", [P, KT, GH])]
        ROWS = (0, 64, 96)
        NR = ROWS[2] + GH
        wan = [at([1, NR], CD), at([KT, NR])]
        parts = at([S], NR, BF16)
        rest = at([S], NR)
        pickf = at([GH], NR)
        pick = at([GH, P], NR, BF16)
        featS = at([2, TB, D])
        selfS = sb("selfS", [P, 2, TB, GH])
        self02 = sb("self02", [P, 2, TB, GH])
        NB = at([2, GH, S])
        U = at([4, TB, S])
        L = at([2, TB, S])
        M = sb("M", [P, 2, TB])
        Ex = at([2, TB, S])
        Sm = sb("Sm", [P, 2, TB, GH])
        Ri = sb("Ri", [P, TB, GH])
        rX = at([TB, GH, GO])
        rT = at([KT, S])
        ETs = at([2, TB, S])
        y0 = at([KT, S])
        r0 = at([KT, S])
        hT = [at([KT, S]), at([KT, S])]
        place[0] = 0
        gwT = sb("gwT", [P, KT, E])
        Lp = sb("Lp", [P, NT, E + TOPK])
        top8 = sb("top8", [P, NT, 8])
        rep = sb("rep", [P, NT, E + TOPK])
        sel = sb("sel", [P, NT, E])
        selb = sb("selb", [P, NT, E], BF16)
        prob = sb("prob", [P, NT, E])
        wgt = sb("wgt", [P, NT, E])
        ssum = sb("ssum", [P, NT])
        srec = sb("srec", [P, NT])
        keep = sb("keep", [P, NT, E])
        slotf = sb("slotf", [P, NT, E])
        slotv = sb("slotv", [P, NT, E], F16)
        key = sb("key", [P, NT, E])
        rowof = sb("rowof", [P, E])
        keytop = sb("keytop", [P, NT, 8])
        idx = sb("idx", [P, NT, TOPK], U32)
        eq = sb("eq", [P, NT, TOPK, E])
        wk = sb("wk", [P, NT, TOPK])
        upper = sb("upper", [P, P], BF16)
        upperf = sb("upperf", [P, P])
        onesb = sb("onesb", [P, P], BF16)
        iotaf = sb("iotaf", [P, CAP])
        iotah = sb("iotah", [P, CAP], F16)
        xhi = sb("xhi", [P, NT, D], F16)
        xlo = sb("xlo", [P, NT, D], F16)
        arena = sb("arena", [P, 17408])
        gath = arena[:, 8192:16384].rearrange("p (j d) -> p j d", j=NT * TOPK)
        wq = arena[:, 0:4096].rearrange("p (h d) -> p h d", h=AH)
        wo = arena[:, 4096:8192].rearrange("p (h d) -> p h d", h=AH)
        kcqT = arena[0:96, 8192:12288].rearrange("p (t n) -> p t n", t=2)
        qrT = arena[0:AR, 12288:15360].rearrange("p (h q) -> p h q", h=AH)
        krT = arena[0:AR, 15360:16384].rearrange("p (h c) -> p h c", h=AH)
        kckv = arena[:, 16384:17408].rearrange("p (h c) -> p h c", h=AH)
        xgT = at([KT, E * CAP])
        kblk = xgT[:, 0, :].rearrange("p (b h s) -> p b h s", b=B, h=2)
        zrow = sb("zrow", [1, D])
        sgs = at([512])
        smid = at([3, 512])
        lgT = smid[0:E, 0:2, :].rearrange("p a c -> p (a c)")
        IH = IE // 2
        esg = sgs[0:IH, :].rearrange("p (f c) -> p f c", f=2)
        emid = smid[0:IH, 0, :].rearrange("p (f j c) -> p f j c", f=2, j=2)
        eoS = smid[:, 1, :].rearrange("p (f d) -> p f d", f=2)
        NW = 4
        wg = at([NW, KT, IE])
        wu = at([NW, KT, IE])
        wd = at([NW, 2, D], IH)
        swd = sb("swd", [P, 3, D])
        AJ = AH // 2
        early2 = work[:, 0:4096 + 4 * 512]
        cT = early2[:, 0:AJ * AQ].rearrange("p (j q) -> p j q", j=AJ)
        cQ = early2[0:96, AJ * AQ:AJ * AQ + 2 * AJ * P].rearrange("p (j t c) -> p j t c", j=AJ, t=2)
        dT = early2[:, 3584:4608].rearrange("p (j k) -> p j k", j=AJ)
        dK = early2[:, 4608:5632].rearrange("p (j c) -> p j c", j=AJ)
        nT = early2[:, 0:AJ * D].rearrange("p (j d) -> p j d", j=AJ)
        early = Pw[:, :, :].rearrange("p j d -> p (j d)")
        kv = early[:, 0:512].rearrange("p (t c) -> p t c", t=NT)
        kvt = early[:, 512:1024].rearrange("p (t c) -> p t c", t=NT)
        cosd = early[:, 1024:1152].rearrange("p (t c) -> p t c", t=TB)
        sind = early[:, 1152:1280].rearrange("p (t c) -> p t c", t=TB)
        kvr = sb("kvr", [P, NT, 2, CD])
        w13f = arena[:, 0:KT * 2 * HID].rearrange("p (k n) -> p k n", k=KT)
        w2f = arena[:, 2816:2816 + 6 * D].rearrange("p (k n) -> p k n", k=6)
        before = place[0]
        disp = at([NT, E, CAP], dt=F16)
        place[0] = before
        w13p = at([3, KT, 2 * HID], dt=BF16)
        w2p = at([3, 6, D], dt=BF16)
        swg = at([KT, IS])
        swu = at([KT, IS])
        nwb = arena[:, 4352:4352 + HID]
        spare = 4096 + 512 + 3 * 512
        qT = work[:, spare:spare + 2048].rearrange("p (j s) -> p j s", j=AH // 2)
        E2 = work[:, spare + 2048:spare + 4096].rearrange("p (f t h s) -> p f t h s", f=2, t=TB, h=2)
        ET2 = arena[:, 12288:14336].rearrange("p (f h t s) -> p f h t s", f=2, h=2, t=TB)
        cxT = arena[:, 14336:16384].rearrange("p (j s) -> p j s", j=AH // 2)
        xT3 = arena[:, 16384:16896].rearrange("p (k s) -> p k s", k=KT)
        kvb = sb("kvb", [P, TB, CD])
        nmx = sb("nmx", [P, 2, TB, 2])
        S2 = sb("S2", [P, 2, TB, 2])
        R2 = sb("R2", [P, 2, TB, 2])
        spot = [0]

        def piece(shape, dt=F32):
            n = int(np.prod(shape)) // (1 if dt is F32 else 2)
            lo = spot[0]
            spot[0] += n
            assert spot[0] <= 4352 or lo >= 4352 + HID and spot[0] <= 8192
            x = arena[:, lo:spot[0]]
            x = x if dt is F32 else x.bitcast(dt)
            names = "abcd"[:len(shape)]
            return x.rearrange(f"p ({' '.join(names)}) -> p {' '.join(names)}", **dict(zip(names[1:], shape[1:])))

        r1 = piece([HID])
        r2 = piece([HID])
        gated = piece([HID])
        tmp2 = piece([HID])
        tmp1 = piece([D])
        q1 = piece([2, D], BF16)
        q1T = piece([2, KT * P], BF16)
        q2T = piece([2, 6 * P], BF16)
        spot[0] = 4352 + HID
        q2 = piece([2, HID], BF16)
        yt = piece([2, D])
        weighed = piece([HID])
        is1 = sb("is1", [P, 2])
        is2 = sb("is2", [P, 2])
        fstat = sb("fstat", [P, B, 6])
        fveps = sb("fveps", [P, B, TB])
        fnow = sb("fnow", [P, 6])
        amax1 = sb("amax1", [P, 1])
        amax2 = sb("amax2", [P, 1])
        scl1 = sb("scl1", [P, 1])
        scl2 = sb("scl2", [P, 1])
        ms = sb("ms", [P, 1])
        msq = sb("msq", [P, 1])
        rms = sb("rms", [P, 1])
        unround = sb("unround", [P, 1])

        eout = nc.dram_tensor("eout", (ZROW + 1, D), F32, kind="Internal").ap()

        ld_x = sem("ld_x")
        ld_ctxT = sem("ld_ctxT")
        ld_gat = sem("ld_gat")
        ld_const = sem("ld_const")
        ld_attn = sem("ld_attn")
        ld_ffn0 = sem("ld_ffn0")
        ld_sh = sem("ld_sh")
        ld_w13 = sem("ld_w13")
        ld_kv = sem("ld_kv")
        st_out = [sem(f"st_out{g}") for g in range(2)]
        st_eout = [sem(f"st_eout{g}") for g in range(2)]
        st_z = sem("st_z")
        consts_ready = sem("consts_ready")
        abd_ready = sem("abd_ready")
        wa_mm = sem("wa_mm")
        wa_ready = sem("wa_ready")
        ctxb_ready = sem("ctxb_ready")
        nbrow_mm = sem("nbrow_mm")
        nb_split = sem("nb_split")
        prep_mm = sem("prep_mm")
        prep_act = sem("prep_act")
        prep_dve = sem("prep_dve")
        sums_ready = sem("sums_ready")
        sums_mm = sem("sums_mm")
        sums_evac = sem("sums_evac")
        agg_read = sem("agg_read")
        elu_ready = sem("elu_ready")
        elu_exp = sem("elu_exp")
        h_ready = sem("h_ready")
        veps_ready = sem("veps_ready")
        rstd_ready = sem("rstd_ready")
        u_ready = sem("u_ready")
        leak_done = sem("leak_done")
        e_ready = sem("e_ready")
        exp_done = sem("exp_done")
        et_mm = sem("et_mm")
        et_evac = sem("et_evac")
        agg_mm = sem("agg_mm")
        rows_mm = sem("rows_mm")
        x1_ready = sem("x1_ready")
        xln_ready = sem("xln_ready")
        lnT_mm = sem("lnT_mm")
        lnT_evac = sem("lnT_evac")
        cT_mm = sem("cT_mm")
        cT_evac = sem("cT_evac")
        dT_mm = sem("dT_mm")
        dT_evac = sem("dT_evac")
        nT_mm = sem("nT_mm")
        nT_evac = sem("nT_evac")
        c_mm = sem("c_mm")
        c_evac = sem("c_evac")
        d_mm = sem("d_mm")
        d_evac = sem("d_evac")
        n_mm = sem("n_mm")
        n_evac = sem("n_evac")
        p_mm = sem("p_mm")
        p_evac = sem("p_evac")
        logitT_mm = sem("logitT_mm")
        logitT_evac = sem("logitT_evac")
        logit_mm = sem("logit_mm")
        route_exp_in = sem("route_exp_in")
        route_exp = sem("route_exp")
        sel_ready = sem("sel_ready")
        rank_mm = sem("rank_mm")
        disp_ready = sem("disp_ready")
        disp_mm = sem("disp_mm")
        disp_evac = sem("disp_evac")
        idx_ready = sem("idx_ready")
        shg_mm = sem("shg_mm")
        shs_ready = sem("shs_ready")
        shm_ready = sem("shm_ready")
        shd_mm = sem("shd_mm")
        shd_add = sem("shd_add")
        exg_mm = sem("exg_mm")
        exs_ready = sem("exs_ready")
        exm_ready = sem("exm_ready")
        exd_mm = sem("exd_mm")
        exo_ready = sem("exo_ready")
        kvr_ready = sem("kvr_ready")
        kvT_mm = sem("kvT_mm")
        kvT_ready = sem("kvT_ready")
        kvb_ready = sem("kvb_ready")
        l2_veps = sem("l2_veps")
        l2_rstd = sem("l2_rstd")
        l2_xln = sem("l2_xln")
        l2_T_mm = sem("l2_T_mm")
        l2_T_evac = sem("l2_T_evac")
        q_mm = sem("q_mm")
        q_evac = sem("q_evac")
        sc_mm = sem("sc_mm")
        mx_ready = sem("mx_ready")
        ex2_ready = sem("ex2_ready")
        ri2_ready = sem("ri2_ready")
        en2_ready = sem("en2_ready")
        et2_mm = sem("et2_mm")
        et2_act = sem("et2_act")
        et2_dve = sem("et2_dve")
        combined = sem("combined")
        cx_mm = sem("cx_mm")
        cx_evac = sem("cx_evac")
        o_mm = sem("o_mm")
        x3_ready = sem("x3_ready")
        wsplit_ready = sem("wsplit_ready")
        w13_part = sem("w13_part")
        f_veps = sem("f_veps")
        f_rstd = sem("f_rstd")
        f_q1 = sem("f_q1")
        f_q1T_mm = sem("f_q1T_mm")
        f_q1T = sem("f_q1T")
        f_a_mm = sem("f_a_mm")
        f_r_ready = sem("f_r_ready")
        f_g_ready = sem("f_g_ready")
        f_sq_ready = sem("f_sq_ready")
        f_w_ready = sem("f_w_ready")
        f_ms = sem("f_ms")
        f_rms = sem("f_rms")
        f_t2 = sem("f_t2")
        f_q2 = sem("f_q2")
        f_q2T_mm = sem("f_q2T_mm")
        f_q2T = sem("f_q2T")
        f_o_mm = sem("f_o_mm")
        f_out = sem("f_out")
        act_step = sem("act_step")
        f_relu = sem("f_relu")
        dve_step = sem("dve_step")
        pool_step = sem("pool_step")
        zero_ready = sem("zero_ready")
        big_ready = sem("big_ready")
        ld_we = [sem(f"ld_we{i}") for i in range(NW)]
        g_ld = [sem(f"g_ld{i}") for i in range(8)]

        block = ctx.enter_context(nc.Block())

        @block.sync
        def _(sp):
            sp.sem_inc(st_out[0], 16)
            sp.sem_inc(st_out[1], 16)
            sp.sem_inc(st_eout[0], 16)
            sp.sem_inc(st_eout[1], 16)
            sp.dma_start(ctxT[:, :], a["ctxT"]).then_inc(ld_ctxT, 16)
            sp.dma_start(w0T[:, :, :], a["w0T"].rearrange("(k p) n -> p k n", p=P)).then_inc(ld_gat, 16)
            sp.dma_start(w1T[:, :, :], a["w1T"].rearrange("(k p) n -> p k n", p=P)).then_inc(ld_gat, 16)
            sp.dma_start(cols[:, :, :, :], a["cols"].rearrange("p (l i k) -> p l i k", l=2, i=3)).then_inc(ld_gat, 16)
            sp.dma_start(blockmask[:, :, :], a["block"].rearrange("(k p) h -> p k h", p=P)).then_inc(ld_gat, 16)
            sp.dma_start(pickf[:, :], a["pick"]).then_inc(ld_gat, 16)
            sp.dma_start(w0[:, 0, :], a["w0"]).then_inc(ld_gat, 16)
            sp.dma_start(w1[:, :, :], a["w1"].rearrange("(k p) n -> p k n", p=P)).then_inc(ld_gat, 16)
            sp.dma_start(ident[:, :], a["ident"]).then_inc(ld_const, 16)
            sp.dma_start(X[:, :, :], a["x"].rearrange("(t p) d -> p t d", p=P)).then_inc(ld_x, 16)
            sp.dma_start(upperf[:, :], a["upper"]).then_inc(ld_const, 16)
            sp.dma_start(iotaf[:, :], a["iota"]).then_inc(ld_const, 16)
            sp.dma_start(rowof[:, :], a["rowof"]).then_inc(ld_const, 16)
            sp.dma_start(kv[:, :, :], a["ctx"].rearrange("(t p) c -> p t c", p=P)).then_inc(ld_kv, 16)
            sp.dma_start(cosd[:, :, :], a["cos"].rearrange("(t p) c -> p t c", p=P)).then_inc(ld_kv, 16)
            sp.dma_start(sind[:, :, :], a["sin"].rearrange("(t p) c -> p t c", p=P)).then_inc(ld_kv, 16)
            sp.dma_start(gwT[:, :, :], a["gwT"].rearrange("(k p) e -> p k e", p=P)).then_inc(ld_ffn0, 16)
            sp.dma_start(swd[:, 0:2, :], a["swd"][0:2 * P, :].rearrange("(k p) n -> p k n", p=P),
                         ).then_inc(ld_ffn0, 16)
            sp.dma_start(swd[0:IS - 2 * P, 2, :], a["swd"][2 * P:IS, :]).then_inc(ld_ffn0, 16)
            sp.dma_start(wq, a["wq"].rearrange("(h k) d -> k h d", k=P)).then_inc(ld_attn, 16)
            sp.dma_start(wo, a["woT"].rearrange("(h k) d -> k h d", k=P)).then_inc(ld_attn, 16)
            sp.dma_start(kcqT, a["kcqT"].rearrange("(t q) n -> q t n", q=96)).then_inc(ld_attn, 16)
            sp.dma_start(qrT, a["qrT"].rearrange("r (h q) -> r h q", h=AH)).then_inc(ld_attn, 16)
            sp.dma_start(krT, a["krT"].rearrange("r (h c) -> r h c", h=AH)).then_inc(ld_attn, 16)
            sp.dma_start(kckv, a["kckv"].rearrange("k (h c) -> k h c", h=AH)).then_inc(ld_attn, 16)

            def load_expert(e, f):
                gw, uw = (a[n][bass.ds(e, 1), :, :].rearrange("o (k p) n -> p (o k) n", p=P) for n in ("wg", "wu"))
                dw = a["wd"][bass.ds(e, 1), :, :].rearrange("o (j p) n -> p (o j) n", p=IH)
                sp.dma_start(wg[:, f, :, :], gw).then_inc(ld_we[f], 16)
                sp.dma_start(wu[:, f, :, :], uw).then_inc(ld_we[f], 16)
                sp.dma_start(wd[:, f, :, :], dw).then_inc(ld_we[f], 16)

            sp.wait_ge(rows_mm, B)
            sp.wait_ge(h_ready, 2 * B)
            for f in range(NW):
                load_expert(f, f)
            sp.wait_ge(zero_ready, 1)
            sp.dma_start(eout[ZROW:ZROW + 1, :], zrow[:, :]).then_inc(st_z, 16)

            sp.wait_ge(n_evac, 4)
            sp.wait_ge(p_evac, 4)
            sp.dma_start(nwb[:, :], a["nw"].partition_broadcast(P)).then_inc(ld_w13, 16)
            sp.dma_start(w13f, a["w13T"].rearrange("(k p) n -> p k n", p=P)).then_inc(ld_w13, 16)
            sp.dma_start(w2f[:, 0:5, :], a["w2T"][0:5 * P, :].rearrange("(k p) n -> p k n", p=P),
                         ).then_inc(ld_w13, 16)
            sp.dma_start(w2f[0:HID - 5 * P, 5, :], a["w2T"][5 * P:HID, :]).then_inc(ld_w13, 16)
            sp.wait_ge(disp_mm, 8)
            sp.dma_start(swg[:, :, :], a["swg"].rearrange("(k p) n -> p k n", p=P)).then_inc(ld_sh, 16)
            sp.dma_start(swu[:, :, :], a["swu"].rearrange("(k p) n -> p k n", p=P)).then_inc(ld_sh, 16)
            with sp.Fori(0, E // NW - 1) as i:
                for f in range(NW):
                    sp.wait_ge(exo_ready, i * NW + (f + 1) + 1)
                    sp.dma_start(eout[bass.ds(i * (NW * CAP) + f * CAP, CAP), :], eoS[:, f % 2, :],
                                 ).then_inc(st_eout[f % 2], 16)
                    load_expert(i * NW + (NW + f), f)
            for f in range(NW):
                sp.wait_ge(exo_ready, E - NW + f + 1 + 1)
                sp.dma_start(eout[(E - NW + f) * CAP:(E - NW + f + 1) * CAP, :], eoS[:, f % 2, :],
                             ).then_inc(st_eout[f % 2], 16)
            with sp.Fori(0, B) as b:
                for t in range(TB):
                    sp.wait_ge(f_out, b * TB + (t + 1) + 1)
                    sp.dma_start(out[bass.ds(b * S + t * P, P), :], yt[:, t, :]).then_inc(st_out[t], 16)
            sp.wait_ge(st_out[0], 16 * B + 16)
            sp.wait_ge(st_out[1], 16 * B + 16)
            sp.wait_ge(st_eout[0], 16 * (E // 2) + 16)
            sp.wait_ge(st_eout[1], 16 * (E // 2) + 16)
            sp.wait_ge(st_z, 16)

        @block.tensor
        def _(pe):
            pe.sem_inc(agg_mm, 1)
            pe.sem_inc(et_mm, 1)
            pe.sem_inc(q_mm, 1)
            pe.sem_inc(et2_mm, 1)
            pe.sem_inc(cx_mm, 1)
            pe.sem_inc(exd_mm, 1)
            pe.sem_inc(o_mm, 1)
            pe.sem_inc(f_q2T_mm, 1)
            pe.sem_inc(f_o_mm, 1)
            pe.sem_inc(prep_mm, 1)
            pe.wait_ge(ld_gat, 16 * 7)
            pe.wait_ge(abd_ready, 4)
            for k in range(KT):
                mm = pe.matmul(bank[0][0:CD, 0:16], w0T[:, k, :], abd[:, 0, k, :], start=k == 0, stop=k == 1)
            mm.then_inc(wa_mm, 1)
            for f in range(KT):
                for k in range(KT):
                    mm = pe.matmul(bank[1 + f][:, 0:16], w1T[:, k, f * P:(f + 1) * P], abd[:, 1, k, :],
                                   start=k == 0, stop=k == 1)
            mm.then_inc(wa_mm, 1)
            pe.wait_ge(wa_ready, 13)
            pe.wait_ge(ld_const, 16 * 4)

            def prep(p, k, j):
                l, bb = k // 2, k % 2
                nk = l + 1
                ft = [ctxb[:, bb, :]] if l == 0 else [hT[bb][:, 0, :], hT[bb][:, 1, :]]
                if j == 2:
                    pe.wait_ge(nb_split, p * 4 + (k + 1))
                elif j == 3:
                    pe.wait_ge(lnT_evac, p * 2 + 1)
                elif j % 2 == 0:
                    pe.wait_ge(prep_dve, p * 12 + (k * 3 + j // 4) + 1)
                else:
                    pe.wait_ge(prep_act, p * 12 + (k * 3 + j // 4) + 1)
                bk = bank[j % 4]
                if j < 2:
                    for t in range(TB):
                        for i in range(nk):
                            rhs, c = ((was[l][:, i, :], GH), ((w1 if l else w0)[:, i, :], D))[j]
                            mm = pe.matmul(bk[:, t * c:(t + 1) * c], ft[i][:, t * P:(t + 1) * P], rhs,
                                           start=i == 0, stop=i == nk - 1)
                else:
                    for h in (2 * j - 4, 2 * j - 3):
                        mm = pe.matmul(bk[:, (h % 2) * S:(h % 2 + 1) * S], pick[:, h, :], parts[:, :],
                                       start=True, stop=True)
                mm.then_inc(prep_mm, 1)

            def neighbour_rows(p, k):
                l, bb = k // 2, k % 2
                if l == 0:
                    pe.wait_ge(ctxb_ready, p * 2 + (bb + 1))
                else:
                    pe.wait_ge(h_ready, p * 4 + (k - 1))
                pe.wait_ge(sums_evac, p * 4 + max(k - 1, 0) + 1)
                pe.wait_ge(prep_dve, p * 12 + 3 * k + 1)
                ft = [ctxb[:, bb, :]] if l == 0 else [hT[bb][:, 0, :], hT[bb][:, 1, :]]
                for i in range(l + 1):
                    mm = pe.matmul(bank[2][0:NR, 0:S], wan[l][:, i, :], ft[i], start=i == 0, stop=i == l)
                mm.then_inc(nbrow_mm, 1)

            def head_transposes(p, i):
                n = p * 32 + i
                pe.wait_ge(exp_done, p * 64 + (2 * i + 2) + 1)
                pe.wait_ge(et_evac, p * 32 + max(i - 1, 0) + 1)
                for t in range(TB):
                    for m in range(TB):
                        c = m * S + t * P
                        mm = pe.transpose(bank[4 + i % 2][:, c:c + P], Ex[:, i % 2, t, m * P:(m + 1) * P], ident[:, :])
                mm.then_inc(et_mm, 1)

            def head_sum(p, i):
                k, h = i // GH, i % GH
                if h == 0:
                    pe.wait_ge(prep_act, p * 12 + (3 * k + 1) + 1)
                    pe.wait_ge(agg_read, p * 4 + max(k - 1, 0) + 1)
                pe.wait_ge(et_evac, p * 32 + (i + 1) + 1)
                j = h % 4
                for m in range(TB):
                    mm = pe.matmul(bank[6 + k % 2][32 * j:32 * j + 32, (h // 4) * S:(h // 4 + 1) * S],
                                   featS[:, k % 2, m, h * GO:(h + 1) * GO], ETs[:, i % 2, m, :],
                                   start=m == 0, stop=m == 1, tile_position=(0, 32 * j))
                mm.then_inc(agg_mm, 1)

            def spread_sums(p, k):
                pe.wait_ge(sums_ready, p * 4 + (k + 1))
                pe.wait_ge(sums_evac, p * 4 + k + 1)
                if k < 3:
                    pe.wait_ge(prep_dve, p * 12 + (3 * k + 5) + 1)
                for g in range(KT):
                    for t in range(TB):
                        c = g * S + t * P
                        mm = pe.transpose(bank[2][:, c:c + P],
                                          rX[:, t, 4 * g:4 * g + 4, :].rearrange("p h o -> p (h o)"), ident[:, :])
                mm.then_inc(sums_mm, 1)

            def to_rows(p, bb):
                pe.wait_ge(h_ready, p * 4 + (bb + 3))
                pe.wait_ge(lnT_evac, p * 2 + bb + 1)
                for t in range(TB):
                    for g in range(KT):
                        c = t * D + g * P
                        mm = pe.transpose(bank[3][:, c:c + P], hT[bb][:, g, t * P:(t + 1) * P], ident[:, :])
                mm.then_inc(rows_mm, 1)

            def ln_transposes(p, bb):
                pe.wait_ge(xln_ready, p * 4 + (2 * bb + 2))
                for k in range(KT):
                    for t in range(TB):
                        c = k * S + t * P
                        mm = pe.transpose(bank[3][:, c:c + P], xln[:, t, k * P:(k + 1) * P], ident[:, :])
                mm.then_inc(lnT_mm, 1)

            with pe.Fori(0, B // 2) as p:
                neighbour_rows(p, 0)
                for j in range(6):
                    prep(p, 0, j)
                for i in range(4 * GH + 1):
                    k, h = i // GH, i % GH
                    if i < 4 * GH:
                        head_transposes(p, i)
                    if i > 0:
                        head_sum(p, i - 1)
                        if h == 0:
                            spread_sums(p, k - 1)
                    if k < 3 and h >= 3:
                        if h == 3:
                            neighbour_rows(p, k + 1)
                            prep(p, k + 1, 0)
                        if h == 4:
                            prep(p, k + 1, 1)
                        if h == 5:
                            prep(p, k + 1, 2)
                        if h == 6:
                            prep(p, k + 1, 3)
                            prep(p, k + 1, 4)
                        if h == 7:
                            prep(p, k + 1, 5)
                    if k == 3 and h == 4:
                        to_rows(p, 0)
                    if i == 4 * GH:
                        ln_transposes(p, 0)
                to_rows(p, 1)
                ln_transposes(p, 1)

            pe.wait_ge(lnT_evac, B + 1)
            pe.wait_ge(ld_ffn0, 16 * 3)
            for c in range(2):
                for k in range(KT):
                    mm = pe.matmul(bank[6 + c][0:E, :], gwT[:, k, :], xlnT[:, k, c * 512:(c + 1) * 512],
                                   start=k == 0, stop=k == 1)
                mm.then_inc(logitT_mm, 1)
            for t in range(NT):
                pe.wait_ge(logitT_evac, t // 4 + 1)
                mm = pe.transpose(bank[5][:, t * E:(t + 1) * E], lgT[:, t * P:(t + 1) * P], ident[0:E, 0:E])
            mm.then_inc(logit_mm, 1)

            pe.wait_ge(ld_attn, 16 * 6)
            for j in range(AJ):
                for h in (2 * j, 2 * j + 1):
                    mm = pe.matmul(bank[j // 2][h % 2 * CD:(h % 2 + 1) * CD, j % 2 * AQ:(j % 2 + 1) * AQ],
                                   krT[:, h, :], qrT[:, h, :], start=True, stop=True, tile_position=(0, h % 2 * CD))
                if j % 2 == 1:
                    mm.then_inc(cT_mm, 1)

            pe.wait_ge(sel_ready, 1)
            mm = pe.matmul(bank[6][:, 0:P], upper[:, :], selb[:, :, :].rearrange("p t e -> p (t e)"),
                           start=True, stop=True)
            for k in range(1, NT):
                mm = pe.matmul(bank[6][:, k * E:P], onesb[:, :], selb[:, 0:NT - k, :].rearrange("p t e -> p (t e)"),
                               start=False, stop=True, skip_group_check=True)
            mm.then_inc(rank_mm, 1)

            for q in range(4):
                pe.wait_ge(cT_evac, q + 1)
                for j in (2 * q, 2 * q + 1):
                    for t in range(2):
                        c = (j % 2 * 2 + t) * P
                        mm = pe.transpose(bank[(4, 5, 0, 1)[q]][0:96, c:c + P], cT[:, j, t * 96:(t + 1) * 96],
                                          ident[:, :])
                mm.then_inc(c_mm, 1)
            for q in range(2):
                pe.wait_ge(cT_evac, 4)
                pe.wait_ge(c_evac, 2 * q + 2)
                for j in range(4 * q, 4 * q + 4):
                    for h in (2 * j, 2 * j + 1):
                        for t in range(2):
                            mm = pe.matmul(bank[2 + q][h % 2 * CD:(h % 2 + 1) * CD, j % 4 * P:(j % 4 + 1) * P],
                                           cQ[:, j, t, h % 2 * CD:(h % 2 + 1) * CD], kcqT[:, t, h * AK:(h + 1) * AK],
                                           start=t == 0, stop=t == 1, tile_position=(0, h % 2 * CD))
                mm.then_inc(dT_mm, 1)
            for q in range(2):
                pe.wait_ge(dT_evac, q + 1)
                for j in range(4 * q, 4 * q + 4):
                    mm = pe.transpose(bank[4 + q][:, j % 4 * P:(j % 4 + 1) * P], dT[:, j, :], ident[:, :])
                mm.then_inc(d_mm, 1)
            for q in range(4):
                pe.wait_ge(c_evac, 4)
                pe.wait_ge(d_evac, q // 2 + 1)
                for h in range(4 * q, 4 * q + 4):
                    mm = pe.matmul(bank[q][h % 2 * CD:(h % 2 + 1) * CD, h % 4 // 2 * D:(h % 4 // 2 + 1) * D],
                                   dK[:, h // 2, h % 2 * CD:(h % 2 + 1) * CD], wq[:, h, :], start=True, stop=True,
                                   tile_position=(0, h % 2 * CD))
                mm.then_inc(nT_mm, 1)
            for q in range(4):
                pe.wait_ge(d_evac, 2)
                pe.wait_ge(p_evac, max(q - 1, 0))
                for h in range(4 * q, 4 * q + 4):
                    mm = pe.matmul(bank[4 + q % 2][h % 2 * CD:(h % 2 + 1) * CD, h % 4 // 2 * D:(h % 4 // 2 + 1) * D],
                                   kckv[:, h, :], wo[:, h, :], start=True, stop=True,
                                   tile_position=(0, h % 2 * CD))
                mm.then_inc(p_mm, 1)
            for q in range(4):
                pe.wait_ge(nT_evac, q + 1)
                for j in (2 * q, 2 * q + 1):
                    for t in range(2):
                        c = (j % 2 * 2 + t) * P
                        mm = pe.transpose(bank[q][:, c:c + P], nT[:, j, t * P:(t + 1) * P], ident[:, :])
                mm.then_inc(n_mm, 1)

            pe.wait_ge(n_evac, 4)
            pe.wait_ge(p_evac, 4)
            n = 0
            for g in range(4):
                pe.wait_ge(disp_ready, (g + 1) * NT)
                for k in range(KT):
                    pe.wait_ge(disp_evac, max(n - 1, 0))
                    for t in range(NT):
                        for i, part in enumerate((xhi, xlo)):
                            mm = pe.matmul(bank[n % 2][:, :], part[:, t, k * P:(k + 1) * P],
                                           disp[:, t, 4 * g:4 * g + 4, :].rearrange("p e s -> p (e s)"),
                                           start=t == 0 and i == 0, stop=t == NT - 1 and i == 1)
                    mm.then_inc(disp_mm, 1)
                    n += 1
            pe.wait_ge(disp_evac, 8)

            with pe.Fori(0, E // NW) as i:
                for f in range(NW + 1):
                    if f < NW:
                        g = f % 2
                        pe.wait_ge(ld_we[f], i * 48 + 48)
                        pe.wait_ge(exm_ready, i * NW + max(f, 1))
                        for wt, bk in ((wg, 0), (wu, 2)):
                            for j in range(2):
                                for k in range(KT):
                                    mm = pe.matmul(bank[bk + g][0:IH, j * CAP:(j + 1) * CAP],
                                                   wt[:, f, k, j * IH:(j + 1) * IH],
                                                   xgT[:, k, bass.ds(i * (NW * CAP) + f * CAP, CAP)],
                                                   start=k == 0, stop=k == 1)
                        mm.then_inc(exg_mm, 1)
                    if f > 0:
                        g = (f - 1) % 2
                        pe.wait_ge(exm_ready, i * NW + f + 1)
                        pe.wait_ge(exo_ready, i * NW + max(f - 1, 1))
                        for j in range(2):
                            mm = pe.matmul(bank[4 + g][:, 0:D], emid[:, g, j, :], wd[:, f - 1, j, :],
                                           start=j == 0, stop=j == 1)
                        mm.then_inc(exd_mm, 1)

            def att_ln_transposes(b):
                pe.wait_ge(l2_xln, b * 2 + 2)
                pe.wait_ge(q_evac, b * 8 + 1)
                for k in range(KT):
                    for t in range(TB):
                        c = k * S + t * P
                        mm = pe.transpose(bank[6][:, c:c + P], xln[:, t, k * P:(k + 1) * P], ident[:, :])
                mm.then_inc(l2_T_mm, 1)

            def att_queries(b, j, first=False):
                pe.wait_ge(l2_T_evac, b + 1)
                pe.wait_ge(q_evac, b * 8 + max(j, 1))
                if j % 2 == 1 and not first:
                    pe.wait_ge(x3_ready, b)
                for k in range(KT):
                    mm = pe.matmul(bank[6 + j % 2][:, 0:S], Nw[:, k, j * P:(j + 1) * P], xT3[:, k, :],
                                   start=k == 0, stop=k == 1)
                mm.then_inc(q_mm, 1)

            def att_back_transposes(b, j):
                pe.wait_ge(en2_ready, b * 32 + (4 * j + 4) + 1)
                for h in range(2):
                    if h == 0:
                        pe.wait_ge(et2_act, b * 8 + j + 1)
                    else:
                        pe.wait_ge(et2_dve, b * 8 + j + 1)
                    for t in range(TB):
                        for m in range(TB):
                            c = m * S + t * P
                            mm = pe.transpose(bank[2 + h][:, c:c + P], E2[:, j % 2, t, h, m * P:(m + 1) * P],
                                              ident[:, :])
                    mm.then_inc(et2_mm, 1)

            def att_scores(b, j, first=False):
                pe.wait_ge(q_evac, b * 8 + (j + 1) + 1)
                for t in range(TB):
                    if not first:
                        pe.wait_ge(ex2_ready, b * 32 + (4 * j + 2 * t - 1))
                    mm = pe.matmul(bank[t][:, :], qT[:, j, t * P:(t + 1) * P],
                                   kblk[:, bass.ds(b, 1), :, :].rearrange("p b h s -> p (b h s)"),
                                   start=True, stop=True)
                    mm.then_inc(sc_mm, 1)

            def att_context(b, j):
                pe.wait_ge(cx_evac, b * 8 + max(j, 1))
                pe.wait_ge(kvb_ready, b + 1)
                pe.wait_ge(et2_act, b * 8 + (j + 1) + 1)
                pe.wait_ge(et2_dve, b * 8 + (j + 1) + 1)
                for h in range(2):
                    for m in range(TB):
                        mm = pe.matmul(bank[4 + j % 2][h * CD:(h + 1) * CD, 0:S], kvb[:, m, :],
                                       ET2[:, j % 2, h, m, :], start=m == 0, stop=m == 1,
                                       tile_position=(0, h * CD))
                mm.then_inc(cx_mm, 1)

            def att_output(b, last=False):
                pe.wait_ge(cx_evac, b * 8 + 8 + 1)
                pe.wait_ge(q_evac, b * 8 + (8 if last else 16) + 1)
                for t in range(TB):
                    for j in range(AH // 2):
                        mm = pe.matmul(bank[7][:, t * D:(t + 1) * D], cxT[:, j, t * P:(t + 1) * P], Pw[:, j, :],
                                       start=j == 0, stop=j == AH // 2 - 1)
                mm.then_inc(o_mm, 1)

            def kv_transposes(b):
                pe.wait_ge(kvT_ready, 2 * b)
                for t in range(TB):
                    mm = pe.transpose(bank[6][:, t * P:(t + 1) * P],
                                      kvr[:, b * TB + t, :, :].rearrange("p a c -> p (a c)"), ident[:, :])
                mm.then_inc(kvT_mm, 1)

            pe.wait_ge(kvr_ready, 1)
            pe.wait_ge(ld_sh, 32)
            pe.wait_ge(exm_ready, E + 1)
            pe.wait_ge(exo_ready, E + 1)
            n = 0
            for c in range(2):
                for i in range(3):
                    m = min(P, IS - i * P)
                    pe.wait_ge(shm_ready, max(n - 1, 0))
                    for wt, bk in ((swg, 0), (swu, 2)):
                        for k in range(KT):
                            mm = pe.matmul(bank[bk + n % 2][0:m, :], wt[:, k, i * P:i * P + m],
                                           xlnT[:, k, c * 512:(c + 1) * 512], start=k == 0, stop=k == 1)
                    mm.then_inc(shg_mm, 1)
                    if n < B:
                        kv_transposes(n)
                    n += 1
                if c == 1:
                    pe.wait_ge(kvT_ready, 2 * B)
                    att_ln_transposes(0)
                pe.wait_ge(shm_ready, n)
                for t in range(4):
                    pe.wait_ge(shd_add, max(c * 4 + t - 1, 0))
                    for i in range(3):
                        m = min(P, IS - i * P)
                        mm = pe.matmul(bank[4 + t % 2][:, 0:D], smid[0:m, i, t * P:(t + 1) * P], swd[0:m, i, :],
                                       start=i == 0, stop=i == 2)
                    mm.then_inc(shd_mm, 1)
                    if c == 1:
                        att_queries(0, 2 * t, first=True)
                        att_queries(0, 2 * t + 1, first=True)
            pe.wait_ge(shd_add, NT)

            trs = bank[6][:, :].bitcast(BF16)

            def ff_in_transposes(n, g, first=False):
                pe.wait_ge(f_q1, n + 1)
                if not first:
                    pe.wait_ge(f_q1T, n)
                    pe.wait_ge(f_q2T, n - 1)
                for k in range(KT):
                    mm = pe.transpose(trs[:, k * P:(k + 1) * P], q1[:, g, k * P:(k + 1) * P], identh[:, :])
                mm.then_inc(f_q1T_mm, 1)

            def ff_in(n, g):
                pe.wait_ge(f_q1T, n + 1)
                pe.wait_ge(f_g_ready, max(n, 1) if isinstance(n, int) else n)
                for u in range(2):
                    for lo, w, bk, c in ((0, 512, u, 0), (512, HID - 512, 2, u * (HID - 512))):
                        i = 0
                        for part in range(3):
                            for k in range(KT):
                                mm = pe.matmul(bank[3 * g + bk][:, c:c + w], q1T[:, g, k * P:(k + 1) * P],
                                               w13p[:, part, k, u * HID + lo:u * HID + lo + w],
                                               start=i == 0, stop=i == 5)
                                i += 1
                mm.then_inc(f_a_mm, 1)

            def ff_back_transposes(n, g):
                pe.wait_ge(f_q2, n + 1 + 1)
                pe.wait_ge(f_q1T, min(n + 3, NT) if isinstance(n, int) else n + 3)
                for k in range(6):
                    m = min(P, HID - k * P)
                    mm = pe.transpose(trs[0:m, k * P:(k + 1) * P], q2[:, g, k * P:k * P + m], identh[:, :])
                mm.then_inc(f_q2T_mm, 1)

            def ff_out(n, g):
                pe.wait_ge(f_q2T, n + 1 + 1)
                pe.wait_ge(f_out, n + 1)
                for k in range(6):
                    m = min(P, HID - k * P)
                    for part in range(3):
                        mm = pe.matmul(bank[7][:, 0:D], q2T[0:m, g, k * P:(k + 1) * P], w2p[0:m, part, k, :],
                                       start=k == 0 and part == 0, stop=k == 5 and part == 2)
                mm.then_inc(f_o_mm, 1)

            att_scores(0, 0, first=True)
            att_scores(0, 1)
            with pe.Fori(0, B - 1) as b:
                for j in range(2, AH // 2):
                    att_back_transposes(b, j - 2)
                    att_scores(b, j)
                    att_context(b, j - 2)
                    if j == 3:
                        att_ln_transposes(b + 1)
                    if j >= 4:
                        att_queries(b + 1, 2 * j - 8)
                        att_queries(b + 1, 2 * j - 7)
                for j in range(2):
                    att_back_transposes(b, j + 6)
                    att_scores(b + 1, j)
                    att_context(b, j + 6)
                att_output(b)
            for j in range(2, AH // 2 + 2):
                att_back_transposes(B - 1, j - 2)
                if j < AH // 2:
                    att_scores(B - 1, j)
                att_context(B - 1, j - 2)
                if j == 5:
                    ff_in_transposes(0, 0, first=True)
                if j == 7:
                    pe.wait_ge(f_q1T, 1)
                    ff_in_transposes(1, 1, first=True)
            pe.wait_ge(wsplit_ready, 1)
            pe.wait_ge(w13_part, 3)
            ff_in(0, 0)
            att_output(B - 1, last=True)
            ff_in(1, 1)
            ff_in_transposes(2, 0)
            ff_back_transposes(0, 0)
            ff_in(2, 0)
            ff_in_transposes(3, 1)
            pe.wait_ge(x3_ready, B + 1)
            ff_out(0, 0)
            with pe.Fori(1, B - 1) as b:
                for t in range(TB):
                    ff_back_transposes(b * TB + (t - 1), 1 - t)
                    ff_in(b * TB + (t + 1), 1 - t)
                    ff_out(b * TB + (t - 1), 1 - t)
                    ff_in_transposes(b * TB + (t + 2), t)
            ff_back_transposes(NT - 3, 1)
            ff_in(NT - 1, 1)
            ff_out(NT - 3, 1)
            ff_back_transposes(NT - 2, 0)
            ff_out(NT - 2, 0)
            ff_back_transposes(NT - 1, 1)
            ff_out(NT - 1, 1)

        @block.scalar
        def _(act):
            act.sem_inc(prep_act, 1)
            act.sem_inc(sums_evac, 1)
            act.sem_inc(elu_exp, 1)
            act.sem_inc(et_evac, 1)
            act.sem_inc(lnT_evac, 1)
            act.sem_inc(exo_ready, 1)
            act.sem_inc(q_evac, 1)
            act.sem_inc(ex2_ready, 1)
            act.sem_inc(et2_act, 1)
            act.sem_inc(exp_done, 1)
            act.sem_inc(f_q2, 1)
            act.sem_inc(f_q2T, 1)

            def prep_copy(p, k, j):
                act.wait_ge(prep_mm, p * 24 + (6 * k + j + 1) + 1)
                if j == 1:
                    act.wait_ge(agg_mm, p * 32 + max(8 * (k - 1), 0) + 1)
                    dst = featS[:, k % 2, :, :].rearrange("p t d -> p (t d)")
                else:
                    act.wait_ge(leak_done, p * 64 + max(16 * (k - 1), 0) + 1)
                    dst = NB[:, k % 2, 2 * j - 4:2 * j - 2, :].rearrange("p h s -> p (h s)")
                act.activation(dst, bank[j % 4][:, :], ACT.Copy).then_inc(prep_act, 1)

            with act.Fori(0, B // 2) as p:
                act.wait_ge(ld_ctxT, 16)
                act.wait_ge(prep_mm, p * 24 + 1)
                for bb in range(2):
                    act.activation(ctxb[:, bb, :], ctxT[:, bass.ds(p * (2 * S) + bb * S, S)],
                                   ACT.Copy).then_inc(ctxb_ready, 1)
                for j in (1, 3):
                    prep_copy(p, 0, j)
                for i in range(4 * GH + 1):
                    k, h = i // GH, i % GH
                    if i < 4 * GH:
                        act.wait_ge(et_mm, p * 32 + max(i - 1, 0) + 1)
                        for t in range(TB):
                            act.wait_ge(e_ready, p * 64 + (2 * i + t + 1))
                            act.activation(Ex[:, i % 2, t, :], L[:, i % 2, t, :], ACT.Exp,
                                           bias=M[:, i % 2, t:t + 1], scale=-1.0,
                                           accum_out=Sm[:, k % 2, t, h:h + 1]).then_inc(exp_done, 1)
                    if i > 0:
                        act.wait_ge(et_mm, p * 32 + i + 1)
                        act.wait_ge(agg_mm, p * 32 + max(i - 2, 0) + 1)
                        act.activation(ETs[:, (i - 1) % 2, :, :].rearrange("p t s -> p (t s)"),
                                       bank[4 + (i - 1) % 2][:, :], ACT.Copy).then_inc(et_evac, 1)
                    if h == 0 and i > 0:
                        act.wait_ge(sums_mm, p * 4 + k)
                        act.wait_ge(agg_read, p * 4 + (k - 1) + 1)
                        act.activation(rT[:, :, :].rearrange("p g s -> p (g s)"), bank[2][:, :],
                                       ACT.Copy).then_inc(sums_evac, 1)
                    if (h == 2 and i > 2) or i == 4 * GH:
                        n = k - 1
                        act.wait_ge(elu_ready, p * 4 + (n + 1))
                        act.activation(y0[:, :, :], y0[:, :, :], ACT.Exp).then_inc(elu_exp, 1)
                    if k < 4 and h == 1:
                        prep_copy(p, k, 5)
                    if k < 3 and h in (5, 7):
                        prep_copy(p, k + 1, h - 4)
                    if i == 4 * GH:
                        act.wait_ge(lnT_mm, p * 2 + 1)
                        act.activation(xlnT[:, :, bass.ds(p * (2 * S), S)],
                                       bank[3][:, :].rearrange("p (k s) -> p k s", k=KT),
                                       ACT.Copy).then_inc(lnT_evac, 1)
                act.wait_ge(lnT_mm, p * 2 + 2)
                act.activation(xlnT[:, :, bass.ds(p * (2 * S) + S, S)],
                               bank[3][:, :].rearrange("p (k s) -> p k s", k=KT), ACT.Copy).then_inc(lnT_evac, 1)

            for c in range(2):
                act.wait_ge(logitT_mm, c + 1)
                act.activation(lgT[:, c * 512:(c + 1) * 512], bank[6 + c][0:E, :], ACT.Copy).then_inc(logitT_evac, 1)
            act.wait_ge(route_exp_in, 1)
            act.activation(prob[:, :, :], prob[:, :, :], ACT.Exp).then_inc(route_exp, 1)

            for q in range(4):
                act.wait_ge(cT_mm, q + 1)
                act.activation(cT[:, 2 * q:2 * q + 2, :].rearrange("p j q -> p (j q)"), bank[q][:, 0:2 * AQ],
                               ACT.Copy).then_inc(cT_evac, 1)
            for q in range(4):
                act.wait_ge(c_mm, q + 1)
                act.activation(cQ[:, 2 * q:2 * q + 2, :, :].rearrange("p j t c -> p (j t c)"),
                               bank[(4, 5, 0, 1)[q]][0:96, :], ACT.Copy).then_inc(c_evac, 1)
            for q in range(2):
                act.wait_ge(dT_mm, q + 1)
                act.activation(dT[:, 4 * q:4 * q + 4, :].rearrange("p j k -> p (j k)"), bank[2 + q][:, :],
                               ACT.Copy).then_inc(dT_evac, 1)
            for q in range(2):
                act.wait_ge(d_mm, q + 1)
                act.activation(dK[:, 4 * q:4 * q + 4, :].rearrange("p j c -> p (j c)"), bank[4 + q][:, :],
                               ACT.Copy).then_inc(d_evac, 1)
            for q in range(4):
                act.wait_ge(nT_mm, q + 1)
                act.activation(nT[:, 2 * q:2 * q + 2, :].rearrange("p j d -> p (j d)"), bank[q][:, :],
                               ACT.Copy).then_inc(nT_evac, 1)
            act.wait_ge(kvr_ready, 1)
            for q in range(4):
                act.wait_ge(p_mm, q + 1)
                act.activation(Pw[:, 2 * q:2 * q + 2, :].rearrange("p j d -> p (j d)"), bank[4 + q % 2][:, :],
                               ACT.Copy).then_inc(p_evac, 1)
            for q in range(4):
                act.wait_ge(n_mm, q + 1)
                src = bank[q][:, :].rearrange("p (j t c) -> p t j c", j=2, t=2)
                dst = Nw[:, :, q * 4 * CD:(q + 1) * 4 * CD].rearrange("p t (j c) -> p t j c", j=2)
                act.activation(dst, src, ACT.Copy).then_inc(n_evac, 1)

            for n in range(0, 8, 2):
                act.wait_ge(disp_mm, n + 1)
                act.activation(xgT[:, 0, n // 2 * 512:(n // 2 + 1) * 512], bank[n % 2][:, :],
                               ACT.Copy).then_inc(disp_evac, 1)
                act.wait_ge(disp_mm, n + 2)
                act.activation(xgT[:, 1, n // 2 * 512:(n // 2 + 1) * 512], bank[1][:, :],
                               ACT.Copy).then_inc(disp_evac, 1)
            with act.Fori(0, E // NW) as i:
                for f in range(NW + 1):
                    if f < NW:
                        act.wait_ge(exg_mm, i * NW + (f + 1))
                        act.wait_ge(exm_ready, i * NW + max(f, 1))
                        act.activation(esg[:, f % 2, :], bank[f % 2][0:IH, 0:2 * CAP],
                                       ACT.Silu).then_inc(exs_ready, 1)
                    if f > 0:
                        act.wait_ge(exd_mm, i * NW + f + 1)
                        act.wait_ge(st_eout[(f - 1) % 2], i * (NW * 8) + (f - 1) // 2 * 16 + 16)
                        act.activation(eoS[:, (f - 1) % 2, :], bank[4 + (f - 1) % 2][:, 0:D],
                                       ACT.Copy).then_inc(exo_ready, 1)

            def att_ln_evac(b):
                act.wait_ge(l2_T_mm, b + 1)
                act.wait_ge(q_mm, b * 8 + 1)
                act.activation(xT3[:, :, :].rearrange("p k s -> p (k s)"), bank[6][:, :],
                               ACT.Copy).then_inc(l2_T_evac, 1)

            def att_query_evac(b, j, first=False):
                act.wait_ge(q_mm, b * 8 + (j + 1) + 1)
                if not first:
                    act.wait_ge(sc_mm, b * 16 + (2 * j + 2 - 16))
                act.activation(qT[:, j, :], bank[6 + j % 2][:, 0:S], ACT.Copy).then_inc(q_evac, 1)

            def att_back_evac(b, j):
                act.wait_ge(et2_mm, b * 16 + (2 * j + 1) + 1)
                act.wait_ge(cx_mm, b * 8 + max(j, 1))
                act.activation(ET2[:, j % 2, 0, :, :].rearrange("p t s -> p (t s)"), bank[2][:, :],
                               ACT.Copy).then_inc(et2_act, 1)

            def att_exp(b, j, first=False):
                if not first:
                    act.wait_ge(et2_mm, b * 16 + (2 * j - 2) + 1)
                    act.wait_ge(ri2_ready, b * 8 + j)
                for t in range(TB):
                    act.wait_ge(mx_ready, b * 16 + (2 * j + t + 1))
                    for h in range(2):
                        act.activation(E2[:, j % 2, t, h, :], bank[t][:, h * S:(h + 1) * S], ACT.Exp,
                                       bias=nmx[:, j % 2, t, h:h + 1],
                                       accum_out=S2[:, j % 2, t, h:h + 1]).then_inc(ex2_ready, 1)

            trs = bank[6][:, :].bitcast(BF16)

            def ff_in_evac(n, g, first=False):
                act.wait_ge(f_q1T_mm, n + 1)
                if not first:
                    act.wait_ge(f_a_mm, n - 1)
                act.activation(q1T[:, g, :], trs[:, 0:KT * P], ACT.Copy).then_inc(f_q1T, 1)

            def ff_relu(n, g, first=False):
                if not first:
                    act.wait_ge(f_sq_ready, n)
                act.wait_ge(f_a_mm, n + 1)
                act.wait_ge(f_g_ready, n + 1)
                for lo, w, bk in ((0, 512, 0), (512, HID - 512, 2)):
                    act.activation(r1[:, lo:lo + w], bank[3 * g + bk][:, 0:w], ACT.Relu,
                                   scale=is1[:, g:g + 1]).then_inc(f_relu, 1)
                act.wait_ge(f_relu, n * 2 + 2)
                act.activation(r2[:, :], r1[:, :], ACT.Square).then_inc(f_r_ready, 1)

            def ff_square(n):
                act.wait_ge(f_g_ready, n + 1 + 1)
                act.activation(r1[:, :], gated[:, :], ACT.Square, accum_out=ms[:, :]).then_inc(f_sq_ready, 1)

            def ff_integers(n, g):
                act.wait_ge(f_t2, n + 1)
                act.activation(q2[:, g, :], tmp2[:, :], ACT.Identity, bias=unround[:, :]).then_inc(f_q2, 1)

            def ff_back_evac(n, g):
                act.wait_ge(f_q2T_mm, n + 1 + 1)
                act.activation(q2T[:, g, 0:5 * P], trs[:, 0:5 * P], ACT.Copy).then_inc(act_step, 1)
                act.activation(q2T[0:HID - 5 * P, g, 5 * P:6 * P], trs[0:HID - 5 * P, 5 * P:6 * P],
                               ACT.Copy).then_inc(f_q2T, 1)

            act.wait_ge(zero_ready, 4)
            n = 0
            for c in range(2):
                for i in range(3):
                    m = min(P, IS - i * P)
                    act.wait_ge(shg_mm, n + 1)
                    act.wait_ge(shm_ready, n)
                    act.activation(sgs[0:m, :], bank[n % 2][0:m, :], ACT.Silu).then_inc(shs_ready, 1)
                    if n < B:
                        act.wait_ge(kvT_mm, n + 1)
                        for h in range(2):
                            act.activation(kblk[h * CD:(h + 1) * CD, n, h, :], bank[6][h * CD:(h + 1) * CD, 0:S],
                                           ACT.Copy).then_inc(kvT_ready, 1)
                    n += 1
            att_ln_evac(0)
            for j in range(AH // 2):
                att_query_evac(0, j, first=True)

            att_exp(0, 0, first=True)
            att_exp(0, 1, first=True)
            act.wait_ge(combined, 1)
            with act.Fori(0, B - 1) as b:
                for j in range(2, AH // 2):
                    att_back_evac(b, j - 2)
                    att_exp(b, j)
                    if j == 3:
                        att_ln_evac(b + 1)
                    if j >= 4:
                        att_query_evac(b + 1, 2 * j - 8)
                        att_query_evac(b + 1, 2 * j - 7)
                for j in range(2):
                    att_back_evac(b, j + 6)
                    att_exp(b + 1, j)
            for j in range(2, AH // 2 + 2):
                att_back_evac(B - 1, j - 2)
                if j < AH // 2:
                    att_exp(B - 1, j)
                if j == 5:
                    ff_in_evac(0, 0, first=True)
                if j == 7:
                    ff_in_evac(1, 1, first=True)

            ff_relu(0, 0, first=True)
            ff_square(0)
            ff_relu(1, 1)
            ff_in_evac(2, 0)
            ff_integers(0, 0)
            ff_square(1)
            ff_back_evac(0, 0)
            ff_relu(2, 0)
            ff_in_evac(3, 1)
            ff_integers(1, 1)
            with act.Fori(1, B - 1) as b:
                for t in range(TB):
                    n = b * TB + t
                    ff_square(n)
                    ff_back_evac(b * TB + (t - 1), 1 - t)
                    ff_relu(b * TB + (t + 1), 1 - t)
                    ff_in_evac(b * TB + (t + 2), t)
                    ff_integers(n, t)
            ff_square(NT - 2)
            ff_back_evac(NT - 3, 1)
            ff_relu(NT - 1, 1)
            ff_integers(NT - 2, 0)
            ff_square(NT - 1)
            ff_back_evac(NT - 2, 0)
            ff_integers(NT - 1, 1)
            ff_back_evac(NT - 1, 1)

        @block.vector
        def _(dve):
            dve.sem_inc(prep_dve, 1)
            dve.sem_inc(agg_read, 1)
            dve.sem_inc(x1_ready, 1)
            dve.sem_inc(x3_ready, 1)
            dve.sem_inc(et2_dve, 1)
            dve.sem_inc(exm_ready, 1)
            dve.sem_inc(cx_evac, 1)
            dve.sem_inc(f_g_ready, 1)
            dve.sem_inc(f_out, 1)
            dve.sem_inc(leak_done, 1)
            dve.sem_inc(ri2_ready, 1)
            steps = [0]

            def link(ins, base=0, alone=False):
                steps[0] += 1
                ins.then_inc(dve_step, 1)
                count = base + steps[0]
                if alone:
                    count = dve.to_reg(count)
                    dve.wait_ge(consts_ready, 1)
                dve.wait_ge(dve_step, count)

            def row(b, t):
                return X[:, bass.ds(b * TB + t, 1), :].rearrange("p o d -> p (o d)")

            def layernorm_stats(b, base, veps_sem, keep_at=None):
                stats, var = (mv[:, :, :], veps[:, :]) if keep_at is None else (
                    fstat[:, keep_at, 0:4].rearrange("p (t c) -> p t c", t=TB), fveps[:, keep_at, :])
                for t in range(TB):
                    link(dve.bn_stats(bnst[:, t, :], row(b, t)), base, True)
                link(dve.bn_aggr(stats[:, 0, :], bnst[:, 0, :]), base, True)
                link(dve.bn_aggr(stats[:, 1, :], bnst[:, 1, :]), base)
                dve.tensor_scalar(var, stats[:, :, 1], LN_EPS, None, ALU.add).then_inc(veps_sem, 1)

            def layernorm_apply(b, base, rstd_sem, count, dst, signal=None):
                dve.wait_ge(rstd_sem, count)
                for t in range(TB):
                    ins = dve.tensor_scalar(dst[:, t, :], row(b, t), mv[:, t, 0:1], rstd[:, t:t + 1],
                                            ALU.subtract, ALU.mult)
                    if signal is None:
                        link(ins, base)
                    else:
                        ins.then_inc(signal, 1)

            def layernorm(b, base, veps_sem, rstd_sem, count, dst):
                layernorm_stats(b, base, veps_sem)
                layernorm_apply(b, base, rstd_sem, count, dst)

            dve.memset(unround[:, :], -ROUND).then_inc(big_ready, 1)
            dve.memset(half[:, :], -0.5).then_inc(consts_ready, 1)
            dve.memset(zrow[:, :], 0.0).then_inc(zero_ready, 1)
            for w in wan:
                dve.memset(w[:, :, :], 0.0).then_inc(zero_ready, 1)
            dve.memset(onesb[:, :], 1.0).then_inc(big_ready, 1)
            dve.memset(Lp[:, :, E:E + TOPK], BIG).then_inc(big_ready, 1)
            dve.wait_ge(ld_gat, 16 * 7)
            for l in range(2):
                for i in range(2):
                    dve.tensor_tensor(abd[:, l, :, i * GH:(i + 1) * GH], blockmask[:, :, :],
                                      acol[:, l, i, :].unsqueeze(2).to_broadcast([P, KT, GH]),
                                      ALU.mult).then_inc(abd_ready, 1)
            dve.tensor_copy(pick[:, :, :], pickf[:, :].unsqueeze(2).to_broadcast([NR, GH, P])).then_inc(wa_ready, 1)
            dve.wait_ge(zero_ready, 3)
            dve.wait_ge(wa_mm, 1)
            dve.tensor_copy(was[0][:, 0, :], bank[0][0:CD, 0:GH]).then_inc(wa_ready, 1)
            for r in ROWS:
                dve.tensor_copy(wan[0][:, 0, r:r + GH], bank[0][0:CD, GH:2 * GH]).then_inc(wa_ready, 1)
            dve.wait_ge(wa_mm, 2)
            for f in range(KT):
                dve.tensor_copy(was[1][:, f, :], bank[1 + f][:, 0:GH]).then_inc(wa_ready, 1)
                for r in ROWS:
                    dve.tensor_copy(wan[1][:, f, r:r + GH], bank[1 + f][:, GH:2 * GH]).then_inc(wa_ready, 1)

            dve.wait_ge(ld_const, 16 * 4)
            dve.tensor_copy(identh[:, :], ident[:, :]).then_inc(big_ready, 1)
            dve.tensor_copy(upper[:, :], upperf[:, :]).then_inc(big_ready, 1)
            dve.tensor_copy(iotah[:, :], iotaf[:, :]).then_inc(big_ready, 1)

            dve.wait_ge(ld_x, 16)
            GAT_STEPS = 62

            def prep_copy(p, k, j):
                dve.wait_ge(prep_mm, p * 24 + (6 * k + j + 1) + 1)
                if j == 0:
                    selfp = bank[0][:, 0:TB * GH].rearrange("p (t h) -> p t h", t=TB)
                    link(dve.tensor_copy(selfS[:, k % 2, :, :], selfp), p * GAT_STEPS)
                    dve.tensor_scalar(self02[:, k % 2, :, :], selfp, 0.2, None, ALU.mult).then_inc(prep_dve, 1)
                else:
                    dve.tensor_copy(NB[:, k % 2, 2 * j - 4:2 * j - 2, :].rearrange("p h s -> p (h s)"),
                                    bank[j % 4][:, :]).then_inc(prep_dve, 1)

            def split_rows(p, k):
                dve.wait_ge(nbrow_mm, p * 4 + (k + 1))
                dve.wait_ge(prep_mm, p * 24 + 6 * k + 1)
                link(dve.tensor_copy(parts[:, :], bank[2][0:NR, 0:S]), p * GAT_STEPS)
                link(dve.tensor_tensor(rest[64:NR, :], bank[2][64:NR, 0:S], parts[64:NR, :], ALU.subtract),
                     p * GAT_STEPS)
                link(dve.tensor_copy(parts[64:NR, :], rest[64:NR, :]), p * GAT_STEPS)
                link(dve.tensor_tensor(rest[96:NR, :], rest[96:NR, :], parts[96:NR, :], ALU.subtract), p * GAT_STEPS)
                dve.tensor_copy(parts[96:NR, :], rest[96:NR, :]).then_inc(nb_split, 1)

            def elu_first(p, k):
                base = p * GAT_STEPS
                l = k // 2
                dve.wait_ge(sums_evac, p * 4 + (k + 1) + 1)
                dve.wait_ge(agg_mm, p * 32 + (8 * k + 8) + 1)
                dve.wait_ge(elu_exp, p * 4 + k + 1)
                dve.tensor_tensor(y0[:, :, :].rearrange("p g s -> p (g s)"), bank[6 + k % 2][:, :],
                                  rT[:, :, :].rearrange("p g s -> p (g s)"), ALU.mult).then_inc(agg_read, 1)
                dve.wait_ge(agg_read, p * 4 + (k + 1) + 1)
                for g in range(KT):
                    link(dve.tensor_scalar(r0[:, g, :], y0[:, g, :], bcol[:, l, g:g + 1], 0.0, ALU.add, ALU.max), base)
                link(dve.tensor_scalar(y0[:, 0, :], y0[:, 0, :], bcol[:, l, 0:1], 0.0, ALU.add, ALU.min), base)
                dve.tensor_scalar(y0[:, 1, :], y0[:, 1, :], bcol[:, l, 1:2], 0.0, ALU.add,
                                  ALU.min).then_inc(elu_ready, 1)

            def elu_last(p, k):
                dve.wait_ge(elu_exp, p * 4 + (k + 1) + 1)
                dve.scalar_tensor_tensor(hT[k % 2][:, :, :], y0[:, :, :], -1.0, r0[:, :, :], ALU.add,
                                         ALU.add).then_inc(h_ready, 1)

            def add_rows(p, bb):
                dve.wait_ge(rows_mm, p * 2 + (bb + 1))
                xb = X[:, bass.ds(p * (2 * TB) + bb * TB, TB), :].rearrange("p t d -> p (t d)")
                dve.tensor_tensor(xb, xb, bank[3][:, :], ALU.add).then_inc(x1_ready, 1)
                held = dve.to_reg(p * 2 + (bb + 1) + 1)
                dve.wait_ge(consts_ready, 1)
                dve.wait_ge(x1_ready, held)

            def keep_rows(p, bb):
                t0 = p * (2 * TB) + bb * TB
                xh = xhi[:, bass.ds(t0, TB), :]
                dve.wait_ge(xln_ready, p * 4 + (2 * bb + 2))
                link(dve.tensor_copy(xh, xln[:, :, :]), p * GAT_STEPS)
                link(dve.tensor_tensor(xlo[:, bass.ds(t0, TB), :], xln[:, :, :], xh, ALU.subtract), p * GAT_STEPS)

            def adjacency(p, bb):
                layernorm_apply(p * 2 + bb, p * GAT_STEPS, rstd_ready, p * 4 + (bb + 1), maskN[:, bb, :, :])
                link(dve.tensor_scalar(maskN[:, bb, :, :], maskN[:, bb, :, :], 1.0, -MASK, ALU.subtract,
                                       ALU.mult), p * GAT_STEPS)

            with dve.Fori(0, B // 2) as p:
                base = p * GAT_STEPS
                steps[0] = 0
                layernorm_stats(p * 2, base, veps_ready)
                split_rows(p, 0)
                prep_copy(p, 0, 0)
                prep_copy(p, 0, 2)
                adjacency(p, 0)
                for i in range(4 * GH + 1):
                    k, h = i // GH, i % GH
                    if i < 4 * GH:
                        if h in (0, 4):
                            dve.wait_ge(prep_dve, p * 12 + (3 * k + 2 + h // 4) + 1)
                        if h in (2, 6):
                            dve.wait_ge(prep_act, p * 12 + (3 * k + 2 + h // 4) + 1)
                        dve.wait_ge(u_ready, p * 64 + (2 * i + 2) + 1)
                        dve.wait_ge(exp_done, p * 64 + max(2 * i - 2, 0) + 1)
                        for t in range(TB):
                            dve.scalar_tensor_tensor(L[:, i % 2, t, :], NB[:, k % 2, h, :],
                                                     selfS[:, k % 2, t, h:h + 1], U[:, i % 4, t, :],
                                                     ALU.add, ALU.min).then_inc(leak_done, 1)
                        for t in range(TB):
                            held = dve.to_reg(p * 64 + (2 * i + t + 1) + 1)
                            dve.wait_ge(consts_ready, 1)
                            dve.wait_ge(leak_done, held)
                            dve.tensor_tensor_reduce(L[:, i % 2, t, :], L[:, i % 2, t, :], maskN[:, k % 2, t, :],
                                                     1.0, 3.4e38, ALU.add, ALU.min, M[:, i % 2, t:t + 1],
                                                     ).then_inc(e_ready, 1)
                    if h == 0 and i > 0:
                        dve.wait_ge(exp_done, p * 64 + 2 * i + 1)
                        link(dve.reciprocal(Ri[:, :, :], Sm[:, (k - 1) % 2, :, :]), base)
                        if k > 1:
                            dve.wait_ge(sums_mm, p * 4 + k - 1)
                        dve.tensor_copy(rX[:, :, :, :], Ri[:, :, :].unsqueeze(3).to_broadcast([P, TB, GH, GO]),
                                        ).then_inc(sums_ready, 1)
                    if (h == 2 and i > 2) or i == 4 * GH:
                        elu_first(p, k - 1)
                    if (h == 3 and i > 3) or i == 4 * GH:
                        elu_last(p, k - 1)
                    if k < 4 and h == 0:
                        prep_copy(p, k, 4)
                    if k < 3 and h == 5:
                        split_rows(p, k + 1)
                    if k < 3 and h in (5, 6):
                        prep_copy(p, k + 1, 2 * h - 10)
                    if i == 2:
                        layernorm_stats(p * 2 + 1, base, veps_ready)
                    if i == 4:
                        adjacency(p, 1)
                    if k == 3 and h == 6:
                        add_rows(p, 0)
                        layernorm_stats(p * 2, base, veps_ready)
                    if k == 3 and h == 7:
                        layernorm_apply(p * 2, base, rstd_ready, p * 4 + 3, xln, xln_ready)
                        keep_rows(p, 0)
                add_rows(p, 1)
                layernorm_stats(p * 2 + 1, base, veps_ready)
                dve.wait_ge(lnT_mm, p * 2 + 1)
                layernorm_apply(p * 2 + 1, base, rstd_ready, p * 4 + 4, xln, xln_ready)
                keep_rows(p, 1)
                assert steps[0] == GAT_STEPS, steps[0]
            dve.wait_ge(lnT_mm, B)
            base = (B // 2) * GAT_STEPS
            steps[0] = 0

            dve.wait_ge(big_ready, 6)
            dve.wait_ge(logit_mm, 1)
            link(dve.tensor_copy(Lp[:, :, 0:E], bank[5][:, 0:NT * E].rearrange("p (t e) -> p t e", t=NT)), base)
            for t in range(NT):
                link(dve.max(top8[:, t, :], Lp[:, t, :]), base)
            dve.tensor_tensor(prob[:, :, :], Lp[:, :, 0:E], top8[:, :, 4:5].to_broadcast([P, NT, E]),
                              ALU.subtract).then_inc(route_exp_in, 1)
            for t in range(NT):
                link(dve.match_replace(rep[:, t, :], top8[:, t, :], Lp[:, t, :], -BIG), base)
            link(dve.tensor_scalar(sel[:, :, :], rep[:, :, 0:E], -BIG, None, ALU.is_equal), base)
            dve.tensor_copy(selb[:, :, :], sel[:, :, :]).then_inc(sel_ready, 1)
            dve.wait_ge(route_exp, 1)
            link(dve.tensor_reduce(ssum[:, :], prob[:, :, :], AX_X, ALU.add), base)
            link(dve.reciprocal(srec[:, :], ssum[:, :]), base)
            link(dve.tensor_tensor(prob[:, :, :], prob[:, :, :], srec[:, :].unsqueeze(2).to_broadcast([P, NT, E]),
                                   ALU.mult), base)
            link(dve.tensor_tensor(wgt[:, :, :], prob[:, :, :], sel[:, :, :], ALU.mult), base)
            link(dve.tensor_reduce(ssum[:, :], wgt[:, :, :], AX_X, ALU.add), base)
            link(dve.tensor_scalar(ssum[:, :], ssum[:, :], 1e-20, None, ALU.add), base)
            link(dve.reciprocal(srec[:, :], ssum[:, :]), base)
            link(dve.tensor_tensor(wgt[:, :, :], wgt[:, :, :], srec[:, :].unsqueeze(2).to_broadcast([P, NT, E]),
                                   ALU.mult), base)

            dve.wait_ge(rank_mm, 1)
            rank = bank[6][:, 0:NT * E].rearrange("p (t e) -> p t e", t=NT)
            link(dve.scalar_tensor_tensor(keep[:, :, :], rank, float(CAP), sel[:, :, :], ALU.is_lt, ALU.mult), base)
            link(dve.scalar_tensor_tensor(slotf[:, :, :], rank, NO_SLOT, keep[:, :, :], ALU.subtract, ALU.mult), base)
            link(dve.tensor_scalar(slotv[:, :, :], slotf[:, :, :], NO_SLOT, None, ALU.add), base)
            for g in range(4):
                for t in range(NT):
                    dve.tensor_tensor(disp[:, t, 4 * g:4 * g + 4, :],
                                      iotah[:, :].unsqueeze(1).to_broadcast([P, 4, CAP]),
                                      slotv[:, t, 4 * g:4 * g + 4].unsqueeze(2).to_broadcast([P, 4, CAP]),
                                      ALU.is_equal).then_inc(disp_ready, 1)
            link(dve.tensor_tensor(key[:, :, :], rowof[:, :].unsqueeze(1).to_broadcast([P, NT, E]), rank,
                                   ALU.subtract), base)
            link(dve.tensor_tensor(key[:, :, :], key[:, :, :], keep[:, :, :], ALU.mult), base)
            for t in range(NT):
                link(dve.max(keytop[:, t, :], key[:, t, :]), base)
            dve.tensor_scalar(idx[:, :, :], keytop[:, :, 0:TOPK], -1.0, float(ZROW), ALU.mult,
                              ALU.add).then_inc(idx_ready, 1)
            link(dve.tensor_tensor(eq[:, :, :, :], key[:, :, :].unsqueeze(2).to_broadcast([P, NT, TOPK, E]),
                                   keytop[:, :, 0:TOPK].unsqueeze(3).to_broadcast([P, NT, TOPK, E]),
                                   ALU.is_equal), base)
            link(dve.tensor_tensor(eq[:, :, :, :], eq[:, :, :, :],
                                   wgt[:, :, :].unsqueeze(2).to_broadcast([P, NT, TOPK, E]), ALU.mult), base)
            link(dve.tensor_reduce(wk[:, :, :], eq[:, :, :, :], AX_X, ALU.add), base)

            with dve.Fori(0, E // NW) as i:
                for f in range(NW):
                    dve.wait_ge(exs_ready, i * NW + (f + 1))
                    dve.wait_ge(exd_mm, i * NW + max(f, 1))
                    dve.tensor_tensor(emid[:, f % 2, :, :].rearrange("p j c -> p (j c)"), esg[:, f % 2, :],
                                      bank[2 + f % 2][0:IH, 0:2 * CAP], ALU.mult).then_inc(exm_ready, 1)

            dve.wait_ge(exg_mm, E)
            dve.memset(kblk[:, :, :, :], 0.0).then_inc(zero_ready, 1)

            def combine(t):
                dve.wait_ge(g_ld[t], 16 * TOPK)
                for k in range(TOPK):
                    link(dve.scalar_tensor_tensor(X[:, t, :], gath[:, t * TOPK + k, :], wk[:, t, k:k + 1],
                                                  X[:, t, :], ALU.mult, ALU.add), base)

            def att_ln_apply(b):
                dve.wait_ge(l2_rstd, b + 1)
                for t in range(TB):
                    dve.tensor_scalar(xln[:, t, :], row(b, t), mv[:, t, 0:1], rstd[:, t:t + 1], ALU.subtract,
                                      ALU.mult).then_inc(l2_xln, 1)

            def split_w2(k):
                rows = min(P, HID - k * P)
                x = w2f[0:rows, k, :]
                for part in range(3):
                    y = w2p[0:rows, part, k, :]
                    link(dve.tensor_copy(y, x), base)
                    if part < 2:
                        link(dve.tensor_tensor(x, x, y, ALU.subtract), base)

            dve.wait_ge(ld_w13, 16 * 4)
            dve.wait_ge(st_eout[0], 16 * (E // 2) + 16)
            dve.wait_ge(st_eout[1], 16 * (E // 2) + 16)
            n = 0
            for c in range(2):
                for i in range(3):
                    rows = min(P, IS - i * P)
                    dve.wait_ge(shs_ready, n + 1)
                    dve.wait_ge(shd_mm, c * 4)
                    dve.tensor_tensor(smid[0:rows, i, :], sgs[0:rows, :], bank[2 + n % 2][0:rows, :],
                                      ALU.mult).then_inc(shm_ready, 1)
                    if n == 5:
                        att_ln_apply(0)
                    split_w2(n)
                    if i > 0:
                        combine(c * 2 + (i - 1))
                    n += 1
                for t in range(4):
                    dve.wait_ge(shd_mm, c * 4 + t + 1)
                    dve.tensor_tensor(X[:, c * 4 + t, :], X[:, c * 4 + t, :], bank[4 + t % 2][:, 0:D],
                                      ALU.add).then_inc(shd_add, 1)
                    if c == 1:
                        dve.wait_ge(shd_add, NT - 3 + t)
                        combine(4 + t)
                if c == 0:
                    dve.wait_ge(shd_add, 4)
                    layernorm_stats(0, base, l2_veps)
            dve.engine_nop().then_inc(wsplit_ready, 1)
            dve.engine_nop().then_inc(combined, 1)

            def att_keys(b):
                dve.tensor_copy(kvb[:, :, :], kvr[:, bass.ds(b * TB, TB), 0, :]).then_inc(kvb_ready, 1)

            def att_back_evac(b, j):
                dve.wait_ge(et2_mm, b * 16 + (2 * j + 2) + 1)
                dve.wait_ge(cx_mm, b * 8 + max(j, 1))
                dve.tensor_copy(ET2[:, j % 2, 1, :, :].rearrange("p t s -> p (t s)"),
                                bank[3][:, :]).then_inc(et2_dve, 1)

            def att_max(b, j, first=False):
                if not first:
                    dve.wait_ge(ex2_ready, b * 32 + (4 * j - 4) + 1)
                for t in range(TB):
                    dve.wait_ge(sc_mm, b * 16 + (2 * j + t + 1))
                    dve.tensor_reduce(nmx[:, j % 2, t, :], bank[t][:, :].rearrange("p (h s) -> p h s", h=2),
                                      AX_X, ALU.max, negate=True).then_inc(mx_ready, 1)

            def att_context_evac(b, j):
                dve.wait_ge(cx_mm, b * 8 + (j + 1) + 1)
                dve.wait_ge(o_mm, b + 1)
                dve.tensor_copy(cxT[:, j, :], bank[4 + j % 2][:, 0:S]).then_inc(cx_evac, 1)

            def att_inverse(b, j, first=False):
                dve.wait_ge(ex2_ready, b * 32 + (4 * j + 4) + 1)
                if not first:
                    dve.wait_ge(en2_ready, b * 32 + (4 * j - 4) + 1)
                dve.reciprocal(R2[:, j % 2, :, :], S2[:, j % 2, :, :]).then_inc(ri2_ready, 1)

            def att_add(b):
                dve.wait_ge(o_mm, b + 1 + 1)
                xb = X[:, bass.ds(b * TB, TB), :].rearrange("p t d -> p (t d)")
                dve.tensor_tensor(xb, xb, bank[7][:, :], ALU.add).then_inc(x3_ready, 1)

            def to_integers(tmp, x, scale, base):
                link(dve.tensor_scalar(tmp, x, scale, ROUND, ALU.mult, ALU.add), base)
                return dve.tensor_scalar(tmp, tmp, ROUND - 128.0, ROUND + 127.0, ALU.max, ALU.min)

            def ff_first(b, t, base):
                if t == 0:
                    dve.wait_ge(f_rstd, b + 1)
                    link(dve.tensor_copy(fnow[:, :], fstat[:, bass.ds(b, 1), :].rearrange("p o c -> p (o c)")), base)
                link(dve.tensor_scalar(xln[:, t, :], row(b, t), fnow[:, 2 * t:2 * t + 1], fnow[:, 4 + t:5 + t],
                                       ALU.subtract, ALU.mult), base)
                link(dve.tensor_reduce(amax1[:, :], xln[:, t, :], AX_X, ALU.max, apply_absolute_value=True), base)
                link(dve.tensor_scalar(is1[:, t:t + 1], amax1[:, :], 1e-5, 1.0 / 127.0, ALU.max, ALU.mult), base)
                link(dve.reciprocal(scl1[:, :], is1[:, t:t + 1]), base)

            def ff_first_integers(n, t, base, first=False):
                link(to_integers(tmp1[:, :], xln[:, t, :], scl1[:, 0:1], base), base)
                if not first:
                    dve.wait_ge(f_q1T_mm, n - 1)
                dve.tensor_scalar(q1[:, t, :], tmp1[:, :], ROUND, None, ALU.subtract).then_inc(f_q1, 1)

            def ff_gate(n, g, base):
                dve.wait_ge(f_r_ready, n + 1)
                link(dve.scalar_tensor_tensor(gated[:, 0:512], bank[3 * g + 1][:, :], is1[:, g:g + 1],
                                              r2[:, 0:512], ALU.mult, ALU.mult), base)
                dve.scalar_tensor_tensor(gated[:, 512:HID], bank[3 * g + 2][:, HID - 512:2 * (HID - 512)],
                                         is1[:, g:g + 1], r2[:, 512:HID], ALU.mult, ALU.mult,
                                         ).then_inc(f_g_ready, 1)

            def ff_mean(n):
                dve.wait_ge(f_sq_ready, n + 1)
                dve.tensor_scalar(msq[:, :], ms[:, :], 1.0 / HID, RMS_EPS, ALU.mult, ALU.add,
                                  ).then_inc(f_ms, 1)

            def ff_largest(n, base):
                dve.wait_ge(f_w_ready, n + 1)
                link(dve.tensor_reduce(amax2[:, :], weighed[:, :], AX_X, ALU.max, apply_absolute_value=True), base)

            def ff_second(n, g, base):
                dve.wait_ge(f_rms, n + 1)
                link(dve.tensor_scalar(amax2[:, :], amax2[:, :], rms[:, 0:1], 1e-5, ALU.mult, ALU.max), base)
                link(dve.tensor_scalar(is2[:, g:g + 1], amax2[:, :], 1.0 / 127.0, None, ALU.mult), base)
                link(dve.reciprocal(scl2[:, :], is2[:, g:g + 1]), base)
                link(dve.tensor_scalar(scl2[:, :], scl2[:, :], rms[:, 0:1], None, ALU.mult), base)
                dve.wait_ge(f_q2, n + 1)
                to_integers(tmp2[:, :], weighed[:, :], scl2[:, 0:1], base).then_inc(f_t2, 1)

            def ff_result(n, b, t):
                dve.wait_ge(f_o_mm, n + 1 + 1)
                dve.wait_ge(st_out[t], b * 16 + 16)
                dve.scalar_tensor_tensor(yt[:, t, :], bank[7][:, 0:D], is2[:, t:t + 1], row(b, t), ALU.mult,
                                         ALU.add).then_inc(f_out, 1)

            att_keys(0)
            att_max(0, 0, first=True)
            att_inverse(0, 0, first=True)
            att_max(0, 1, first=True)
            att_inverse(0, 1, first=True)
            base += steps[0]
            ATT_STEPS = 4
            with dve.Fori(0, B - 1) as b:
                base2 = b * ATT_STEPS + base
                steps[0] = 0
                for j in range(2, AH // 2):
                    att_back_evac(b, j - 2)
                    att_max(b, j)
                    att_context_evac(b, j - 2)
                    if j == 2:
                        layernorm_stats(b + 1, base2, l2_veps)
                    if j == 3:
                        dve.wait_ge(l2_T_mm, b + 1)
                        att_ln_apply(b + 1)
                    att_inverse(b, j)
                for j in range(2):
                    att_back_evac(b, j + 6)
                    att_max(b + 1, j)
                    att_context_evac(b, j + 6)
                    att_inverse(b + 1, j)
                att_keys(b + 1)
                att_add(b)
                assert steps[0] == ATT_STEPS, steps[0]
            base += (B - 1) * ATT_STEPS
            steps[0] = 0
            dve.wait_ge(x3_ready, B)
            for j in range(2, AH // 2 + 2):
                att_back_evac(B - 1, j - 2)
                if j < AH // 2:
                    att_max(B - 1, j)
                att_context_evac(B - 1, j - 2)
                if j in (2, 3, 5):
                    b = (2, 3, 5).index(j)
                    layernorm_stats(b, base, f_veps, keep_at=b)
                if j < AH // 2:
                    att_inverse(B - 1, j)
                if j == 4:
                    ff_first(0, 0, base)
                    ff_first_integers(0, 0, base, first=True)
                if j == 6:
                    ff_first(0, 1, base)
                    ff_first_integers(1, 1, base, first=True)
            ff_gate(0, 0, base)
            ff_first(1, 0, base)
            ff_first_integers(2, 0, base)
            ff_mean(0)
            ff_largest(0, base)
            ff_second(0, 0, base)
            att_add(B - 1)
            ff_gate(1, 1, base)
            ff_first(1, 1, base)
            ff_first_integers(3, 1, base)
            ff_mean(1)
            ff_largest(1, base)
            ff_second(1, 1, base)
            dve.wait_ge(x3_ready, B + 1)
            layernorm_stats(B - 1, base, f_veps, keep_at=B - 1)
            base += steps[0]
            FF_STEPS = 27
            with dve.Fori(1, B - 1) as b:
                base3 = b * FF_STEPS + (base - FF_STEPS)
                steps[0] = 0
                for t in range(TB):
                    n = b * TB + t
                    ff_gate(n, t, base3)
                    ff_result(b * TB + (t - 2), b - 1, t)
                    ff_first(b + 1, t, base3)
                    ff_first_integers(b * TB + (t + 2), t, base3)
                    ff_mean(n)
                    ff_largest(n, base3)
                    ff_second(n, t, base3)
                assert steps[0] == FF_STEPS, steps[0]
            base += (B - 2) * FF_STEPS
            steps[0] = 0
            for n in range(NT - 2, NT):
                ff_gate(n, n % 2, base)
                ff_result(n - 2, n // 2 - 1, n % 2)
                ff_mean(n)
                ff_largest(n, base)
                ff_second(n, n % 2, base)
            for n in range(NT - 2, NT):
                ff_result(n, n // 2, n % 2)

        @block.gpsimd
        def _(pool):
            pool.sem_inc(u_ready, 1)
            pool.sem_inc(en2_ready, 1)
            pool.wait_ge(consts_ready, 1)

            def root(count, veps_sem, rstd_sem, src=None, dst=None):
                pool.wait_ge(veps_sem, count)
                src = veps[:, :] if src is None else src
                dst = rstd[:, :] if dst is None else dst
                pool.tensor_tensor(dst, src, half[:, 0:src.shape[1]], ALU.pow).then_inc(rstd_sem, 1)

            with pool.Fori(0, B // 2) as p:
                root(p * 4 + 1, veps_ready, rstd_ready)
                for i in range(4 * GH):
                    k, h = i // GH, i % GH
                    if i == 4:
                        root(p * 4 + 2, veps_ready, rstd_ready)
                    if h % 2 == 0:
                        held = pool.to_reg(p * 12 + (3 * k + 2 + h // 4) + 1)
                        pool.wait_ge(consts_ready, 1)
                    if h in (0, 4):
                        pool.wait_ge(prep_dve, held)
                    if h in (2, 6):
                        pool.wait_ge(prep_act, held)
                    held = pool.to_reg(p * 64 + 2 * max(i - 3, 0) + 1)
                    pool.wait_ge(consts_ready, 1)
                    pool.wait_ge(leak_done, held)
                    for t in range(TB):
                        pool.tensor_scalar(U[:, i % 4, t, :], NB[:, k % 2, h, :], 0.2, self02[:, k % 2, t, h:h + 1],
                                           ALU.mult, ALU.add).then_inc(u_ready, 1)
                root(p * 4 + 3, veps_ready, rstd_ready)
                root(p * 4 + 4, veps_ready, rstd_ready)

            pool.wait_ge(ld_kv, 16 * 3)
            for b in range(B):
                k4 = kv[:, b * TB:(b + 1) * TB, :]
                d4 = kvr[:, b * TB:(b + 1) * TB, 0, :]
                t4 = kvt[:, b * TB:(b + 1) * TB, :]
                H2 = CD // 2
                pool.tensor_tensor(d4, k4, cosd[:, :, :], ALU.mult).then_inc(pool_step, 1)
                pool.tensor_tensor(t4[:, :, 0:H2], k4[:, :, H2:CD], sind[:, :, 0:H2], ALU.mult,
                                   ).then_inc(pool_step, 1)
                pool.tensor_tensor(t4[:, :, H2:CD], k4[:, :, 0:H2], sind[:, :, H2:CD], ALU.mult,
                                   ).then_inc(pool_step, 1)
                pool.wait_ge(pool_step, 5 * b + 3)
                pool.tensor_tensor(d4[:, :, 0:H2], d4[:, :, 0:H2], t4[:, :, 0:H2], ALU.subtract,
                                   ).then_inc(pool_step, 1)
                pool.tensor_tensor(d4[:, :, H2:CD], d4[:, :, H2:CD], t4[:, :, H2:CD], ALU.add,
                                   ).then_inc(pool_step, 1)
            pool.wait_ge(pool_step, 5 * B)
            pool.tensor_copy(kvr[:, :, 1, :], kvr[:, :, 0, :]).then_inc(kvr_ready, 1)

            pool.wait_ge(ld_w13, 16 * 4)
            pool.wait_ge(disp_mm, 8)
            for part in range(3):
                y = w13p[:, part, :, :]
                pool.wait_ge(pool_step, 5 * B + part)
                pool.tensor_copy(y, w13f).then_inc(w13_part, 1)
                pool.wait_ge(w13_part, part + 1)
                if part < 2:
                    pool.tensor_tensor(w13f, w13f, y, ALU.subtract).then_inc(pool_step, 1)

            pool.wait_ge(idx_ready, 1)
            pool.wait_ge(st_eout[0], 16 * (E // 2) + 16)
            pool.wait_ge(st_eout[1], 16 * (E // 2) + 16)
            pool.wait_ge(st_z, 16)
            for t in range(NT):
                if t == 6:
                    root(1, l2_veps, l2_rstd)
                for k in range(TOPK):
                    pool.indirect_dma_start(out=gath[:, t * TOPK + k, :], out_offset=None, in_=eout[:, :],
                                            in_offset=bass.IndirectOffsetOnAxis(ap=idx[:, t, k:k + 1], axis=0),
                                            ).then_inc(g_ld[t], 16)

            def normalise(b, j):
                held = pool.to_reg(b * 8 + (j + 1) + 1)
                pool.wait_ge(consts_ready, 1)
                pool.wait_ge(ri2_ready, held)
                for t in range(TB):
                    for h in range(2):
                        pool.tensor_scalar(E2[:, j % 2, t, h, :], E2[:, j % 2, t, h, :],
                                           R2[:, j % 2, t, h:h + 1], 1.0, ALU.mult,
                                           ALU.mult).then_inc(en2_ready, 1)

            normalise(0, 0)
            normalise(0, 1)
            with pool.Fori(0, B - 1) as b:
                root(b + 2, l2_veps, l2_rstd)
                for j in range(2, AH // 2):
                    normalise(b, j)
                for j in range(2):
                    normalise(b + 1, j)
            def ff_root(b):
                root(b + 1, f_veps, f_rstd, fveps[:, b, :], fstat[:, b, 4:6])

            def ff_weigh(n, first=False):
                held = pool.to_reg(n + 1 + 1)
                pool.wait_ge(consts_ready, 1)
                pool.wait_ge(f_g_ready, held)
                if not first:
                    held = pool.to_reg(n)
                    pool.wait_ge(consts_ready, 1)
                    pool.wait_ge(f_t2, held)
                pool.tensor_tensor(weighed[:, :], gated[:, :], nwb[:, :], ALU.mult).then_inc(f_w_ready, 1)
                root(n + 1, f_ms, f_rms, msq[:, :], rms[:, :])

            for j in range(2, AH // 2):
                if j in (2, 3, 5):
                    ff_root((2, 3, 5).index(j))
                normalise(B - 1, j)
            ff_weigh(0, first=True)
            ff_weigh(1)
            ff_root(B - 1)
            with pool.Fori(1, B - 1) as b:
                for t in range(TB):
                    ff_weigh(b * TB + t)
            for n in range(NT - 2, NT):
                ff_weigh(n)


def _layouts(inp):
    f = lambda n: np.asarray(inp[n])
    rows = lambda n: f(n).reshape(T, -1)
    pos = np.arange(S, dtype=np.float32)
    inv = (np.float32(1.0) / np.float32(10000.0) ** (np.arange(0, CD, 2, dtype=np.float32) / np.float32(CD)))
    freqs = pos[:, None] * inv.astype(np.float32)[None, :]
    block = np.zeros((2 * P, GH), np.float32)
    for h in range(GH):
        block[h * GO:(h + 1) * GO, h] = -1.0
    pick = np.zeros((96 + GH, GH), np.float32)
    for r in (0, 64, 96):
        pick[r:r + GH] = np.eye(GH, dtype=np.float32)
    return {
        "x": rows("x"),
        "ctx": rows("ctx_512"),
        "ctxT": rows("ctx_512").T,
        "w0": f("L0_xattn_W0").transpose(1, 0, 2).reshape(CD, D),
        "w0T": f("L0_xattn_W0").transpose(0, 2, 1).reshape(D, CD),
        "w1": f("L0_xattn_W1").transpose(1, 0, 2).reshape(D, D),
        "w1T": f("L0_xattn_W1").transpose(0, 2, 1).reshape(D, D),
        "cols": np.stack([f(f"L0_xattn_{n}{l}").reshape(KT, P) for l in range(2) for n in ("a_self", "a_neigh", "b")],
                         ).reshape(-1, P).T,
        "gwT": f("L0_ffn_gate_w").T,
        "wg": f("L0_ffn_w_gate"), "wu": f("L0_ffn_w_up"), "wd": f("L0_ffn_w_down"),
        "swg": f("L0_ffn_sw_gate"), "swu": f("L0_ffn_sw_up"), "swd": f("L0_ffn_sw_down"),
        "wq": f("L1_xattn_Wq"),
        "kcqT": f("L1_xattn_w_kc_q").transpose(2, 0, 1).reshape(AQ, AH * AK),
        "kckv": f("L1_xattn_w_kc_kv").transpose(1, 0, 2).reshape(AK, AH * CD),
        "qrT": f("L1_xattn_W_qr").transpose(2, 0, 1).reshape(AR, AH * AQ),
        "krT": f("L1_xattn_W_kr").transpose(2, 0, 1).reshape(AR, AH * CD),
        "woT": f("L1_xattn_Wo").T,
        "w13T": f("L1_ffn_w13").T, "w2T": f("L1_ffn_w2").T, "nw": f("L1_ffn_norm_w"),
        "ident": np.eye(P, dtype=np.float32),
        "upper": np.triu(np.ones((P, P), np.float32), 1),
        "iota": np.tile(np.arange(CAP, dtype=np.float32), (P, 1)),
        "rowof": np.tile(ZROW - CAP * np.arange(E, dtype=np.float32), (P, 1)),
        "block": block, "pick": pick,
        "cos": np.repeat(np.cos(freqs), 2, axis=-1).astype(np.float32),
        "sin": np.repeat(np.sin(freqs), 2, axis=-1).astype(np.float32),
    }


def kernel(**inputs):
    import concourse.bacc as _bacc
    from concourse.bass_utils import run_bass_kernel_spmd as _run

    nc = _bacc.Bacc("TRN2", target_bir_lowering=False, num_devices=1)
    arrays, a = {}, {}
    for name, x in _layouts(inputs).items():
        x = np.ascontiguousarray(x)
        arrays[f"in_{name}"] = x
        a[name] = nc.dram_tensor(f"in_{name}", x.shape, mybir.dt.from_np(x.dtype), kind="ExternalInput").ap()
    out = nc.dram_tensor("out_0", (T, D), F32, kind="ExternalOutput").ap()
    build(nc, a, out)
    r = _run(nc, [arrays], core_ids=[0])
    return r.results[0]["out_0"].reshape(B, S, D)
```
